# Optimizing a Trainium2 kernel written in Bass

```python
import numpy as np
import jax
import jax.numpy as jnp

def _softmax(x, axis=-1):
    return jax.nn.softmax(x, axis=axis)

def _gelu(x):
    return jax.nn.gelu(x, approximate=True)

def _silu(x):
    return jax.nn.silu(x)

def _sigmoid(x):
    return jax.nn.sigmoid(x)

def _layernorm(x, axis=-1, eps=1e-05):
    m = jnp.mean(x, axis=axis, keepdims=True)
    v = jnp.var(x, axis=axis, keepdims=True)
    return (x - m) / jnp.sqrt(v + eps)

def _scatter_add(tgt, idx, src, axis=0):
    return tgt.at[idx].add(src)

def _segment_sum(src, seg, n):
    return jax.ops.segment_sum(src, seg, n)
kernel_name = 'mk_early_fusion_d1_tok_img768_r4_8e5db4'

def setup_inputs(seed: int=0):
    np.random.seed(seed)
    _w = jnp.asarray

    def _rec_inputs():
        import jax
        import jax.numpy as jnp
        _rk = jax.random.key(seed)
        x = -0.000596345 + 1.00056 * jax.random.normal(jax.random.fold_in(_rk, 1), (2, 3, 64, 64), jnp.float32)
        txt = -0.000190561 + 0.886117 * jax.random.normal(jax.random.fold_in(_rk, 2), (2, 32, 192), jnp.float32)
        return (x, txt)
    x, txt = _rec_inputs()

    def _L0_tok_setup():
        import jax, jax.numpy as jnp
        import numpy as np
        B = 16
        IMG = 64
        CH = 3
        EMBED = 64
        GP = 16
        PRE = [1, 2, 4]
        N_LEVELS = 3
        FUSED = EMBED * N_LEVELS

        def hilbert_flat_indices(n):
            t = np.arange(n * n, dtype=np.int64)
            x = np.zeros(n * n, dtype=np.int64)
            y = np.zeros(n * n, dtype=np.int64)
            s = 1
            while s < n:
                rx = 1 & t // 2
                ry = 1 & (t ^ rx)
                swap = ry == 0
                flip = swap & (rx == 1)
                x = np.where(flip, s - 1 - x, x)
                y = np.where(flip, s - 1 - y, y)
                x2 = np.where(swap, y, x)
                y2 = np.where(swap, x, y)
                x, y = (x2, y2)
                x = x + s * rx
                y = y + s * ry
                t = t // 4
                s *= 2
            return y * n + x

        def _level(x, idx, W, b, p, gp):
            Bsz, C, H, _ = x.shape
            h = H // p
            t = x.reshape(Bsz, C, h, p, h, p).transpose(0, 2, 4, 3, 5, 1).reshape(Bsz, h * h, p * p * C)
            t = t[:, idx]
            t = t.reshape(Bsz, h * h // gp, gp * p * p * C)
            return t @ W.T + b

        def _interp_linear(x, n_out):
            L = x.shape[1]
            pos = (jnp.arange(n_out, dtype=jnp.float32) + 0.5) * (L / n_out) - 0.5
            pos = jnp.clip(pos, 0.0, L - 1)
            i0 = jnp.floor(pos).astype(jnp.int32)
            i1 = jnp.minimum(i0 + 1, L - 1)
            w = (pos - i0).astype(x.dtype)
            return x[:, i0] * (1.0 - w)[None, :, None] + x[:, i1] * w[None, :, None]
        key = jax.random.key(seed)
        ks = jax.random.split(key, 9)
        inp = {'x': jax.random.normal(ks[0], (B, CH, IMG, IMG), jnp.float32)}
        for i, p in enumerate(PRE):
            din = CH * p * p * GP
            inp[f'W{i}'] = jax.random.normal(ks[1 + 2 * i], (EMBED, din), jnp.float32) * din ** (-0.5)
            inp[f'b{i}'] = jax.random.normal(ks[2 + 2 * i], (EMBED,), jnp.float32) * 0.02
        inp['Wf'] = jax.random.normal(ks[7], (FUSED, FUSED), jnp.float32) * FUSED ** (-0.5)
        inp['bf'] = jax.random.normal(ks[8], (FUSED,), jnp.float32) * 0.02
        for i, p in enumerate(PRE):
            inp[f'idx{i}'] = jnp.asarray(hilbert_flat_indices(IMG // p), jnp.int32)
        return inp
    _L0_tok_all = _L0_tok_setup()
    _L0_tok_in = {k: v for k, v in _L0_tok_all.items() if k in ('W0', 'b0', 'W1', 'b1', 'W2', 'b2', 'Wf', 'bf', 'idx0', 'idx1', 'idx2')}
    del _L0_tok_all

    def _L0_attn_setup():
        import jax, jax.numpy as jnp
        import numpy as np
        DIM = 192
        NUM_HEADS = 12
        HEAD_DIM = DIM // NUM_HEADS
        HIDDEN = int(DIM * 4.0)
        EPS = 1e-08

        def layer_norm(x, w, b):
            mu = jnp.mean(x, axis=-1, keepdims=True)
            var = jnp.mean(jnp.square(x - mu), axis=-1, keepdims=True)
            return (x - mu) * jax.lax.rsqrt(var + EPS) * w + b

        def linear_attention(x, qkv_w, qkv_b, proj_w, proj_b):
            B, N, C = x.shape
            qkv = (x @ qkv_w + qkv_b).reshape(B, N, 3, NUM_HEADS, HEAD_DIM)
            qkv = qkv.transpose(2, 0, 3, 1, 4)
            q, k, v = (qkv[0], qkv[1], qkv[2])
            q = jax.nn.elu(q) + 1.0
            k = jax.nn.elu(k) + 1.0
            kv = jnp.einsum('bhsd,bhse->bhde', k, v)
            z = 1.0 / jnp.einsum('bhsd,bhd->bhs', q, k.sum(axis=-2))
            out = jnp.einsum('bhde,bhsd,bhs->bhse', kv, q, z)
            out = out.transpose(0, 2, 1, 3).reshape(B, N, C)
            return out @ proj_w + proj_b
        key = jax.random.key(seed)
        ks = jax.random.split(key, 10)
        s = 0.02
        return {'x': jax.random.normal(ks[0], (16, 1024, DIM), dtype=jnp.float32), 'qkv_w': jax.random.normal(ks[1], (DIM, 3 * DIM), dtype=jnp.float32) * s, 'qkv_b': jnp.zeros((3 * DIM,), dtype=jnp.float32), 'proj_w': jax.random.normal(ks[2], (DIM, DIM), dtype=jnp.float32) * s, 'proj_b': jnp.zeros((DIM,), dtype=jnp.float32), 'fc1_w': jax.random.normal(ks[3], (DIM, HIDDEN), dtype=jnp.float32) * s, 'fc1_b': jnp.zeros((HIDDEN,), dtype=jnp.float32), 'fc2_w': jax.random.normal(ks[4], (HIDDEN, DIM), dtype=jnp.float32) * s, 'fc2_b': jnp.zeros((DIM,), dtype=jnp.float32), 'ln1_w': jnp.ones((DIM,), dtype=jnp.float32), 'ln1_b': jnp.zeros((DIM,), dtype=jnp.float32), 'ln2_w': jnp.ones((DIM,), dtype=jnp.float32), 'ln2_b': jnp.zeros((DIM,), dtype=jnp.float32)}
    _L0_attn_all = _L0_attn_setup()
    _L0_attn_in = {k: v for k, v in _L0_attn_all.items() if k in ('qkv_w', 'qkv_b', 'proj_w', 'proj_b', 'fc1_w', 'fc1_b', 'fc2_w', 'fc2_b', 'ln1_w', 'ln1_b', 'ln2_w', 'ln2_b')}
    del _L0_attn_all

    def _L0_ffn_setup():
        import jax, jax.numpy as jnp
        import numpy as np
        E, TOPK = (32, 2)
        D, HID, BOT, OUT = (192, 512, 64, 192)
        B, S = (2, 128)
        key = jax.random.key(seed)
        ks = jax.random.split(key, 7)
        p = lambda k, shape: jax.random.normal(k, shape, dtype=jnp.float32) * 0.02
        return {'x': jax.random.normal(ks[0], (B, S, D), dtype=jnp.float32), 'gate_w': p(ks[1], (E, D)), 'W1': p(ks[2], (E, D, HID)), 'b1': jnp.zeros((E, HID), jnp.float32), 'W2': p(ks[3], (E, HID, HID)), 'b2': jnp.zeros((E, HID), jnp.float32), 'W3': p(ks[4], (E, HID, BOT)), 'b3': jnp.zeros((E, BOT), jnp.float32), 'Wl': p(ks[5], (E, BOT, OUT)), 'bl': jnp.zeros((E, OUT), jnp.float32)}
    _L0_ffn_all = _L0_ffn_setup()
    _L0_ffn_in = {k: v for k, v in _L0_ffn_all.items() if k in ('gate_w', 'W1', 'b1', 'W2', 'b2', 'W3', 'b3', 'Wl', 'bl')}
    del _L0_ffn_all
    return {'x': x, 'txt': txt, 'L0_tok_W0': _L0_tok_in['W0'], 'L0_tok_b0': _L0_tok_in['b0'], 'L0_tok_W1': _L0_tok_in['W1'], 'L0_tok_b1': _L0_tok_in['b1'], 'L0_tok_W2': _L0_tok_in['W2'], 'L0_tok_b2': _L0_tok_in['b2'], 'L0_tok_Wf': _L0_tok_in['Wf'], 'L0_tok_bf': _L0_tok_in['bf'], 'L0_tok_idx0': _L0_tok_in['idx0'], 'L0_tok_idx1': _L0_tok_in['idx1'], 'L0_tok_idx2': _L0_tok_in['idx2'], 'L0_attn_qkv_w': _L0_attn_in['qkv_w'], 'L0_attn_qkv_b': _L0_attn_in['qkv_b'], 'L0_attn_proj_w': _L0_attn_in['proj_w'], 'L0_attn_proj_b': _L0_attn_in['proj_b'], 'L0_attn_fc1_w': _L0_attn_in['fc1_w'], 'L0_attn_fc1_b': _L0_attn_in['fc1_b'], 'L0_attn_fc2_w': _L0_attn_in['fc2_w'], 'L0_attn_fc2_b': _L0_attn_in['fc2_b'], 'L0_attn_ln1_w': _L0_attn_in['ln1_w'], 'L0_attn_ln1_b': _L0_attn_in['ln1_b'], 'L0_attn_ln2_w': _L0_attn_in['ln2_w'], 'L0_attn_ln2_b': _L0_attn_in['ln2_b'], 'L0_ffn_gate_w': _L0_ffn_in['gate_w'], 'L0_ffn_W1': _L0_ffn_in['W1'], 'L0_ffn_b1': _L0_ffn_in['b1'], 'L0_ffn_W2': _L0_ffn_in['W2'], 'L0_ffn_b2': _L0_ffn_in['b2'], 'L0_ffn_W3': _L0_ffn_in['W3'], 'L0_ffn_b3': _L0_ffn_in['b3'], 'L0_ffn_Wl': _L0_ffn_in['Wl'], 'L0_ffn_bl': _L0_ffn_in['bl']}

def reference(x, txt, L0_tok_W0, L0_tok_b0, L0_tok_W1, L0_tok_b1, L0_tok_W2, L0_tok_b2, L0_tok_Wf, L0_tok_bf, L0_tok_idx0, L0_tok_idx1, L0_tok_idx2, L0_attn_qkv_w, L0_attn_qkv_b, L0_attn_proj_w, L0_attn_proj_b, L0_attn_fc1_w, L0_attn_fc1_b, L0_attn_fc2_w, L0_attn_fc2_b, L0_attn_ln1_w, L0_attn_ln1_b, L0_attn_ln2_w, L0_attn_ln2_b, L0_ffn_gate_w, L0_ffn_W1, L0_ffn_b1, L0_ffn_W2, L0_ffn_b2, L0_ffn_W3, L0_ffn_b3, L0_ffn_Wl, L0_ffn_bl):
    import jax
    import jax.numpy as jnp

    def _L0_tok_ref(x, W0, b0, W1, b1, W2, b2, Wf, bf, idx0, idx1, idx2):
        import jax, jax.numpy as jnp
        import numpy as np
        B = 16
        IMG = 64
        CH = 3
        EMBED = 64
        GP = 16
        PRE = [1, 2, 4]
        N_LEVELS = 3
        FUSED = EMBED * N_LEVELS

        def hilbert_flat_indices(n):
            t = np.arange(n * n, dtype=np.int64)
            x = np.zeros(n * n, dtype=np.int64)
            y = np.zeros(n * n, dtype=np.int64)
            s = 1
            while s < n:
                rx = 1 & t // 2
                ry = 1 & (t ^ rx)
                swap = ry == 0
                flip = swap & (rx == 1)
                x = np.where(flip, s - 1 - x, x)
                y = np.where(flip, s - 1 - y, y)
                x2 = np.where(swap, y, x)
                y2 = np.where(swap, x, y)
                x, y = (x2, y2)
                x = x + s * rx
                y = y + s * ry
                t = t // 4
                s *= 2
            return y * n + x

        def _level(x, idx, W, b, p, gp):
            Bsz, C, H, _ = x.shape
            h = H // p
            t = x.reshape(Bsz, C, h, p, h, p).transpose(0, 2, 4, 3, 5, 1).reshape(Bsz, h * h, p * p * C)
            t = t[:, idx]
            t = t.reshape(Bsz, h * h // gp, gp * p * p * C)
            return t @ W.T + b

        def _interp_linear(x, n_out):
            L = x.shape[1]
            pos = (jnp.arange(n_out, dtype=jnp.float32) + 0.5) * (L / n_out) - 0.5
            pos = jnp.clip(pos, 0.0, L - 1)
            i0 = jnp.floor(pos).astype(jnp.int32)
            i1 = jnp.minimum(i0 + 1, L - 1)
            w = (pos - i0).astype(x.dtype)
            return x[:, i0] * (1.0 - w)[None, :, None] + x[:, i1] * w[None, :, None]
        Ws = [(idx0, W0, b0, PRE[0]), (idx1, W1, b1, PRE[1]), (idx2, W2, b2, PRE[2])]
        outs = [_level(x, idx, W, b, p, GP) for idx, W, b, p in Ws]
        n_tokens = outs[0].shape[1]
        outs = [outs[0]] + [_interp_linear(o, n_tokens) for o in outs[1:]]
        y = jnp.concatenate(outs, axis=-1)
        return y @ Wf.T + bf

    def _L0_attn_ref(x, qkv_w, qkv_b, proj_w, proj_b, fc1_w, fc1_b, fc2_w, fc2_b, ln1_w, ln1_b, ln2_w, ln2_b):
        import jax, jax.numpy as jnp
        import numpy as np
        DIM = 192
        NUM_HEADS = 12
        HEAD_DIM = DIM // NUM_HEADS
        HIDDEN = int(DIM * 4.0)
        EPS = 1e-08

        def layer_norm(x, w, b):
            mu = jnp.mean(x, axis=-1, keepdims=True)
            var = jnp.mean(jnp.square(x - mu), axis=-1, keepdims=True)
            return (x - mu) * jax.lax.rsqrt(var + EPS) * w + b

        def linear_attention(x, qkv_w, qkv_b, proj_w, proj_b):
            B, N, C = x.shape
            qkv = (x @ qkv_w + qkv_b).reshape(B, N, 3, NUM_HEADS, HEAD_DIM)
            qkv = qkv.transpose(2, 0, 3, 1, 4)
            q, k, v = (qkv[0], qkv[1], qkv[2])
            q = jax.nn.elu(q) + 1.0
            k = jax.nn.elu(k) + 1.0
            kv = jnp.einsum('bhsd,bhse->bhde', k, v)
            z = 1.0 / jnp.einsum('bhsd,bhd->bhs', q, k.sum(axis=-2))
            out = jnp.einsum('bhde,bhsd,bhs->bhse', kv, q, z)
            out = out.transpose(0, 2, 1, 3).reshape(B, N, C)
            return out @ proj_w + proj_b
        y = linear_attention(layer_norm(x, ln1_w, ln1_b), qkv_w, qkv_b, proj_w, proj_b)
        x = x + y
        h = layer_norm(x, ln2_w, ln2_b)
        h = jax.nn.gelu(h @ fc1_w + fc1_b, approximate=False) @ fc2_w + fc2_b
        return x + h

    def _L0_ffn_ref(x, gate_w, W1, b1, W2, b2, W3, b3, Wl, bl):
        import jax, jax.numpy as jnp
        import numpy as np
        E, TOPK = (32, 2)
        D, HID, BOT, OUT = (192, 512, 64, 192)
        B, S = (2, 128)
        Bz, Sl, d = x.shape
        xt = x.reshape(-1, d)
        scores = jax.nn.softmax(xt @ gate_w.T, axis=-1)
        topk_w, topk_idx = jax.lax.top_k(scores, TOPK)
        topk_w = topk_w / (topk_w.sum(-1, keepdims=True) + 1e-20)
        gelu = lambda v: jax.nn.gelu(v, approximate=False)
        h = gelu(jnp.einsum('nd,edh->enh', xt, W1) + b1[:, None, :])
        h = gelu(jnp.einsum('enh,ehg->eng', h, W2) + b2[:, None, :])
        z = jnp.einsum('eng,egb->enb', h, W3) + b3[:, None, :]
        out_all = jnp.einsum('enb,ebo->eno', z, Wl) + bl[:, None, :]
        sel = jnp.take_along_axis(out_all.transpose(1, 0, 2), topk_idx[:, :, None], axis=1)
        y = (sel * topk_w[:, :, None]).sum(axis=1)
        return y.reshape(Bz, Sl, OUT)
    h = _L0_tok_ref(x, L0_tok_W0, L0_tok_b0, L0_tok_W1, L0_tok_b1, L0_tok_W2, L0_tok_b2, L0_tok_Wf, L0_tok_bf, L0_tok_idx0, L0_tok_idx1, L0_tok_idx2)
    h = jnp.concatenate([h, txt], axis=1)
    h = h + _L0_attn_ref(_layernorm(h, axis=-1), L0_attn_qkv_w, L0_attn_qkv_b, L0_attn_proj_w, L0_attn_proj_b, L0_attn_fc1_w, L0_attn_fc1_b, L0_attn_fc2_w, L0_attn_fc2_b, L0_attn_ln1_w, L0_attn_ln1_b, L0_attn_ln2_w, L0_attn_ln2_b)
    h = h + _L0_ffn_ref(_layernorm(h, axis=-1), L0_ffn_gate_w, L0_ffn_W1, L0_ffn_b1, L0_ffn_W2, L0_ffn_b2, L0_ffn_W3, L0_ffn_b3, L0_ffn_Wl, L0_ffn_bl)
    return h

_drawn_inputs = setup_inputs


def setup_inputs(seed=0):
    import zlib

    import numpy as np

    out = dict(_drawn_inputs(seed))
    spreads = {'L0_attn_qkv_b': (0.0, 0.468),
     'L0_attn_proj_b': (0.0, 0.1),
     'L0_attn_fc1_b': (0.0, 0.47),
     'L0_attn_fc2_b': (0.0, 0.1),
     'L0_attn_ln1_w': (1.0, 0.6),
     'L0_attn_ln1_b': (0.0, 0.8),
     'L0_attn_ln2_w': (1.0, 0.6),
     'L0_attn_ln2_b': (0.0, 0.8),
     'L0_ffn_b1': (0.0, 0.8),
     'L0_ffn_b2': (0.0, 0.8),
     'L0_ffn_b3': (0.0, 0.8),
     'L0_ffn_bl': (0.0, 0.8)}
    factors = {'L0_tok_b0': 4.508,
     'L0_tok_b1': 4.547,
     'L0_tok_b2': 4.082,
     'L0_attn_qkv_w': 6.664,
     'L0_attn_proj_w': 3.2,
     'L0_ffn_W1': 8.0,
     'L0_ffn_W2': 8.0,
     'L0_ffn_W3': 8.0,
     'L0_ffn_Wl': 8.0}
    for name, (base, spread) in spreads.items():
        noise = np.random.default_rng([zlib.crc32(name.encode()), seed]).standard_normal(out[name].shape)
        drawn = base * np.exp(spread * noise) if base else spread * noise
        out[name] = jnp.asarray(drawn.astype(out[name].dtype))
    for name, factor in factors.items():
        out[name] = (out[name] * factor).astype(out[name].dtype)
    return out
```

```python
from contextlib import ExitStack

import concourse.bass as bass
from concourse import mybir

ALU = mybir.AluOpType
ACT = mybir.ActivationFunctionType
AX_X = mybir.AxisListType.X
F32 = mybir.dt.float32
BF16 = mybir.dt.bfloat16
I32 = mybir.dt.int32
U32 = mybir.dt.uint32

NBATCH, CH, IMG = 2, 3, 64
TXT = 32
EMB = 64
D = 192
NIMG = IMG * IMG // 16
NTOK = NIMG + TXT
HEAD = 16
HID = 768
E = 32
EHID, BOT = 512, 64
LEVELS = ((1, 5, 6), (2, 3, 24), (4, 1, 96))

TC = 96
NC = NBATCH * NTOK // TC
CPB = NTOK // TC
NT = NBATCH * NTOK
DH = D // 2
SLOTS = 64
MAXJ = NT // SLOTS
MAXB = 2 * NT // SLOTS + E
SHARED = 11520
WBUF = 8
NQ = 42
GROUPS = [(4 * g, min(4, NQ - 4 * g)) for g in range(11)]
PAIRS = [(2 * i, 0 if i < 16 else 1 if i < 20 else 2) for i in range(21)]


def dram_views(a):
    x = a["x"]
    v = {}
    v["x0"] = x.rearrange("b c y (h w) -> (y h) (b c) w", h=2)
    v["x1"] = x.rearrange("b c (p i) (h w) -> h p (b c) i w", i=2, h=4)
    v["x2"] = x.rearrange("b c (p i) (h w) -> h p (b c) i w", i=4, h=8)
    v["i0"] = a["L0_tok_idx0"].rearrange("(t p g) -> p t g", t=2, p=128)
    v["i1"] = a["L0_tok_idx1"].rearrange("(p k) -> p k", k=8)
    v["i2"] = a["L0_tok_idx2"].rearrange("(p k) -> p k", k=2)
    return v


def column(ap):
    return ap.rearrange("(n o) -> n o", o=1)


def row(ap):
    return ap.rearrange("(o n) -> o n", o=1)


def fusion_kernel(nc, a, out):
    ydram = nc.dram_tensor("expert_rows", [MAXB * SLOTS + MAXJ * SLOTS, D], F32, kind="Internal").ap()
    dv = dram_views(a)
    out_chunks = out.rearrange("b (c p) d -> (b c) p d", p=TC)

    with ExitStack() as ctx:
        def sb(name, shape, dt=F32):
            return ctx.enter_context(nc.sbuf_tensor(name, shape, dt))

        def sem(name):
            return ctx.enter_context(nc.semaphore(name))

        shared = sb("shared", [128, SHARED])

        def carver(start=0):
            at = [start]

            def carve(name, shape):
                n = 1
                for k in shape[1:]:
                    n *= k
                at[0] += n
                assert at[0] <= SHARED, name
                v = shared[0:shape[0], at[0] - n:at[0]]
                if len(shape) == 3:
                    return v.rearrange("p (a b) -> p a b", b=shape[2])
                return v.rearrange("p (a b c) -> p a b c", b=shape[2], c=shape[3]) if len(shape) == 4 else v
            return carve

        early, late, attn = carver(), carver(), carver(3 * NC * D)
        routing = carver(3 * NC * D + 6 * NT)

        bank = [ctx.enter_context(nc.psum_tensor(f"bank{i}", [128, 512], F32)) for i in range(8)]

        ident = sb("ident", [128, 128]); ident_bf = sb("ident_bf", [128, 128], BF16)
        iota_slot = sb("iota_slot", [128, MAXJ * SLOTS + SLOTS])
        iota_lo = iota_slot[:, 0:32]
        neg_part = sb("neg_part", [128, 1])
        ones = sb("ones", [128, 128]); earlier = sb("earlier", [TC, TC]); heads = sb("heads", [DH, DH])
        minus_half = sb("minus_half", [128, NC])
        hat1 = early("hat1", [128, NBATCH, NIMG]); hat2 = sb("hat2", [32, NBATCH, NIMG])
        hat_t = early("hat_t", [128, NBATCH, NIMG])
        off1 = sb("off1", [128, NBATCH]); off2 = sb("off2", [32, NBATCH])
        x0 = early("x0", [128, 6, 32]); x1 = early("x1", [128, 6, 2, 16]); x2 = early("x2", [128, 6, 4, 8])
        x1r = early("x1r", [128, 24, 8]); x2r = early("x2r", [128, 96, 2])
        idx = sb("idx", [128, NQ], I32); hi_i = sb("hi_i", [128, NQ], I32); lo_i = sb("lo_i", [128, NQ], I32)
        hi_bf = sb("hi_bf", [128, NQ], BF16); lo_f = sb("lo_f", [128, NQ])
        lo_mask = [early("lo_mask0", [128, 32, 32]), early("lo_mask1", [128, 8, 8]), early("lo_mask2", [128, 2, 2])]
        hot_t = early("hot_t", [128, 2, 512]); hot = early("hot", [128, 2, 512])
        picked = early("picked", [128, 2, 384])
        feat = [early("feat0", [128, 2, 32 * 3]), early("feat1", [128, 2, 8 * 12]), early("feat2", [128, 2, 2 * 48])]
        w0 = early("w0", [EMB, 48]); w1 = early("w1", [EMB, 192]); w2 = early("w2", [EMB, 768])
        wf = early("wf", [DH, 2, D]); gate = early("gate", [E, D])
        eb1 = early("eb1", [E, EHID]); eb2 = early("eb2", [E, EHID]); eb3 = early("eb3", [E, BOT])
        w2T = early("w2T", [96, 8, EMB]); w0T = sb("w0T", [48, EMB]); w1T = sb("w1T", [96, 2, EMB])
        wfT = sb("wfT", [EMB, 3, D]); gateT = sb("gateT", [DH, 2, E])
        b1T = sb("b1T", [128, 4, E + 1]); b2T = sb("b2T", [128, 4, E + 1]); b3T = sb("b3T", [BOT, E + 1])
        tb = sb("tb", [EMB, 3]); bf_bc = sb("bf_bc", [TC, D])
        f0T = early("f0T", [48, 512]); f12T = early("f12T", [96, 4, 128])
        y0T = early("y0T", [EMB, 512]); y1T = sb("y1T", [EMB, 128]); y2T = sb("y2T", [EMB, 32])
        g1 = sb("g1", [128, D]); g2 = sb("g2", [32, D])
        h3 = late("h3", [TC, NC, D]); x2t = late("x2t", [TC, NC, D]); xT = late("xT", [DH + 1, 2, NT])
        h1T = late("h1T", [128, 6, NT])
        h = sb("h", [TC, NC, D]); an = sb("an", [TC, NC, D]); norm = sb("norm", [TC, NC, D])
        stats = sb("stats", [TC, NC, 6]); mv = sb("mv", [TC, NC, 2])
        var_e = sb("var_e", [TC, NC]); r1 = sb("r1", [TC, NC]); r2 = sb("r2", [TC, NC]); r12 = sb("r12", [TC, NC])
        rt = sb("rt", [TC, NC])
        qT = attn("qT", [DH, 2, NT]); oT = attn("oT", [DH + 1, 2, NT])
        qe = attn("qe", [DH, 2, NTOK]); ke = attn("ke", [TC, 2, D])
        kt = attn("kt", [TC, NC, D]); vt = attn("vt", [TC, NC, 2, DH + 1])
        kv = attn("kv", [DH, 4, DH]); ks = attn("ks", [DH, 4, DH]); ksum = sb("ksum", [DH, 4])
        den = attn("den", [DH, 2, NTOK])
        qkv_w = sb("qkv_w", [DH + 1, 2, 3 * D]); proj_w = sb("proj_w", [DH + 1, 2, D])
        fc1_w = sb("fc1_w", [DH, 2, HID]); fc2_w = sb("fc2_w", [128, 6, D])
        fc1_b = sb("fc1_b", [128, 6]); fc2_bc = sb("fc2_bc", [TC, D])
        lnw = sb("lnw", [DH, 4, 2])
        sc = routing("sc", [TC, NC, E]); sm = sb("sm", [TC, NC]); top = sb("top", [TC, NC, 8])
        topi = sb("topi", [TC, NC, 8], U32); topf = sb("topf", [TC, NC, 2]); tw = sb("tw", [TC, NC, 2])
        tws = sb("tws", [TC, NC]); oneh = routing("oneh", [TC, 2, NC, E]); sel = routing("sel", [TC, NC, E])
        cnt = routing("cnt", [TC, NC, E]); pre = routing("pre", [TC, NC + 1, E]); rank = routing("rank", [TC, NC, E])
        place = routing("place", [TC, NC, E]); placed = routing("placed", [TC, NC, E]); slot_of = routing("slot_of", [TC, NC, E])
        dest_f = sb("dest_f", [TC, NC, 2]); dest = sb("dest", [TC, NC, 2], I32)
        blk_i = sb("blk_i", [TC, 2, E], I32); blk_f = sb("blk_f", [TC, E]); cum = sb("cum", [TC, 2, E])
        sched = sb("sched", [1, 2, E], I32)
        ew1 = [sb(f"ew1_{s}", [DH, 2, EHID]) for s in range(WBUF)]
        ew2 = [sb(f"ew2_{s}", [128, 4, EHID]) for s in range(WBUF)]
        ew3 = [sb(f"ew3_{s}", [128, 4, BOT]) for s in range(WBUF)]
        ewl = [sb(f"ewl_{s}", [BOT + 1, D]) for s in range(WBUF)]
        zero = sb("zero", [SLOTS, D])
        onehot = routing("onehot", [TC, NC, SLOTS]); distance = routing("distance", [TC, NC, SLOTS])
        bxT = routing("bxT", [DH, 2, SLOTS]); bh1 = routing("bh1", [128, 4, SLOTS]); bh2 = routing("bh2", [128, 4, SLOTS])
        bz = sb("bz", [BOT + 1, SLOTS]); by = routing("by", [SLOTS, D])
        base = an
        picked_y = h1T[0:TC, :, 0:2 * D].rearrange("p c (k d) -> p c k d", k=2)

        s_x = sem("x_loaded"); s_x12 = sem("x12_loaded"); s_idx = sem("idx_loaded")
        s_tw = sem("token_weights_loaded"); s_aw = sem("attn_weights_loaded"); s_txt = sem("text_loaded")
        s_id = sem("identity_built"); s_cst = sem("constants_built"); s_off = sem("hat_offsets_built")
        s_wT = sem("weights_turned"); s_wTc = sem("turned_weights_copied")
        s_hi = sem("hi_ready"); s_bc = sem("hi_spread"); s_hot = sem("hi_onehot_ready"); s_gat = sem("pair_gathered")
        s_pick = sem("pair_picked"); s_xr = sem("x_reordered"); s_hatp = sem("hat_position"); s_hat = sem("hats_built")
        s_fT = sem("features_turned"); s_fTc = sem("features_copied"); s_y = sem("levels_done"); s_yc = sem("levels_copied")
        s_g = sem("level_fused"); s_gc = sem("level_fused_copied"); s_h = sem("h_summed"); s_hc = sem("h_ready")
        s_st = sem("stats_ready"); s_r = sem("rstd_ready"); s_n = sem("normed"); s_nT = sem("normed_turned")
        s_xT = sem("xT_ready"); s_q = sem("q_done"); s_qe = sem("q_exp"); s_qc = sem("q_ready")
        s_kv = sem("kv_done"); s_ke = sem("k_exp"); s_vc = sem("v_ready"); s_kc = sem("k_ready")
        s_kvs = sem("kv_summed"); s_kvc = sem("kv_ready"); s_o = sem("attn_out"); s_oc = sem("attn_out_ready")
        s_pr = sem("proj_done"); s_x2 = sem("x2_ready"); s_base = sem("base_ready")
        s_f1 = sem("fc1_done"); s_f1c = sem("fc1_ready"); s_f2 = sem("fc2_done"); s_h3 = sem("h3_ready")
        s_lg = sem("logits_done"); s_mx = sem("logits_shifted"); s_ex = sem("exp_done"); s_sel = sem("selected")
        s_rk = sem("ranks_done"); s_sched = sem("schedule_ready"); s_bzo = sem("ones_row_set")
        s_dist = sem("block_distance_ready"); s_hot_b = sem("block_onehot_ready"); s_gb = sem("block_gathered"); s_bx = sem("block_x_ready")
        s_w1 = [sem(f"block_w1_done_{g}") for g in range(2)]; s_h1 = sem("block_h1_ready"); s_w2 = [sem(f"block_w2_done_{g}") for g in range(2)]
        s_h2 = sem("block_h2_ready"); s_w3 = sem("block_w3_done"); s_z = sem("block_z_ready")
        s_wl = sem("block_wl_done"); s_by = sem("block_y_ready"); s_ys = sem("block_y_stored")
        s_ed = sem("expert_done"); s_ew = [sem(f"expert_weights_{s}") for s in range(WBUF)]
        s_pk = sem("rows_picked"); s_o1 = sem("weighted"); s_fin = sem("out_ready"); s_zero = sem("zeros_ready"); s_out = sem("out_stored")
        s_dc = sem("vector_chain"); s_pc = sem("pool_chain"); s_ac = sem("scalar_chain"); s_ones = sem("ones_rows")

        block = ctx.enter_context(nc.Block())

        def trips(eng, e):
            n = eng.value_load(sched[0:1, 0, bass.ds(e, 1)], min_val=1, max_val=MAXJ)
            first = eng.value_load(sched[0:1, 1, bass.ds(e, 1)], min_val=0, max_val=MAXB)
            return n, first

        def chained(eng, s):
            count = [0]

            def link(ins):
                count[0] += 1
                ins.then_inc(s, 1)
                eng.wait_ge(s, count[0])
            return link

        def load_expert(sp, e, s):
            def at(name):
                return a[name][bass.ds(e, 1)]
            sp.dma_start(ew1[s][:, :, :], at("L0_ffn_W1").rearrange("o (k p) h -> p (o k) h", p=DH)).then_inc(s_ew[s], 16)
            sp.dma_start(ew2[s][:, :, :], at("L0_ffn_W2").rearrange("o (k p) h -> p (o k) h", p=128)).then_inc(s_ew[s], 16)
            sp.dma_start(ew3[s][:, :, :], at("L0_ffn_W3").rearrange("o (k p) h -> p (o k) h", p=128)).then_inc(s_ew[s], 16)
            sp.dma_start(ewl[s][0:BOT, :], at("L0_ffn_Wl").rearrange("o p h -> (o p) h")).then_inc(s_ew[s], 16)
            sp.dma_start(ewl[s][BOT:BOT + 1, :], at("L0_ffn_bl")).then_inc(s_ew[s], 16)

        @block.sync
        def _(sp):
            sp.dma_start(idx[:, 0:32].rearrange("p (t g) -> p t g", t=2), dv["i0"]).then_inc(s_idx, 16)
            sp.dma_start(idx[:, 32:40], dv["i1"]).then_inc(s_idx, 16)
            sp.dma_start(idx[:, 40:42], dv["i2"]).then_inc(s_idx, 16)
            sp.dma_start(x0[:, :, :], dv["x0"]).then_inc(s_x, 16)
            for i in range(4):
                for bc in range(6):
                    sp.dma_start(x1[i:128:4, bc, :, :], dv["x1"][i, :, bc]).then_inc(s_x12, 16)
            for i in range(8):
                for bc in range(6):
                    sp.dma_start(x2[i:128:8, bc, :, :], dv["x2"][i, :, bc]).then_inc(s_x12, 16)
            for s in range(WBUF):
                load_expert(sp, s, s)
            sp.wait_ge(s_zero, 1)
            sp.dma_start(ydram[E * SLOTS:, :].rearrange("(k p) d -> p k d", p=SLOTS),
                         zero[:, :].unsqueeze(1).to_broadcast([SLOTS, MAXB + MAXJ - E, D])).then_inc(s_ys, 16)
            sp.wait_ge(s_ys, 16)
            sp.wait_ge(s_sched, 1)

            def store_rows(n, first):
                with sp.Fori(0, n) as j:
                    b = sp.snap(first + j)
                    sp.wait_ge(s_by, b + 1)
                    sp.nop(nofuse=True)
                    sp.dma_start(ydram[bass.ds(b * SLOTS, SLOTS), :], by[:, :]).then_inc(s_ys, 16)

            with sp.Fori(0, E // WBUF - 1) as i:
                for s in range(WBUF):
                    e = sp.snap(i * WBUF + s)
                    n, first = trips(sp, e)
                    store_rows(n, first)
                    sp.wait_ge(s_ed, e + 1)
                    sp.nop(nofuse=True)
                    load_expert(sp, e + WBUF, s)
            with sp.Fori(E - WBUF, E) as e:
                n, first = trips(sp, e)
                store_rows(n, first)
            for c in range(NC):
                sp.wait_ge(s_fin, c + 1)
                sp.dma_start(out_chunks[c], an[:, c, :]).then_inc(s_out, 16)
            sp.wait_ge(s_out, 16 * NC)

        @block.gpsimd
        def _(pool):
            link = chained(pool, s_pc)
            link(pool.memset(ident[:, :], 0.0))
            link(pool.affine_select(out=ident[:, :], in_=ident[:, :], compare_op=ALU.not_equal, fill=1.0, base=0,
                                    pattern=[[-1, 128]], channel_multiplier=1))
            pool.tensor_copy(ident_bf[:, :], ident[:, :]).then_inc(s_id, 1)
            pool.iota(neg_part[:, :], [[0, 1]], base=0, channel_multiplier=-1,
                      allow_small_or_imprecise_dtypes=True).then_inc(s_id, 1)
            pool.iota(iota_slot[:, :], [[1, MAXJ * SLOTS + SLOTS]], base=0, channel_multiplier=0,
                      allow_small_or_imprecise_dtypes=True).then_inc(s_id, 1)
            pool.iota(hat_t[:, :, :], [[0, NBATCH], [1, NIMG]], base=0, channel_multiplier=0,
                      allow_small_or_imprecise_dtypes=True).then_inc(s_off, 1)
            pool.iota(off1[:, :], [[64, NBATCH]], base=0, channel_multiplier=-1,
                      allow_small_or_imprecise_dtypes=True).then_inc(s_off, 1)
            pool.iota(off2[:, :], [[16, NBATCH]], base=0, channel_multiplier=-1,
                      allow_small_or_imprecise_dtypes=True).then_inc(s_off, 1)
            pool.memset(ones[:, :], 1.0).then_inc(s_cst, 1)
            pool.memset(minus_half[:, :], -0.5).then_inc(s_cst, 1)
            link(pool.memset(earlier[:, :], 1.0))
            pool.affine_select(out=earlier[:, :], in_=earlier[:, :], compare_op=ALU.is_gt, fill=0.0, base=0,
                               pattern=[[1, TC]], channel_multiplier=-1).then_inc(s_cst, 1)
            link(pool.memset(heads[:, :], 1.0))
            hv = heads[:, :].rearrange("p (h d) -> p h d", d=HEAD)
            link(pool.affine_select(out=hv, in_=hv, compare_op=ALU.is_ge, fill=0.0, base=0,
                                    pattern=[[-HEAD, DH // HEAD], [0, HEAD]], channel_multiplier=1))
            pool.affine_select(out=hv, in_=hv, compare_op=ALU.is_ge, fill=0.0, base=HEAD - 1,
                               pattern=[[HEAD, DH // HEAD], [0, HEAD]], channel_multiplier=-1).then_inc(s_cst, 1)

            for i, name in enumerate(("L0_tok_W0", "L0_tok_W1", "L0_tok_W2")):
                pool.dma_start((w0, w1, w2)[i][:, :], a[name]).then_inc(s_tw, 16)
            pool.dma_start(wf[:, :, :], a["L0_tok_Wf"].rearrange("(k p) d -> p k d", p=DH)).then_inc(s_tw, 16)
            pool.dma_start(gate[:, :], a["L0_ffn_gate_w"]).then_inc(s_tw, 16)
            for t, name in ((eb1, "L0_ffn_b1"), (eb2, "L0_ffn_b2"), (eb3, "L0_ffn_b3")):
                pool.dma_start(t[:, :], a[name]).then_inc(s_tw, 16)
            for i in range(3):
                pool.dma_start(tb[:, i:i + 1], column(a[f"L0_tok_b{i}"])).then_inc(s_tw, 16)
            pool.dma_start(bf_bc[:, :], row(a["L0_tok_bf"]).to_broadcast([TC, D])).then_inc(s_tw, 16)
            for b in range(NBATCH):
                pool.dma_start(h[TC - TXT:TC, CPB * b + CPB - 1, :], a["txt"][b]).then_inc(s_txt, 16)
            pool.dma_start(qkv_w[0:DH, :, :], a["L0_attn_qkv_w"].rearrange("(k p) n -> p k n", p=DH)).then_inc(s_aw, 16)
            pool.dma_start(qkv_w[DH:DH + 1, 1, :], row(a["L0_attn_qkv_b"])).then_inc(s_aw, 16)
            pool.dma_start(proj_w[0:DH, :, :], a["L0_attn_proj_w"].rearrange("(k p) n -> p k n", p=DH)).then_inc(s_aw, 16)
            pool.dma_start(proj_w[DH:DH + 1, 1, :], row(a["L0_attn_proj_b"])).then_inc(s_aw, 16)
            for i, name in enumerate(("ln1_w", "ln1_b", "ln2_w", "ln2_b")):
                for k in range(2):
                    pool.dma_start(lnw[:, i, k:k + 1], column(a[f"L0_attn_{name}"][k * DH:(k + 1) * DH])).then_inc(s_aw, 16)
            pool.dma_start(fc1_w[:, :, :], a["L0_attn_fc1_w"].rearrange("(k p) n -> p k n", p=DH)).then_inc(s_aw, 16)
            pool.dma_start(fc2_w[:, :, :], a["L0_attn_fc2_w"].rearrange("(k p) n -> p k n", p=128)).then_inc(s_aw, 16)
            for k in range(6):
                pool.dma_start(fc1_b[:, k:k + 1], column(a["L0_attn_fc1_b"][k * 128:(k + 1) * 128])).then_inc(s_aw, 16)
            pool.dma_start(fc2_bc[:, :], row(a["L0_attn_fc2_b"]).to_broadcast([TC, D])).then_inc(s_aw, 16)

            pool.wait_ge(s_st, 1)
            link(pool.tensor_scalar(var_e[:, :], mv[:, :, 1], 1e-5, None, ALU.add))
            link(pool.tensor_tensor(r1[:, :], var_e[:, :], minus_half[0:TC, :], ALU.pow))
            link(pool.tensor_tensor(rt[:, :], r1[:, :], r1[:, :], ALU.mult))
            link(pool.tensor_tensor(rt[:, :], rt[:, :], mv[:, :, 1], ALU.mult))
            link(pool.tensor_scalar(rt[:, :], rt[:, :], 1e-8, None, ALU.add))
            link(pool.tensor_tensor(r2[:, :], rt[:, :], minus_half[0:TC, :], ALU.pow))
            pool.tensor_tensor(r12[:, :], r1[:, :], r2[:, :], ALU.mult).then_inc(s_r, 1)
            pool.wait_ge(s_r, 1)
            for t in (oT, xT):
                link(pool.memset(t[DH:DH + 1, 1, :], 1.0))
            link(pool.memset(bz[BOT:BOT + 1, :], 1.0))
            pool.memset(vt[:, :, :, DH:DH + 1], 1.0).then_inc(s_ones, 1)
            pool.wait_ge(s_st, 2)
            link(pool.tensor_scalar(var_e[:, :], mv[:, :, 1], 1e-8, None, ALU.add))
            pool.tensor_tensor(r1[:, :], var_e[:, :], minus_half[0:TC, :], ALU.pow).then_inc(s_r, 1)
            pool.wait_ge(s_aw, 16 * 21)
            for c in range(NC):
                link(pool.tensor_tensor(base[:, c, :], h[:, c, :], x2t[:, c, :], ALU.add))
                pool.tensor_tensor(base[:, c, :], base[:, c, :], fc2_bc[:, :], ALU.add).then_inc(s_base, 1)
            pool.wait_ge(s_st, 3)
            link(pool.tensor_scalar(var_e[:, :], mv[:, :, 1], 1e-5, None, ALU.add))
            pool.tensor_tensor(r1[:, :], var_e[:, :], minus_half[0:TC, :], ALU.pow).then_inc(s_r, 1)

            pool.wait_ge(s_sched, 1)

            def slot_distance(e, j, b):
                pool.wait_ge(s_hot_b, b + 1)
                pool.nop(nofuse=True)
                pool.tensor_tensor(distance[:, :, :],
                                   iota_slot[0:TC, bass.ds(j * SLOTS, SLOTS)].unsqueeze(1).to_broadcast([TC, NC, SLOTS]),
                                   slot_of[:, :, bass.ds(e, 1)].to_broadcast([TC, NC, SLOTS]),
                                   ALU.subtract).then_inc(s_dist, 1)

            with pool.Fori(0, E) as e:
                n, first = trips(pool, e)
                with pool.Fori(0, n) as j:
                    slot_distance(e, j, pool.snap(first + j))
            n, first = trips(pool, E - 1)
            last = pool.snap(first + n)
            slot_distance(E - 1, 0, last)
            slot_distance(E - 1, 0, pool.snap(last + 1))

            pool.wait_ge(s_ys, last * 16 + 16)
            pool.nop(nofuse=True)
            for c in range(NC):
                for k in range(2):
                    pool.indirect_dma_start(out=picked_y[:, c, k, :], out_offset=None, in_=ydram[:, :],
                                            in_offset=bass.IndirectOffsetOnAxis(ap=dest[:, c, k:k + 1], axis=0)
                                            ).then_inc(s_pk, 16)

        @block.vector
        def _(dve):
            link = chained(dve, s_dc)
            dve.memset(zero[:, :], 0.0).then_inc(s_zero, 1)
            dve.wait_ge(s_idx, 48)
            for (at, n), bits in zip(((0, 32), (32, 8), (40, 2)), (5, 3, 1)):
                dve.tensor_scalar(hi_i[:, at:at + n], idx[:, at:at + n], bits, None, ALU.logical_shift_right)
                last = dve.tensor_scalar(lo_i[:, at:at + n], idx[:, at:at + n], (1 << bits) - 1, None, ALU.bitwise_and)
            link(last)
            dve.tensor_copy(hi_bf[:, :], hi_i[:, :]).then_inc(s_hi, 1)
            link(dve.tensor_copy(lo_f[:, :], lo_i[:, :]))
            dve.wait_ge(s_id, 3)
            for l, (at, n) in enumerate(((0, 32), (32, 8), (40, 2))):
                w = 1 << LEVELS[l][1]
                last = dve.tensor_tensor(lo_mask[l][:, :, :], iota_lo[:, 0:w].unsqueeze(1).to_broadcast([128, n, w]),
                                         lo_f[:, at:at + n].unsqueeze(2).to_broadcast([128, n, w]), ALU.is_equal)
            link(last)
            dve.wait_ge(s_off, 3)
            for l, (t, n) in enumerate(((hat1, 64), (hat2, 16))):
                p = t.shape[0]
                link(dve.tensor_scalar(t[:, :, :], hat_t[0:p, :, :], n / NIMG, 0.5 * n / NIMG - 0.5, ALU.mult, ALU.add))
                dve.tensor_scalar(t[:, :, :], t[:, :, :], 0.0, float(n - 1), ALU.max, ALU.min).then_inc(s_hatp, 1)
            for i, (q, l) in enumerate(PAIRS):
                f, w = LEVELS[l][2], 1 << LEVELS[l][1]
                q0 = q - (0, 32, 40)[l]
                dve.wait_ge(s_gat, i + 1)
                tmp = picked[:, i % 2, :].rearrange("p (k f w) -> p k f w", k=2, w=w)
                link(dve.tensor_tensor(tmp, bank[6 + i % 2][:, 0:384].rearrange("p (k f w) -> p k f w", k=2, w=w),
                                       lo_mask[l][:, q0:q0 + 2, :].unsqueeze(2).to_broadcast([128, 2, f, w]), ALU.mult))
                dst = feat[l][:, :, :].rearrange("p b (k f) -> p k b f", f=f // 2)[:, q0:q0 + 2]
                src = picked[:, i % 2, :].rearrange("p (k b f w) -> p k b f w", k=2, b=2, w=w)
                dve.tensor_reduce(dst, src, AX_X, ALU.add).then_inc(s_pick, 1)
            dve.wait_ge(s_fT, 2)
            dve.tensor_copy(f12T[:, :, :], bank[1][0:96, :].rearrange("p (a q) -> p a q", a=4)).then_inc(s_fTc, 1)
            dve.wait_ge(s_y, 2)
            dve.wait_ge(s_tw, 16 * 12)
            dve.tensor_scalar(y1T[:, :], bank[3][0:EMB, 0:128], tb[:, 1:2], None, ALU.add).then_inc(s_yc, 1)
            dve.tensor_scalar(y2T[:, :], bank[3][0:EMB, 128:160], tb[:, 2:3], None, ALU.add).then_inc(s_yc, 1)
            dve.wait_ge(s_txt, 32)
            for c in range(NC):
                m = TC if c % CPB < CPB - 1 else TC - TXT
                dve.wait_ge(s_h, c + 1)
                link(dve.tensor_tensor(h[0:m, c, :], bank[6 + c % 2][0:m, 0:D], bf_bc[0:m, :], ALU.add))
                s_hc_ins = dve.bn_stats(stats[:, c, :], h[:, c, :])
                link(s_hc_ins)
                ins = dve.bn_aggr(mv[:, c, :], stats[:, c, :])
                ins.then_inc(s_hc, 1)
            dve.wait_ge(s_hc, NC)
            dve.nop(nofuse=True).then_inc(s_st, 1)

            def normalise(dst, src, scale, c):
                return dve.tensor_scalar(dst[:, c, :], src[:, c, :], mv[:, c, 0:1], scale[:, c:c + 1],
                                         ALU.subtract, ALU.mult)

            def turned(first, k_lnw):
                for k in range(2):
                    for b in range(NBATCH):
                        i = 2 * k + b
                        dve.wait_ge(s_nT, first + i + 1)
                        dst = xT[0:DH, k, b * NTOK:(b + 1) * NTOK]
                        if k_lnw is None:
                            ins = dve.tensor_copy(dst, bank[i][0:DH, 0:NTOK])
                        else:
                            ins = dve.tensor_scalar(dst, bank[i][0:DH, 0:NTOK], lnw[:, k_lnw, k:k + 1],
                                                    lnw[:, k_lnw + 1, k:k + 1], ALU.mult, ALU.add)
                        ins.then_inc(s_xT, 1)

            dve.wait_ge(s_r, 1)
            for c in range(NC):
                normalise(norm, h, r12, c).then_inc(s_n, 1)
            for c in range(NC):
                last = normalise(an, h, r1, c)
            link(last)
            dve.wait_ge(s_aw, 16 * 21)
            turned(0, 0)
            for i in range(4):
                m, b = i // 2, i % 2
                dve.wait_ge(s_qe, i + 1)
                link(dve.tensor_scalar(qe[:, i % 2, :], qe[:, i % 2, :], 1.0, None, ALU.min))
                dve.scalar_tensor_tensor(out=qT[:, m, b * NTOK:(b + 1) * NTOK], in0=bank[4 + i][0:DH, 0:NTOK], scalar=0.0,
                                         in1=qe[:, i % 2, :], op0=ALU.max, op1=ALU.add).then_inc(s_qc, 1)
            for c in range(NC):
                dve.wait_ge(s_ke, c + 1)
                link(dve.tensor_scalar(ke[:, c % 2, :], ke[:, c % 2, :], 1.0, None, ALU.min))
                dve.scalar_tensor_tensor(out=kt[:, c, :], in0=bank[c % 2][0:TC, 0:D], scalar=0.0,
                                         in1=ke[:, c % 2, :], op0=ALU.max, op1=ALU.add).then_inc(s_kc, 1)
            dve.wait_ge(s_cst, 4)
            dve.wait_ge(s_kvs, 1)
            kvp = bank[2][0:DH, 0:4 * (DH + 1)].rearrange("p (g n) -> p g n", g=4)
            dve.tensor_tensor(kv[:, :, :], kvp[:, :, 0:DH], heads[:, :].unsqueeze(1).to_broadcast([DH, 4, DH]), ALU.mult).then_inc(s_kvc, 1)
            link(dve.tensor_copy(ksum[:, :], kvp[:, :, DH]))
            dve.tensor_tensor(ks[:, :, :], heads[:, :].unsqueeze(1).to_broadcast([DH, 4, DH]),
                              ksum[:, :].unsqueeze(2).to_broadcast([DH, 4, DH]), ALU.mult).then_inc(s_kvc, 1)
            for i in range(4):
                b, m = i // 2, i % 2
                dve.wait_ge(s_o, i + 1)
                link(dve.reciprocal(den[:, i % 2, :], bank[6 + i % 2][0:DH, 0:NTOK]))
                dve.tensor_tensor(oT[0:DH, m, b * NTOK:(b + 1) * NTOK], bank[4 + i % 2][0:DH, 0:NTOK], den[:, i % 2, :],
                                  ALU.mult).then_inc(s_oc, 1)
            for c in range(NC):
                dve.wait_ge(s_pr, c + 1)
                ins = dve.tensor_tensor(x2t[:, c, :], bank[c % 2][0:TC, 0:D], an[:, c, :], ALU.add)
                ins.then_inc(s_x2, 1)
                dve.wait_ge(s_x2, c + 1)
                link(dve.bn_stats(stats[:, c, :], x2t[:, c, :]))
                link(dve.bn_aggr(mv[:, c, :], stats[:, c, :]))
            dve.nop(nofuse=True).then_inc(s_st, 1)
            dve.wait_ge(s_r, 2)
            for c in range(NC):
                normalise(norm, x2t, r1, c).then_inc(s_n, 1)
            turned(4, 2)
            for c in range(NC):
                dve.wait_ge(s_base, c + 1)
                dve.wait_ge(s_f2, c + 1)
                ins = dve.tensor_tensor(h3[:, c, :], bank[c % 2][0:TC, 0:D], base[:, c, :], ALU.add)
                ins.then_inc(s_h3, 1)
                dve.wait_ge(s_h3, c + 1)
                link(dve.bn_stats(stats[:, c, :], h3[:, c, :]))
                link(dve.bn_aggr(mv[:, c, :], stats[:, c, :]))
            dve.nop(nofuse=True).then_inc(s_st, 1)
            dve.wait_ge(s_r, 3)
            for c in range(NC):
                normalise(norm, h3, r1, c).then_inc(s_n, 1)
            turned(8, None)

            dve.wait_ge(s_lg, 1)
            lg = bank[4][0:TC, 0:NC * E].rearrange("p (c e) -> p c e", c=NC)
            link(dve.tensor_reduce(sm[:, :], lg, AX_X, ALU.max))
            dve.tensor_tensor(sc[:, :, :], lg, sm[:, :].unsqueeze(2).to_broadcast([TC, NC, E]), ALU.subtract).then_inc(s_mx, 1)
            dve.wait_ge(s_ex, 1)
            link(dve.tensor_reduce(sm[:, :], sc[:, :, :], AX_X, ALU.add))
            link(dve.reciprocal(sm[:, :], sm[:, :]))
            link(dve.tensor_tensor(sc[:, :, :], sc[:, :, :], sm[:, :].unsqueeze(2).to_broadcast([TC, NC, E]), ALU.mult))
            for c in range(NC):
                last = dve.max(top[:, c, :], sc[:, c, :])
            link(last)
            for c in range(NC):
                last = dve.max_index(topi[:, c, :], top[:, c, :], sc[:, c, :])
            link(last)
            link(dve.tensor_copy(topf[:, :, :], topi[:, :, 0:2]))
            for k in range(2):
                last = dve.tensor_tensor(oneh[:, k, :, :], iota_slot[0:TC, 0:E].unsqueeze(1).to_broadcast([TC, NC, E]),
                                         topf[:, :, k:k + 1].to_broadcast([TC, NC, E]), ALU.is_equal)
            link(last)
            ins = dve.tensor_tensor(sel[:, :, :], oneh[:, 0, :, :], oneh[:, 1, :, :], ALU.add)
            ins.then_inc(s_sel, 1)
            link(dve.tensor_tensor(tws[:, :], top[:, :, 0], top[:, :, 1], ALU.add))
            link(dve.tensor_scalar(tws[:, :], tws[:, :], 1e-20, None, ALU.add))
            link(dve.reciprocal(tws[:, :], tws[:, :]))
            link(dve.tensor_tensor(tw[:, :, :], top[:, :, 0:2], tws[:, :].unsqueeze(2).to_broadcast([TC, NC, 2]), ALU.mult))
            dve.wait_ge(s_rk, 1)
            link(dve.tensor_copy(cnt[:, :, :], bank[5][0:TC, 0:NC * E].rearrange("p (c e) -> p c e", c=NC)))
            link(dve.memset(pre[:, 0, :], 0.0))
            for c in range(NC):
                link(dve.tensor_tensor(pre[:, c + 1, :], pre[:, c, :], cnt[:, c, :], ALU.add))
            link(dve.tensor_tensor(rank[:, :, :], bank[5][0:TC, NC * E:2 * NC * E].rearrange("p (c e) -> p c e", c=NC),
                                   pre[:, 0:NC, :], ALU.add))
            link(dve.tensor_scalar(blk_f[:, :], pre[:, NC, :], float(SLOTS - 1), float(SLOTS), ALU.add, ALU.max))
            link(dve.tensor_copy(blk_i[:, 0, :], blk_f[:, :]))
            link(dve.tensor_scalar(blk_i[:, 1, :], blk_i[:, 0, :], SLOTS.bit_length() - 1, None, ALU.logical_shift_right))
            link(dve.tensor_copy(blk_f[:, :], blk_i[:, 1, :]))
            link(dve.tensor_copy(cum[:, 0, :], blk_f[:, :]))
            at, step = 0, 1
            while step < E:
                dve.tensor_copy(cum[:, 1 - at, 0:step], cum[:, at, 0:step])
                link(dve.tensor_tensor(cum[:, 1 - at, step:E], cum[:, at, step:E], cum[:, at, 0:E - step], ALU.add))
                at, step = 1 - at, 2 * step
            link(dve.tensor_tensor(cum[:, 1 - at, :], cum[:, at, :], blk_f[:, :], ALU.subtract))
            first_blk = cum[:, 1 - at, :]
            link(dve.tensor_scalar(placed[:, :, :], rank[:, :, :], 1.0, None, ALU.add))
            link(dve.tensor_tensor(placed[:, :, :], placed[:, :, :], sel[:, :, :], ALU.mult))
            link(dve.tensor_scalar(slot_of[:, :, :], placed[:, :, :], -1.0, None, ALU.add))
            dve.tensor_copy(sched[:, 0, :], blk_f[0:1, :])
            link(dve.tensor_copy(sched[:, 1, :], first_blk[0:1, :]))
            dve.nop(nofuse=True).then_inc(s_sched, 1)
            link(dve.scalar_tensor_tensor(out=place[:, :, :], in0=first_blk.unsqueeze(1).to_broadcast([TC, NC, E]),
                                          scalar=float(SLOTS), in1=rank[:, :, :], op0=ALU.mult, op1=ALU.add))
            for k in range(2):
                link(dve.tensor_tensor(placed[:, :, :], place[:, :, :], oneh[:, k, :, :], ALU.mult))
                link(dve.tensor_reduce(dest_f[:, :, k], placed[:, :, :], AX_X, ALU.add))
            link(dve.tensor_copy(dest[:, :, :], dest_f[:, :, :]))

            def copy_x(b1):
                dve.wait_ge(s_gb, b1)
                dve.nop(nofuse=True)
                dve.tensor_copy(bxT[:, :, :], bank[4][0:DH, 0:2 * SLOTS].rearrange("p (k s) -> p k s", k=2)).then_inc(s_bx, 1)

            def slots_onehot(b1):
                dve.wait_ge(s_dist, b1)
                dve.nop(nofuse=True)
                dve.tensor_scalar(onehot[:, :, :], distance[:, :, :], 0.0, None, ALU.is_equal).then_inc(s_hot_b, 1)

            dve.nop(nofuse=True).then_inc(s_hot_b, 1)
            slots_onehot(1)
            copy_x(1)
            slots_onehot(2)
            with dve.Fori(0, E) as e:
                n, first = trips(dve, e)
                with dve.Fori(0, n) as j:
                    b = dve.snap(first + j)
                    copy_x(b + 2)
                    slots_onehot(b + 3)
                    dve.wait_ge(s_w3, b + 1)
                    dve.nop(nofuse=True)
                    dve.tensor_scalar(bz[0:BOT, :], bank[5][0:BOT, 0:SLOTS], b3T[:, bass.ds(e, 1)], None, ALU.add).then_inc(s_z, 1)
                    dve.wait_ge(s_wl, b + 1)
                    dve.nop(nofuse=True)
                    dve.wait_ge(s_ys, b * 16 + 16)
                    dve.nop(nofuse=True)
                    dve.tensor_copy(by[:, :], bank[6][0:SLOTS, 0:D]).then_inc(s_by, 1)

            dve.wait_ge(s_pk, 16 * 2 * NC)
            for c in range(NC):
                link(dve.scalar_tensor_tensor(out=norm[:, c, :], in0=picked_y[:, c, 0, :], scalar=tw[:, c, 0:1],
                                              in1=h3[:, c, :], op0=ALU.mult, op1=ALU.add))
                dve.scalar_tensor_tensor(out=an[:, c, :], in0=picked_y[:, c, 1, :], scalar=tw[:, c, 1:2],
                                         in1=norm[:, c, :], op0=ALU.mult, op1=ALU.add).then_inc(s_fin, 1)

        @block.scalar
        def _(act):
            link = chained(act, s_ac)
            act.wait_ge(s_x12, 16 * 72)
            for b in range(NBATCH):
                for iy in range(2):
                    o = b * 12 + iy * 6
                    act.copy(x1r[:, o:o + 6, :].rearrange("p (x c) l -> p c x l", c=3),
                             x1[:, 3 * b:3 * b + 3, iy, :].rearrange("p c (l x) -> p c x l", x=2)).then_inc(s_xr, 1)
                for iy in range(4):
                    o = b * 48 + iy * 12
                    act.copy(x2r[:, o:o + 12, :].rearrange("p (x c) l -> p c x l", c=3),
                             x2[:, 3 * b:3 * b + 3, iy, :].rearrange("p c (l x) -> p c x l", x=4)).then_inc(s_xr, 1)
            act.wait_ge(s_id, 3)
            for g, (q, n) in enumerate(GROUPS):
                act.wait_ge(s_bc, g + 1)
                if g >= 2:
                    act.wait_ge(s_gat, 2 * (g - 1))
                link(act.activation(hot_t[:, g % 2, 0:n * 128], bank[4 + g % 2][:, 0:n * 128], ACT.Abs, bias=neg_part[:, 0:1]))
                act.activation(hot[:, g % 2, 0:n * 128], hot_t[:, g % 2, 0:n * 128], ACT.Relu, scale=-1.0, bias=1.0).then_inc(s_hot, 1)
            act.wait_ge(s_hatp, 2)
            for t, o in ((hat1, off1), (hat2, off2)):
                for b in range(NBATCH):
                    link(act.activation(t[:, b, :], t[:, b, :], ACT.Abs, bias=o[:, b:b + 1]))
            for t in (hat1, hat2):
                act.activation(t[:, :, :], t[:, :, :], ACT.Relu, scale=-1.0, bias=1.0).then_inc(s_hat, 1)
            act.wait_ge(s_wT, 1)
            act.copy(w2T[:, :, :], bank[0][0:96, :].rearrange("p (g e) -> p g e", g=8)).then_inc(s_wTc, 1)
            act.wait_ge(s_wT, 2)
            act.copy(w0T[:, :], bank[1][0:48, 0:64]).then_inc(s_wTc, 1)
            act.copy(w1T[:, :, :], bank[1][0:96, 64:192].rearrange("p (g e) -> p g e", g=2)).then_inc(s_wTc, 1)
            act.copy(wfT[:, 2, :], bank[1][0:EMB, 192:384]).then_inc(s_wTc, 1)
            act.wait_ge(s_wT, 3)
            act.copy(wfT[:, 0:2, :], bank[2][0:EMB, 0:384].rearrange("p (l d) -> p l d", l=2)).then_inc(s_wTc, 1)
            act.wait_ge(s_wT, 4)
            act.copy(gateT[:, :, :], bank[3][0:DH, 0:64].rearrange("p (k e) -> p k e", k=2)).then_inc(s_wTc, 1)
            act.copy(b1T[:, :, 0:E], bank[3][:, 64:192].rearrange("p (k e) -> p k e", k=4)).then_inc(s_wTc, 1)
            act.copy(b2T[:, :, 0:E], bank[3][:, 192:320].rearrange("p (k e) -> p k e", k=4)).then_inc(s_wTc, 1)
            act.copy(b3T[:, 0:E], bank[3][0:BOT, 320:352]).then_inc(s_wTc, 1)
            act.wait_ge(s_fT, 1)
            act.copy(f0T[:, :], bank[0][0:48, :]).then_inc(s_fTc, 1)
            act.wait_ge(s_y, 1)
            act.wait_ge(s_tw, 16 * 12)
            act.activation(y0T[:, :], bank[2][0:EMB, :], ACT.Identity, bias=tb[:, 0:1]).then_inc(s_yc, 1)
            act.wait_ge(s_g, 1)
            act.copy(g1[:, :], bank[4][:, 0:D]).then_inc(s_gc, 1)
            act.wait_ge(s_g, 2)
            act.copy(g2[:, :], bank[5][0:32, 0:D]).then_inc(s_gc, 1)
            for i in range(4):
                act.wait_ge(s_q, i + 1)
                if i >= 2:
                    act.wait_ge(s_qc, i - 1)
                act.activation(qe[:, i % 2, :], bank[4 + i][0:DH, 0:NTOK], ACT.Exp).then_inc(s_qe, 1)
            for c in range(NC):
                act.wait_ge(s_kv, c + 1)
                if c >= 2:
                    act.wait_ge(s_kc, c - 1)
                act.activation(ke[:, c % 2, :], bank[c % 2][0:TC, 0:D], ACT.Exp).then_inc(s_vc, 1)
                act.copy(vt[:, c, :, 0:DH], bank[c % 2][0:TC, D:2 * D].rearrange("p (m e) -> p m e", m=2)).then_inc(s_ke, 1)
            for i in range(12):
                f, b = i // 2, i % 2
                act.wait_ge(s_f1, i + 1)
                act.activation(h1T[:, f, b * NTOK:(b + 1) * NTOK], bank[4 + i % 4][:, 0:NTOK], ACT.Gelu,
                               bias=fc1_b[:, f:f + 1]).then_inc(s_f1c, 1)
            act.wait_ge(s_mx, 1)
            act.activation(sc[:, :, :], sc[:, :, :], ACT.Exp).then_inc(s_ex, 1)

            act.wait_ge(s_sched, 1)

            def gelu_1(b1, e):
                for g in range(2):
                    act.wait_ge(s_w1[g], b1)
                    act.nop(nofuse=True)
                    for c in (2 * g, 2 * g + 1):
                        act.activation(bh1[:, c, :], bank[g][:, (c % 2) * SLOTS:(c % 2 + 1) * SLOTS], ACT.Gelu,
                                       bias=b1T[:, c, bass.ds(e, 1)]).then_inc(s_h1, 1)

            def gelu_2(b1, e):
                for g in range(2):
                    act.wait_ge(s_w2[g], b1)
                    act.nop(nofuse=True)
                    for c in (2 * g, 2 * g + 1):
                        act.activation(bh2[:, c, :], bank[2 + g][:, (c % 2) * SLOTS:(c % 2 + 1) * SLOTS], ACT.Gelu,
                                       bias=b2T[:, c, bass.ds(e, 1)]).then_inc(s_h2, 1)

            gelu_1(1, 0)
            with act.Fori(0, E - 1) as e:
                n, first = trips(act, e)
                with act.If(n > 1):
                    with act.Fori(1, n) as j:
                        b1 = act.snap(first + j)
                        gelu_2(b1, e)
                        gelu_1(b1 + 1, e)
                b1 = act.snap(first + n)
                gelu_2(b1, e)
                gelu_1(b1 + 1, e + 1)
            n, first = trips(act, E - 1)
            with act.If(n > 1):
                with act.Fori(1, n) as j:
                    b1 = act.snap(first + j)
                    gelu_2(b1, E - 1)
                    gelu_1(b1 + 1, E - 1)
            b1 = act.snap(first + n)
            gelu_2(b1, E - 1)

        @block.tensor
        def _(pe):
            pe.wait_ge(s_hi, 1)
            pe.wait_ge(s_id, 3)

            def spread(g):
                q, n = GROUPS[g]
                if g >= 2:
                    pe.wait_ge(s_hot, g - 1)
                for k in range(n):
                    ins = pe.matmul(bank[4 + g % 2][:, k * 128:(k + 1) * 128], hi_bf[:, q + k:q + k + 1].to_broadcast([128, 128]),
                                    ident_bf[:, :], start=True, stop=True)
                ins.then_inc(s_bc, 1)

            def gather(g):
                q, n = GROUPS[g]
                pe.wait_ge(s_hot, g + 1)
                if g == 0:
                    pe.wait_ge(s_x, 16)
                if g == 8:
                    pe.wait_ge(s_xr, 12)
                for k in range(0, n, 2):
                    i = (q + k) // 2
                    l = PAIRS[i][1]
                    rows = (x0, x1r, x2r)[l][:, :, :].rearrange("p f w -> p (f w)")
                    if i >= 2:
                        pe.wait_ge(s_pick, i - 1)
                    for kk in range(2):
                        ins = pe.matmul(bank[6 + i % 2][:, kk * D:(kk + 1) * D],
                                        hot[:, g % 2, (k + kk) * 128:(k + kk + 1) * 128], rows, start=True, stop=True)
                    ins.then_inc(s_gat, 1)

            def turn_weights():
                pe.wait_ge(s_tw, 16 * 12)
                for g in range(8):
                    ins = pe.transpose(bank[0][0:96, g * 64:(g + 1) * 64], w2[:, g * 96:(g + 1) * 96], ident[0:EMB, 0:EMB])
                ins.then_inc(s_wT, 1)
                pe.transpose(bank[1][0:48, 0:64], w0[:, :], ident[0:EMB, 0:EMB])
                for g in range(2):
                    pe.transpose(bank[1][0:96, 64 + g * 64:128 + g * 64], w1[:, g * 96:(g + 1) * 96], ident[0:EMB, 0:EMB])
                for k in range(2):
                    ins = pe.transpose(bank[1][0:EMB, 192 + k * 96:288 + k * 96], wf[:, k, 128:192], ident[0:DH, 0:DH])
                ins.then_inc(s_wT, 1)
                for l in range(2):
                    for k in range(2):
                        ins = pe.transpose(bank[2][0:EMB, l * D + k * 96:l * D + (k + 1) * 96], wf[:, k, l * 64:(l + 1) * 64],
                                           ident[0:DH, 0:DH])
                ins.then_inc(s_wT, 1)
                for k in range(2):
                    pe.transpose(bank[3][0:DH, k * 32:(k + 1) * 32], gate[:, k * DH:(k + 1) * DH], ident[0:E, 0:E])
                for i, t in enumerate((eb1, eb2)):
                    for k in range(4):
                        pe.transpose(bank[3][:, 64 + i * 128 + k * 32:96 + i * 128 + k * 32], t[:, k * 128:(k + 1) * 128],
                                     ident[0:E, 0:E])
                pe.transpose(bank[3][0:BOT, 320:352], eb3[:, :], ident[0:E, 0:E]).then_inc(s_wT, 1)

            spread(0)
            for g in range(len(GROUPS)):
                if g + 1 < len(GROUPS):
                    spread(g + 1)
                gather(g)
            turn_weights()
            pe.wait_ge(s_wTc, 9)
            pe.wait_ge(s_pick, 16)
            for b in range(NBATCH):
                for t in range(2):
                    ins = pe.transpose(bank[0][0:48, (b * 2 + t) * 128:(b * 2 + t + 1) * 128],
                                       feat[0][:, b, t * 48:(t + 1) * 48], ident[:, :])
            ins.then_inc(s_fT, 1)
            pe.wait_ge(s_pick, 21)
            for b in range(NBATCH):
                pe.transpose(bank[1][0:96, b * 128:(b + 1) * 128], feat[1][:, b, :], ident[:, :])
            for b in range(NBATCH):
                ins = pe.transpose(bank[1][0:96, 256 + b * 128:256 + (b + 1) * 128], feat[2][:, b, :], ident[:, :])
            ins.then_inc(s_fT, 1)
            pe.wait_ge(s_fTc, 2)
            pe.matmul(bank[2][0:EMB, :], w0T[:, :], f0T[:, :], start=True, stop=True).then_inc(s_y, 1)
            t1 = f12T[:, 0:2, :].rearrange("p b (t g) -> p b t g", g=2)
            t2 = f12T[:, 2:4, :].rearrange("p b (t g) -> p b t g", g=8)
            for g in range(2):
                pe.matmul(bank[3][0:EMB, 0:128], w1T[:, g, :], t1[:, :, :, g], start=(g == 0), stop=(g == 1))
            for g in range(8):
                ins = pe.matmul(bank[3][0:EMB, 128:160], w2T[:, g, :], t2[:, :, :, g], start=(g == 0), stop=(g == 7))
            ins.then_inc(s_y, 1)
            pe.wait_ge(s_yc, 3)
            pe.matmul(bank[4][:, 0:D], y1T[:, :], wfT[:, 1, :], start=True, stop=True).then_inc(s_g, 1)
            pe.matmul(bank[5][0:32, 0:D], y2T[:, :], wfT[:, 2, :], start=True, stop=True).then_inc(s_g, 1)
            pe.wait_ge(s_gc, 2)
            pe.wait_ge(s_hat, 2)
            for c in range(NC):
                b, t = c // CPB, c % CPB
                m = TC if t < CPB - 1 else TC - TXT
                if c >= 2:
                    pe.wait_ge(s_hc, c - 1)
                o = bank[6 + c % 2][0:m, 0:D]
                pe.matmul(o, y0T[:, b * NIMG + t * TC:b * NIMG + t * TC + m], wfT[:, 0, :], start=True, stop=False)
                pe.matmul(o, hat1[:, b, t * TC:t * TC + m], g1[:, :], start=False, stop=False)
                pe.matmul(o, hat2[:, b, t * TC:t * TC + m], g2[:, :], start=False, stop=True).then_inc(s_h, 1)

            def turn_normed(first):
                pe.wait_ge(s_n, first + NC)
                for k in range(2):
                    for b in range(NBATCH):
                        for t in range(CPB):
                            ins = pe.transpose(bank[2 * k + b][0:DH, t * TC:(t + 1) * TC],
                                               norm[:, b * CPB + t, k * DH:(k + 1) * DH], ident[0:TC, 0:TC])
                        ins.then_inc(s_nT, 1)

            turn_normed(0)
            pe.wait_ge(s_xT, 4)
            pe.wait_ge(s_aw, 16 * 21)
            pe.wait_ge(s_ones, 1)
            for i in range(4):
                m, b = i // 2, i % 2
                for k in range(2):
                    r = DH + k
                    ins = pe.matmul(bank[4 + i][0:DH, 0:NTOK], qkv_w[0:r, k, m * DH:(m + 1) * DH],
                                    xT[0:r, k, b * NTOK:(b + 1) * NTOK], start=(k == 0), stop=(k == 1))
                ins.then_inc(s_q, 1)
            for c in range(NC):
                if c >= 2:
                    pe.wait_ge(s_kc, c - 1)
                for k in range(2):
                    r = DH + k
                    ins = pe.matmul(bank[c % 2][0:TC, 0:2 * D], xT[0:r, k, c * TC:(c + 1) * TC], qkv_w[0:r, k, D:3 * D],
                                    start=(k == 0), stop=(k == 1))
                ins.then_inc(s_kv, 1)
            pe.wait_ge(s_cst, 4)
            pe.wait_ge(s_kc, NC)
            for b in range(NBATCH):
                for m in range(2):
                    for t in range(CPB):
                        c = b * CPB + t
                        ins = pe.matmul(bank[2][0:DH, (2 * b + m) * (DH + 1):(2 * b + m + 1) * (DH + 1)],
                                        kt[:, c, m * DH:(m + 1) * DH], vt[:, c, m, :], start=(t == 0), stop=(t == CPB - 1))
            ins.then_inc(s_kvs, 1)
            pe.wait_ge(s_kvc, 2)
            pe.wait_ge(s_qc, 4)
            for i in range(4):
                b, m = i // 2, i % 2
                if i >= 2:
                    pe.wait_ge(s_oc, i - 1)
                q = qT[:, m, b * NTOK:(b + 1) * NTOK]
                pe.matmul(bank[4 + i % 2][0:DH, 0:NTOK], kv[:, i, :], q, start=True, stop=True)
                pe.matmul(bank[6 + i % 2][0:DH, 0:NTOK], ks[:, i, :], q, start=True, stop=True).then_inc(s_o, 1)
            pe.wait_ge(s_oc, 4)
            for c in range(NC):
                if c >= 2:
                    pe.wait_ge(s_x2, c - 1)
                for m in range(2):
                    r = DH + m
                    ins = pe.matmul(bank[c % 2][0:TC, 0:D], oT[0:r, m, c * TC:(c + 1) * TC], proj_w[0:r, m, :],
                                    start=(m == 0), stop=(m == 1))
                ins.then_inc(s_pr, 1)
            turn_normed(NC)
            pe.wait_ge(s_xT, 8)
            for i in range(12):
                f, b = i // 2, i % 2
                if i >= 4:
                    pe.wait_ge(s_f1c, i - 3)
                for k in range(2):
                    ins = pe.matmul(bank[4 + i % 4][:, 0:NTOK], fc1_w[:, k, f * 128:(f + 1) * 128],
                                    xT[0:DH, k, b * NTOK:(b + 1) * NTOK], start=(k == 0), stop=(k == 1))
                ins.then_inc(s_f1, 1)
            pe.wait_ge(s_f1c, 12)
            for c in range(NC):
                if c >= 2:
                    pe.wait_ge(s_h3, c - 1)
                for f in range(6):
                    ins = pe.matmul(bank[c % 2][0:TC, 0:D], h1T[:, f, c * TC:(c + 1) * TC], fc2_w[:, f, :],
                                    start=(f == 0), stop=(f == 5))
                ins.then_inc(s_f2, 1)
            turn_normed(2 * NC)
            pe.wait_ge(s_xT, 12)
            for c in range(NC):
                for k in range(2):
                    ins = pe.matmul(bank[4][0:TC, c * E:(c + 1) * E], xT[0:DH, k, c * TC:(c + 1) * TC], gateT[:, k, :],
                                    start=(k == 0), stop=(k == 1))
            ins.then_inc(s_lg, 1)
            pe.wait_ge(s_sel, 1)
            flat = sel[:, :, :].rearrange("p c e -> p (c e)")
            pe.matmul(bank[5][0:TC, 0:NC * E], ones[0:TC, 0:TC], flat, start=True, stop=True)
            pe.matmul(bank[5][0:TC, NC * E:2 * NC * E], earlier[:, :], flat, start=True, stop=True).then_inc(s_rk, 1)

            pe.wait_ge(s_sched, 1)

            def gather_block(b1):
                pe.wait_ge(s_hot_b, b1 + 1)
                pe.nop(nofuse=True)
                for k in range(2):
                    for c in range(NC):
                        ins = pe.matmul(bank[4][0:DH, k * SLOTS:(k + 1) * SLOTS], norm[:, c, k * DH:(k + 1) * DH],
                                        onehot[:, c, :], start=(c == 0), stop=(c == NC - 1))
                ins.then_inc(s_gb, 1)

            def w1_block(b1, s):
                pe.wait_ge(s_bx, b1)
                pe.nop(nofuse=True)
                for c in range(4):
                    for k in range(2):
                        ins = pe.matmul(bank[c // 2][:, (c % 2) * SLOTS:(c % 2 + 1) * SLOTS],
                                        ew1[s][:, k, c * 128:(c + 1) * 128], bxT[:, k, :], start=(k == 0), stop=(k == 1))
                    if c % 2:
                        ins.then_inc(s_w1[c // 2], 1)

            def w2_block(b1, s):
                pe.wait_ge(s_h1, b1 * 4)
                pe.nop(nofuse=True)
                for c in range(4):
                    for k in range(4):
                        ins = pe.matmul(bank[2 + c // 2][:, (c % 2) * SLOTS:(c % 2 + 1) * SLOTS],
                                        ew2[s][:, k, c * 128:(c + 1) * 128], bh1[:, k, :], start=(k == 0), stop=(k == 3))
                    if c % 2:
                        ins.then_inc(s_w2[c // 2], 1)

            def w3_block(b1, s):
                pe.wait_ge(s_h2, b1 * 4)
                pe.nop(nofuse=True)
                for k in range(4):
                    ins = pe.matmul(bank[5][0:BOT, 0:SLOTS], ew3[s][:, k, :], bh2[:, k, :], start=(k == 0), stop=(k == 3))
                ins.then_inc(s_w3, 1)

            def wl_block(b1, s):
                pe.wait_ge(s_z, b1)
                pe.nop(nofuse=True)
                return pe.matmul(bank[6][0:SLOTS, 0:D], bz[:, :], ewl[s][:, :], start=True, stop=True)

            def step(b1, s, s_next):
                w2_block(b1, s)
                w1_block(b1 + 1, s_next)
                w3_block(b1, s)
                gather_block(b1 + 2)
                wl_block(b1, s).then_inc(s_wl, 1)

            def same_expert(n, first, s):
                with pe.If(n > 1):
                    with pe.Fori(1, n) as j:
                        b1 = pe.snap(first + j)
                        step(b1, s, s)

            def expert(e, s, loads_next):
                n, first = trips(pe, e)
                same_expert(n, first, s)
                b1 = pe.snap(first + n)
                pe.wait_ge(s_ew[(s + 1) % WBUF], loads_next)
                pe.nop(nofuse=True)
                step(b1, s, (s + 1) % WBUF)
                pe.nop(nofuse=True).then_inc(s_ed, 1)

            gather_block(1)
            pe.wait_ge(s_ew[0], 80)
            w1_block(1, 0)
            gather_block(2)
            with pe.Fori(0, E // WBUF - 1) as i:
                for s in range(WBUF):
                    expert(pe.snap(i * WBUF + s), s, i * 80 + (80 if s + 1 < WBUF else 160))
            for s in range(WBUF - 1):
                expert(E - WBUF + s, s, 80 * (E // WBUF))
            n, first = trips(pe, E - 1)
            same_expert(n, first, WBUF - 1)
            b1 = pe.snap(first + n)
            w2_block(b1, WBUF - 1)
            w3_block(b1, WBUF - 1)
            wl_block(b1, WBUF - 1).then_inc(s_wl, 1)


_INS = (["x", "txt"] + [f"L0_tok_{n}" for n in ("W0", "b0", "W1", "b1", "W2", "b2", "Wf", "bf", "idx0", "idx1", "idx2")]
        + [f"L0_attn_{n}" for n in ("qkv_w", "qkv_b", "proj_w", "proj_b", "fc1_w", "fc1_b", "fc2_w", "fc2_b",
                                    "ln1_w", "ln1_b", "ln2_w", "ln2_b")]
        + [f"L0_ffn_{n}" for n in ("gate_w", "W1", "b1", "W2", "b2", "W3", "b3", "Wl", "bl")])


def kernel(**inputs):
    import numpy as _np
    import concourse.bacc as _bacc
    from concourse import mybir as _mybir
    from concourse.bass_utils import run_bass_kernel_spmd as _run

    nc = _bacc.Bacc("TRN2", target_bir_lowering=False, num_devices=1)
    arrays, args = {}, {}
    for name in _INS:
        a = _np.ascontiguousarray(inputs[name])
        arrays[f"in_{name}_dram"] = a
        args[name] = nc.dram_tensor(f"in_{name}_dram", a.shape, _mybir.dt.from_np(a.dtype), kind="ExternalInput").ap()
    out = nc.dram_tensor("out_0_dram", (NBATCH, NTOK, D), F32, kind="ExternalOutput").ap()
    fusion_kernel(nc, args, out)
    r = _run(nc, [arrays], core_ids=[0])
    return r.results[0]["out_0_dram"]
```

```python
from contextlib import ExitStack

import concourse.bass as bass
from concourse import mybir

ALU = mybir.AluOpType
ACT = mybir.ActivationFunctionType
AX_X = mybir.AxisListType.X
F32 = mybir.dt.float32
BF16 = mybir.dt.bfloat16
I32 = mybir.dt.int32
U32 = mybir.dt.uint32

NBATCH, CH, IMG = 2, 3, 64
TXT = 32
EMB = 64
D = 192
NIMG = IMG * IMG // 16
NTOK = NIMG + TXT
HEAD = 16
HID = 768
E = 32
EHID, BOT = 512, 64
LEVELS = ((1, 5, 6), (2, 3, 24), (4, 1, 96))

TC = 96
NC = NBATCH * NTOK // TC
CPB = NTOK // TC
NT = NBATCH * NTOK
DH = D // 2
SLOTS = 128
MAXB = 2 * NT // SLOTS + E
SHARED = 11520
WBUF = 4
NUMBER, ACTIVE, SPENT, EXPERT, SLOT = range(5)
NQ = 42
GROUPS = [(4 * g, min(4, NQ - 4 * g)) for g in range(11)]
PAIRS = [(2 * i, 0 if i < 16 else 1 if i < 20 else 2) for i in range(21)]


def dram_views(a):
    x = a["x"]
    v = {}
    v["x0"] = x.rearrange("b c y (h w) -> (y h) (b c) w", h=2)
    v["x1"] = x.rearrange("b c (p i) (h w) -> h p (b c) i w", i=2, h=4)
    v["x2"] = x.rearrange("b c (p i) (h w) -> h p (b c) i w", i=4, h=8)
    v["i0"] = a["L0_tok_idx0"].rearrange("(t p g) -> p t g", t=2, p=128)
    v["i1"] = a["L0_tok_idx1"].rearrange("(p k) -> p k", k=8)
    v["i2"] = a["L0_tok_idx2"].rearrange("(p k) -> p k", k=2)
    return v


def column(ap):
    return ap.rearrange("(n o) -> n o", o=1)


def row(ap):
    return ap.rearrange("(o n) -> o n", o=1)


def fusion_kernel(nc, a, out):
    rows = nc.dram_tensor("expert_rows", [(MAXB + 3) * SLOTS, D], F32, kind="Internal").ap()
    dv = dram_views(a)
    out_chunks = out.rearrange("b (c p) d -> (b c) p d", p=TC)

    with ExitStack() as ctx:
        def sb(name, shape, dt=F32):
            return ctx.enter_context(nc.sbuf_tensor(name, shape, dt))

        def sem(name):
            return ctx.enter_context(nc.semaphore(name))

        shared = sb("shared", [128, SHARED])

        def carver(start=0):
            at = [start]

            def carve(name, shape):
                n = 1
                for k in shape[1:]:
                    n *= k
                at[0] += n
                assert at[0] <= SHARED, name
                v = shared[0:shape[0], at[0] - n:at[0]]
                if len(shape) == 3:
                    return v.rearrange("p (a b) -> p a b", b=shape[2])
                return v.rearrange("p (a b c) -> p a b c", b=shape[2], c=shape[3]) if len(shape) == 4 else v
            return carve

        early, late, attn = carver(), carver(), carver(3 * NC * D)
        routing = carver(3 * NC * D + 6 * NT)

        bank = [ctx.enter_context(nc.psum_tensor(f"bank{i}", [128, 512], F32)) for i in range(8)]

        ident = sb("ident", [128, 128]); ident_bf = sb("ident_bf", [128, 128], BF16)
        iota_slot = sb("iota_slot", [128, E])
        iota_lo = iota_slot[:, 0:32]
        neg_part = sb("neg_part", [128, 1])
        ones = sb("ones", [128, 128]); earlier = sb("earlier", [TC, TC]); heads = sb("heads", [DH, DH])
        minus_half = sb("minus_half", [128, NC])
        hat1 = early("hat1", [128, NBATCH, NIMG]); hat2 = sb("hat2", [32, NBATCH, NIMG])
        hat_t = early("hat_t", [128, NBATCH, NIMG])
        off1 = sb("off1", [128, NBATCH]); off2 = sb("off2", [32, NBATCH])
        x0 = early("x0", [128, 6, 32]); x1 = early("x1", [128, 6, 2, 16]); x2 = early("x2", [128, 6, 4, 8])
        x1r = early("x1r", [128, 24, 8]); x2r = early("x2r", [128, 96, 2])
        idx = sb("idx", [128, NQ], I32); hi_i = sb("hi_i", [128, NQ], I32); lo_i = sb("lo_i", [128, NQ], I32)
        hi_bf = sb("hi_bf", [128, NQ], BF16); lo_f = sb("lo_f", [128, NQ])
        lo_mask = [early("lo_mask0", [128, 32, 32]), early("lo_mask1", [128, 8, 8]), early("lo_mask2", [128, 2, 2])]
        hot_t = early("hot_t", [128, 2, 512]); hot = early("hot", [128, 2, 512])
        picked = early("picked", [128, 2, 384])
        feat = [early("feat0", [128, 2, 32 * 3]), early("feat1", [128, 2, 8 * 12]), early("feat2", [128, 2, 2 * 48])]
        w0 = early("w0", [EMB, 48]); w1 = early("w1", [EMB, 192]); w2 = early("w2", [EMB, 768])
        wf = early("wf", [DH, 2, D]); gate = early("gate", [E, D])
        eb3 = early("eb3", [E, BOT])
        w2T = early("w2T", [96, 8, EMB]); w0T = sb("w0T", [48, EMB]); w1T = sb("w1T", [96, 2, EMB])
        wfT = sb("wfT", [EMB, 3, D]); gateT = sb("gateT", [DH, 2, E])
        b3T = sb("b3T", [BOT, E + 2])
        tb = sb("tb", [EMB, 3]); bf_bc = sb("bf_bc", [TC, D])
        f0T = early("f0T", [48, 512]); f12T = early("f12T", [96, 4, 128])
        y0T = early("y0T", [EMB, 512]); y1T = sb("y1T", [EMB, 128]); y2T = sb("y2T", [EMB, 32])
        g1 = sb("g1", [128, D]); g2 = sb("g2", [32, D])
        h3 = late("h3", [TC, NC, D]); x2t = late("x2t", [TC, NC, D]); xT = late("xT", [DH + 1, 2, NT])
        h1T = late("h1T", [128, 6, NT])
        h = sb("h", [TC, NC, D]); an = sb("an", [TC, NC, D]); norm = sb("norm", [TC, NC, D])
        stats = sb("stats", [TC, NC, 6]); mv = sb("mv", [TC, NC, 2])
        var_e = sb("var_e", [TC, NC]); r1 = sb("r1", [TC, NC]); r2 = sb("r2", [TC, NC]); r12 = sb("r12", [TC, NC])
        rt = sb("rt", [TC, NC])
        qT = attn("qT", [DH, 2, NT]); oT = attn("oT", [DH + 1, 2, NT])
        qe = attn("qe", [DH, 2, NTOK]); ke = attn("ke", [TC, 2, D])
        kt = attn("kt", [TC, NC, D]); vt = attn("vt", [TC, NC, 2, DH + 1])
        kv = attn("kv", [DH, 4, DH]); ks = attn("ks", [DH, 4, DH]); ksum = sb("ksum", [DH, 4])
        den = attn("den", [DH, 2, NTOK])
        qkv_w = sb("qkv_w", [DH + 1, 2, 3 * D]); proj_w = sb("proj_w", [DH + 1, 2, D])
        fc1_w = sb("fc1_w", [DH, 2, HID]); fc2_w = sb("fc2_w", [128, 6, D])
        fc1_b = sb("fc1_b", [128, 6]); fc2_bc = sb("fc2_bc", [TC, D])
        lnw = sb("lnw", [DH, 4, 2])
        sc = routing("sc", [TC, NC, E]); sm = sb("sm", [TC, NC]); top = sb("top", [TC, NC, 8])
        topi = sb("topi", [TC, NC, 8], U32); topf = sb("topf", [TC, NC, 2]); tw = sb("tw", [TC, NC, 2])
        tws = sb("tws", [TC, NC]); oneh = routing("oneh", [TC, 2, NC, E]); sel = routing("sel", [TC, NC, E])
        cnt = routing("cnt", [TC, NC, E]); pre = routing("pre", [TC, NC + 1, E]); rank = routing("rank", [TC, NC, E])
        place = routing("place", [TC, NC, E]); placed = routing("placed", [TC, NC, E])
        dest_f = sb("dest_f", [TC, NC, 2]); dest = sb("dest", [TC, NC, 2], I32)
        blk_i = sb("blk_i", [TC, E], I32); blk = sb("blk", [TC, 2, E])
        cum = sb("cum", [TC, 2, 2, E]); before = sb("before", [TC, 2, E]); due = sb("due", [TC, E])
        part = sb("part", [128, 1]); facts = sb("facts", [TC, 4, E]); fact = sb("fact", [TC, 4])
        table = sb("table", [1, 5, TC], I32); total = sb("total", [1, 2], I32); total_f = sb("total_f", [1, 2])
        ew1 = sb("ew1", [DH + 1, WBUF, 2, EHID]); ew2 = sb("ew2", [128, WBUF, 4, EHID]); ew3 = sb("ew3", [128, WBUF, 4 * BOT])
        ewl = sb("ewl", [BOT + 1, WBUF, D]); eb2 = sb("eb2", [128, WBUF, EHID])
        zero = sb("zero", [SLOTS, D])
        bx = sb("bx", [SLOTS, D]); bxT = sb("bxT", [DH + 1, 2, SLOTS]); bh1 = sb("bh1", [SLOTS, EHID]); bh1T = sb("bh1T", [128, 4, SLOTS])
        bpre = sb("bpre", [SLOTS, EHID]); bh2 = sb("bh2", [SLOTS, EHID]); bh2T = sb("bh2T", [128, 4, SLOTS])
        bw3 = sb("bw3", [128, 4 * BOT]); bzT = sb("bzT", [BOT + 1, SLOTS]); by = sb("by", [SLOTS, D])
        base = an
        picked_y = h1T[0:TC, :, 0:2 * D].rearrange("p c (k d) -> p c k d", k=2)

        s_x = sem("x_loaded"); s_x12 = sem("x12_loaded"); s_idx = sem("idx_loaded")
        s_tw = sem("token_weights_loaded"); s_aw = sem("attn_weights_loaded"); s_txt = sem("text_loaded")
        s_id = sem("identity_built"); s_cst = sem("constants_built"); s_off = sem("hat_offsets_built")
        s_wT = sem("weights_turned"); s_wTc = sem("turned_weights_copied")
        s_hi = sem("hi_ready"); s_bc = sem("hi_spread"); s_hot = sem("hi_onehot_ready"); s_gat = sem("pair_gathered")
        s_pick = sem("pair_picked"); s_xr = sem("x_reordered"); s_hatp = sem("hat_position"); s_hat = sem("hats_built")
        s_fT = sem("features_turned"); s_fTc = sem("features_copied"); s_y = sem("levels_done"); s_yc = sem("levels_copied")
        s_g = sem("level_fused"); s_gc = sem("level_fused_copied"); s_h = sem("h_summed"); s_hc = sem("h_ready")
        s_st = sem("stats_ready"); s_r = sem("rstd_ready"); s_n = sem("normed"); s_nT = sem("normed_turned")
        s_xT = sem("xT_ready"); s_q = sem("q_done"); s_qe = sem("q_exp"); s_qc = sem("q_ready")
        s_kv = sem("kv_done"); s_ke = sem("k_exp"); s_vc = sem("v_ready"); s_kc = sem("k_ready")
        s_kvs = sem("kv_summed"); s_kvc = sem("kv_ready"); s_o = sem("attn_out"); s_oc = sem("attn_out_ready")
        s_pr = sem("proj_done"); s_x2 = sem("x2_ready"); s_base = sem("base_ready")
        s_f1 = sem("fc1_done"); s_f1c = sem("fc1_ready"); s_f2 = sem("fc2_done"); s_h3 = sem("h3_ready")
        s_lg = sem("logits_done"); s_mx = sem("logits_shifted"); s_ex = sem("exp_done"); s_sel = sem("selected")
        s_rk = sem("ranks_done"); s_sched = sem("schedule_ready"); s_bzo = sem("ones_row_set")
        s_dest = sem("row_numbers_ready"); s_fact = sem("facts_ready"); s_tab = sem("tables_spread")
        s_sc = sem("tokens_scattered"); s_xl = sem("block_loaded"); s_xt = sem("block_turned"); s_xc = sem("block_x_ready")
        s_kl = sem("expert_loaded"); s_w1 = sem("block_w1_done"); s_h1 = [sem(f"block_h1_half_{g}") for g in range(2)]
        s_t1 = sem("block_h1_turned"); s_h1T = [sem(f"block_h1T_half_{g}") for g in range(2)]
        s_w2 = sem("block_w2_done"); s_pre = [sem(f"block_w2_b2_half_{g}") for g in range(2)]
        s_h2 = [sem(f"block_h2_half_{g}") for g in range(2)]; s_t2 = sem("block_h2_turned")
        s_h2T = [sem(f"block_h2T_half_{g}") for g in range(2)]; s_w3c = sem("block_w3_weights_ready"); s_w3 = sem("block_w3_done")
        s_z = sem("block_z_ready"); s_wl = sem("block_wl_done"); s_by = sem("block_y_ready"); s_ys = sem("block_y_stored")
        s_zd = sem("zeros_stored"); s_yfree = sem("block_y_free")
        s_ew = [sem(f"expert_weights_{s}") for s in range(WBUF)]
        s_pk = sem("rows_picked"); s_o1 = sem("weighted"); s_fin = sem("out_ready"); s_zero = sem("zeros_ready"); s_out = sem("out_stored")
        s_dc = sem("vector_chain"); s_pc = sem("pool_chain"); s_ac = sem("scalar_chain"); s_ones = sem("ones_rows")

        block = ctx.enter_context(nc.Block())

        def lookup(eng, t, at, lo, hi):
            return eng.value_load(table[0:1, t, bass.ds(at, 1)], min_val=lo, max_val=hi)

        def blocks(eng):
            return eng.value_load(total[0:1, 0:1], min_val=2, max_val=MAXB)

        def chained(eng, s):
            count = [0]

            def link(ins):
                count[0] += 1
                ins.then_inc(s, 1)
                eng.wait_ge(s, count[0])
            return link

        def load_expert(sp, k, s):
            e = lookup(sp, ACTIVE, k, 0, E - 1)

            def at(name):
                return a[name][bass.ds(e, 1)]
            sp.dma_start(ew1[0:DH, s, :, :], at("L0_ffn_W1").rearrange("o (k p) h -> p (o k) h", p=DH)).then_inc(s_ew[s], 16)
            sp.dma_start(ew1[DH:DH + 1, s, 1, :], at("L0_ffn_b1")).then_inc(s_ew[s], 16)
            sp.dma_start(ew2[:, s, :, :], at("L0_ffn_W2").rearrange("o (k p) h -> p (o k) h", p=128)).then_inc(s_ew[s], 16)
            sp.dma_start(eb2[:, s, :], at("L0_ffn_b2").to_broadcast([128, EHID])).then_inc(s_ew[s], 16)
            sp.dma_start(ew3[:, s, :].rearrange("p (k h) -> p k h", k=4),
                         at("L0_ffn_W3").rearrange("o (k p) h -> p (o k) h", p=128)).then_inc(s_ew[s], 16)
            sp.dma_start(ewl[0:BOT, s, :], at("L0_ffn_Wl").rearrange("o p h -> (o p) h")).then_inc(s_ew[s], 16)
            sp.dma_start(ewl[BOT:BOT + 1, s, :], at("L0_ffn_bl")).then_inc(s_ew[s], 16)

        @block.sync
        def _(sp):
            sp.dma_start(idx[:, 0:32].rearrange("p (t g) -> p t g", t=2), dv["i0"]).then_inc(s_idx, 16)
            sp.dma_start(idx[:, 32:40], dv["i1"]).then_inc(s_idx, 16)
            sp.dma_start(idx[:, 40:42], dv["i2"]).then_inc(s_idx, 16)
            sp.dma_start(x0[:, :, :], dv["x0"]).then_inc(s_x, 16)
            for i in range(4):
                for bc in range(6):
                    sp.dma_start(x1[i:128:4, bc, :, :], dv["x1"][i, :, bc]).then_inc(s_x12, 16)
            for i in range(8):
                for bc in range(6):
                    sp.dma_start(x2[i:128:8, bc, :, :], dv["x2"][i, :, bc]).then_inc(s_x12, 16)
            sp.wait_ge(s_zero, 1)
            sp.dma_start(rows.rearrange("(k p) d -> p k d", p=SLOTS),
                         zero[:, :].unsqueeze(1).to_broadcast([SLOTS, MAXB + 3, D])).then_inc(s_zd, 16)
            sp.wait_ge(s_sched, 1)
            rounds = sp.value_load(total[0:1, 1:2], min_val=1, max_val=E // WBUF)

            def tell_loaded(s, loads):
                sp.wait_ge(s_ew[s], loads)
                sp.nop(nofuse=True).then_inc(s_kl, 1)

            with sp.Fori(0, rounds) as i:
                for j in range(WBUF):
                    k = sp.snap(i * WBUF + j)
                    sp.wait_ge(s_wl, lookup(sp, SPENT, k, 1, MAXB + 1))
                    sp.nop(nofuse=True)
                    load_expert(sp, k, (j + 1) % WBUF)
                    if j:
                        tell_loaded(j, i * 112 + 112)
                tell_loaded(0, i * 112 + 112)
            for c in range(NC):
                sp.wait_ge(s_fin, c + 1)
                sp.dma_start(out_chunks[c], an[:, c, :]).then_inc(s_out, 16)
            sp.wait_ge(s_out, 16 * NC)

        @block.gpsimd
        def _(pool):
            link = chained(pool, s_pc)
            link(pool.memset(ident[:, :], 0.0))
            link(pool.affine_select(out=ident[:, :], in_=ident[:, :], compare_op=ALU.not_equal, fill=1.0, base=0,
                                    pattern=[[-1, 128]], channel_multiplier=1))
            pool.tensor_copy(ident_bf[:, :], ident[:, :]).then_inc(s_id, 1)
            pool.iota(neg_part[:, :], [[0, 1]], base=0, channel_multiplier=-1,
                      allow_small_or_imprecise_dtypes=True).then_inc(s_id, 1)
            pool.iota(iota_slot[:, :], [[1, E]], base=0, channel_multiplier=0,
                      allow_small_or_imprecise_dtypes=True).then_inc(s_id, 1)
            pool.iota(hat_t[:, :, :], [[0, NBATCH], [1, NIMG]], base=0, channel_multiplier=0,
                      allow_small_or_imprecise_dtypes=True).then_inc(s_off, 1)
            pool.iota(off1[:, :], [[64, NBATCH]], base=0, channel_multiplier=-1,
                      allow_small_or_imprecise_dtypes=True).then_inc(s_off, 1)
            pool.iota(off2[:, :], [[16, NBATCH]], base=0, channel_multiplier=-1,
                      allow_small_or_imprecise_dtypes=True).then_inc(s_off, 1)
            pool.memset(ones[:, :], 1.0).then_inc(s_cst, 1)
            pool.memset(minus_half[:, :], -0.5).then_inc(s_cst, 1)
            link(pool.memset(earlier[:, :], 1.0))
            pool.affine_select(out=earlier[:, :], in_=earlier[:, :], compare_op=ALU.is_gt, fill=0.0, base=0,
                               pattern=[[1, TC]], channel_multiplier=-1).then_inc(s_cst, 1)
            link(pool.memset(heads[:, :], 1.0))
            hv = heads[:, :].rearrange("p (h d) -> p h d", d=HEAD)
            link(pool.affine_select(out=hv, in_=hv, compare_op=ALU.is_ge, fill=0.0, base=0,
                                    pattern=[[-HEAD, DH // HEAD], [0, HEAD]], channel_multiplier=1))
            pool.affine_select(out=hv, in_=hv, compare_op=ALU.is_ge, fill=0.0, base=HEAD - 1,
                               pattern=[[HEAD, DH // HEAD], [0, HEAD]], channel_multiplier=-1).then_inc(s_cst, 1)

            for i, name in enumerate(("L0_tok_W0", "L0_tok_W1", "L0_tok_W2")):
                pool.dma_start((w0, w1, w2)[i][:, :], a[name]).then_inc(s_tw, 16)
            pool.dma_start(wf[:, :, :], a["L0_tok_Wf"].rearrange("(k p) d -> p k d", p=DH)).then_inc(s_tw, 16)
            pool.dma_start(gate[:, :], a["L0_ffn_gate_w"]).then_inc(s_tw, 16)
            pool.dma_start(eb3[:, :], a["L0_ffn_b3"]).then_inc(s_tw, 16)
            for i in range(3):
                pool.dma_start(tb[:, i:i + 1], column(a[f"L0_tok_b{i}"])).then_inc(s_tw, 16)
            pool.dma_start(bf_bc[:, :], row(a["L0_tok_bf"]).to_broadcast([TC, D])).then_inc(s_tw, 16)
            for b in range(NBATCH):
                pool.dma_start(h[TC - TXT:TC, CPB * b + CPB - 1, :], a["txt"][b]).then_inc(s_txt, 16)
            pool.dma_start(qkv_w[0:DH, :, :], a["L0_attn_qkv_w"].rearrange("(k p) n -> p k n", p=DH)).then_inc(s_aw, 16)
            pool.dma_start(qkv_w[DH:DH + 1, 1, :], row(a["L0_attn_qkv_b"])).then_inc(s_aw, 16)
            pool.dma_start(proj_w[0:DH, :, :], a["L0_attn_proj_w"].rearrange("(k p) n -> p k n", p=DH)).then_inc(s_aw, 16)
            pool.dma_start(proj_w[DH:DH + 1, 1, :], row(a["L0_attn_proj_b"])).then_inc(s_aw, 16)
            for i, name in enumerate(("ln1_w", "ln1_b", "ln2_w", "ln2_b")):
                for k in range(2):
                    pool.dma_start(lnw[:, i, k:k + 1], column(a[f"L0_attn_{name}"][k * DH:(k + 1) * DH])).then_inc(s_aw, 16)
            pool.dma_start(fc1_w[:, :, :], a["L0_attn_fc1_w"].rearrange("(k p) n -> p k n", p=DH)).then_inc(s_aw, 16)
            pool.dma_start(fc2_w[:, :, :], a["L0_attn_fc2_w"].rearrange("(k p) n -> p k n", p=128)).then_inc(s_aw, 16)
            for k in range(6):
                pool.dma_start(fc1_b[:, k:k + 1], column(a["L0_attn_fc1_b"][k * 128:(k + 1) * 128])).then_inc(s_aw, 16)
            pool.dma_start(fc2_bc[:, :], row(a["L0_attn_fc2_b"]).to_broadcast([TC, D])).then_inc(s_aw, 16)

            pool.wait_ge(s_st, 1)
            link(pool.tensor_scalar(var_e[:, :], mv[:, :, 1], 1e-5, None, ALU.add))
            link(pool.tensor_tensor(r1[:, :], var_e[:, :], minus_half[0:TC, :], ALU.pow))
            link(pool.tensor_tensor(rt[:, :], r1[:, :], r1[:, :], ALU.mult))
            link(pool.tensor_tensor(rt[:, :], rt[:, :], mv[:, :, 1], ALU.mult))
            link(pool.tensor_scalar(rt[:, :], rt[:, :], 1e-8, None, ALU.add))
            link(pool.tensor_tensor(r2[:, :], rt[:, :], minus_half[0:TC, :], ALU.pow))
            pool.tensor_tensor(r12[:, :], r1[:, :], r2[:, :], ALU.mult).then_inc(s_r, 1)
            pool.wait_ge(s_r, 1)
            for t in (oT, xT):
                link(pool.memset(t[DH:DH + 1, 1, :], 1.0))
            link(pool.memset(bzT[BOT:BOT + 1, :], 1.0))
            link(pool.memset(bxT[DH:DH + 1, 1, :], 1.0))
            pool.memset(vt[:, :, :, DH:DH + 1], 1.0).then_inc(s_ones, 1)
            pool.wait_ge(s_st, 2)
            link(pool.tensor_scalar(var_e[:, :], mv[:, :, 1], 1e-8, None, ALU.add))
            pool.tensor_tensor(r1[:, :], var_e[:, :], minus_half[0:TC, :], ALU.pow).then_inc(s_r, 1)
            pool.wait_ge(s_aw, 16 * 21)
            for c in range(NC):
                link(pool.tensor_tensor(base[:, c, :], h[:, c, :], x2t[:, c, :], ALU.add))
                pool.tensor_tensor(base[:, c, :], base[:, c, :], fc2_bc[:, :], ALU.add).then_inc(s_base, 1)
            pool.wait_ge(s_st, 3)
            link(pool.tensor_scalar(var_e[:, :], mv[:, :, 1], 1e-5, None, ALU.add))
            pool.tensor_tensor(r1[:, :], var_e[:, :], minus_half[0:TC, :], ALU.pow).then_inc(s_r, 1)

            pool.wait_ge(s_dest, 1)
            pool.wait_ge(s_zd, 16)
            for c in range(NC):
                for k in range(2):
                    pool.indirect_dma_start(out=rows[:, :], out_offset=bass.IndirectOffsetOnAxis(ap=dest[:, c, k:k + 1], axis=0),
                                            in_=norm[:, c, :], in_offset=None).then_inc(s_sc, 16)
            pool.wait_ge(s_sc, 16 * 2 * NC)

            def load_block(b1):
                pool.dma_start(bx[:, :], rows[bass.ds(b1 * SLOTS, SLOTS), :]).then_inc(s_xl, 16)

            def store_block(b1):
                pool.wait_ge(s_by, b1 + 1)
                pool.nop(nofuse=True)
                pool.dma_start(rows[bass.ds(b1 * SLOTS, SLOTS), :], by[:, :]).then_inc(s_ys, 16)
                pool.wait_ge(s_ys, b1 * 16)
                pool.nop(nofuse=True).then_inc(s_yfree, 1)

            pool.nop(nofuse=True).then_inc(s_yfree, 1)
            nb = blocks(pool)
            load_block(1)
            for b1 in (1, 2):
                pool.wait_ge(s_xt, b1)
                load_block(b1 + 1)
            with pool.Fori(1, nb) as b1:
                pool.wait_ge(s_xt, b1 + 2)
                pool.nop(nofuse=True)
                load_block(b1 + 3)
                store_block(b1)
            store_block(nb)

            for c in range(NC):
                for k in range(2):
                    pool.indirect_dma_start(out=picked_y[:, c, k, :], out_offset=None, in_=rows[:, :],
                                            in_offset=bass.IndirectOffsetOnAxis(ap=dest[:, c, k:k + 1], axis=0)
                                            ).then_inc(s_pk, 16)

        @block.vector
        def _(dve):
            link = chained(dve, s_dc)
            dve.memset(zero[:, :], 0.0).then_inc(s_zero, 1)
            dve.wait_ge(s_idx, 48)
            for (at, n), bits in zip(((0, 32), (32, 8), (40, 2)), (5, 3, 1)):
                dve.tensor_scalar(hi_i[:, at:at + n], idx[:, at:at + n], bits, None, ALU.logical_shift_right)
                last = dve.tensor_scalar(lo_i[:, at:at + n], idx[:, at:at + n], (1 << bits) - 1, None, ALU.bitwise_and)
            link(last)
            dve.tensor_copy(hi_bf[:, :], hi_i[:, :]).then_inc(s_hi, 1)
            link(dve.tensor_copy(lo_f[:, :], lo_i[:, :]))
            dve.wait_ge(s_id, 3)
            for l, (at, n) in enumerate(((0, 32), (32, 8), (40, 2))):
                w = 1 << LEVELS[l][1]
                last = dve.tensor_tensor(lo_mask[l][:, :, :], iota_lo[:, 0:w].unsqueeze(1).to_broadcast([128, n, w]),
                                         lo_f[:, at:at + n].unsqueeze(2).to_broadcast([128, n, w]), ALU.is_equal)
            link(last)
            dve.tensor_scalar(part[:, :], neg_part[:, :], -1.0, None, ALU.mult)
            dve.wait_ge(s_off, 3)
            for l, (t, n) in enumerate(((hat1, 64), (hat2, 16))):
                p = t.shape[0]
                link(dve.tensor_scalar(t[:, :, :], hat_t[0:p, :, :], n / NIMG, 0.5 * n / NIMG - 0.5, ALU.mult, ALU.add))
                dve.tensor_scalar(t[:, :, :], t[:, :, :], 0.0, float(n - 1), ALU.max, ALU.min).then_inc(s_hatp, 1)
            for i, (q, l) in enumerate(PAIRS):
                f, w = LEVELS[l][2], 1 << LEVELS[l][1]
                q0 = q - (0, 32, 40)[l]
                dve.wait_ge(s_gat, i + 1)
                tmp = picked[:, i % 2, :].rearrange("p (k f w) -> p k f w", k=2, w=w)
                link(dve.tensor_tensor(tmp, bank[6 + i % 2][:, 0:384].rearrange("p (k f w) -> p k f w", k=2, w=w),
                                       lo_mask[l][:, q0:q0 + 2, :].unsqueeze(2).to_broadcast([128, 2, f, w]), ALU.mult))
                dst = feat[l][:, :, :].rearrange("p b (k f) -> p k b f", f=f // 2)[:, q0:q0 + 2]
                src = picked[:, i % 2, :].rearrange("p (k b f w) -> p k b f w", k=2, b=2, w=w)
                dve.tensor_reduce(dst, src, AX_X, ALU.add).then_inc(s_pick, 1)
            dve.wait_ge(s_fT, 2)
            dve.tensor_copy(f12T[:, :, :], bank[1][0:96, :].rearrange("p (a q) -> p a q", a=4)).then_inc(s_fTc, 1)
            dve.wait_ge(s_y, 2)
            dve.wait_ge(s_tw, 16 * 10)
            dve.tensor_scalar(y1T[:, :], bank[3][0:EMB, 0:128], tb[:, 1:2], None, ALU.add).then_inc(s_yc, 1)
            dve.tensor_scalar(y2T[:, :], bank[3][0:EMB, 128:160], tb[:, 2:3], None, ALU.add).then_inc(s_yc, 1)
            dve.wait_ge(s_txt, 32)
            for c in range(NC):
                m = TC if c % CPB < CPB - 1 else TC - TXT
                dve.wait_ge(s_h, c + 1)
                link(dve.tensor_tensor(h[0:m, c, :], bank[6 + c % 2][0:m, 0:D], bf_bc[0:m, :], ALU.add))
                s_hc_ins = dve.bn_stats(stats[:, c, :], h[:, c, :])
                link(s_hc_ins)
                ins = dve.bn_aggr(mv[:, c, :], stats[:, c, :])
                ins.then_inc(s_hc, 1)
            dve.wait_ge(s_hc, NC)
            dve.nop(nofuse=True).then_inc(s_st, 1)

            def normalise(dst, src, scale, c):
                return dve.tensor_scalar(dst[:, c, :], src[:, c, :], mv[:, c, 0:1], scale[:, c:c + 1],
                                         ALU.subtract, ALU.mult)

            def turned(first, k_lnw):
                for k in range(2):
                    for b in range(NBATCH):
                        i = 2 * k + b
                        dve.wait_ge(s_nT, first + i + 1)
                        dst = xT[0:DH, k, b * NTOK:(b + 1) * NTOK]
                        if k_lnw is None:
                            ins = dve.tensor_copy(dst, bank[i][0:DH, 0:NTOK])
                        else:
                            ins = dve.tensor_scalar(dst, bank[i][0:DH, 0:NTOK], lnw[:, k_lnw, k:k + 1],
                                                    lnw[:, k_lnw + 1, k:k + 1], ALU.mult, ALU.add)
                        ins.then_inc(s_xT, 1)

            dve.wait_ge(s_r, 1)
            for c in range(NC):
                normalise(norm, h, r12, c).then_inc(s_n, 1)
            for c in range(NC):
                last = normalise(an, h, r1, c)
            link(last)
            dve.wait_ge(s_aw, 16 * 21)
            turned(0, 0)
            for i in range(4):
                m, b = i // 2, i % 2
                dve.wait_ge(s_qe, i + 1)
                link(dve.tensor_scalar(qe[:, i % 2, :], qe[:, i % 2, :], 1.0, None, ALU.min))
                dve.scalar_tensor_tensor(out=qT[:, m, b * NTOK:(b + 1) * NTOK], in0=bank[4 + i][0:DH, 0:NTOK], scalar=0.0,
                                         in1=qe[:, i % 2, :], op0=ALU.max, op1=ALU.add).then_inc(s_qc, 1)
            for c in range(NC):
                dve.wait_ge(s_ke, c + 1)
                link(dve.tensor_scalar(ke[:, c % 2, :], ke[:, c % 2, :], 1.0, None, ALU.min))
                dve.scalar_tensor_tensor(out=kt[:, c, :], in0=bank[c % 2][0:TC, 0:D], scalar=0.0,
                                         in1=ke[:, c % 2, :], op0=ALU.max, op1=ALU.add).then_inc(s_kc, 1)
            dve.wait_ge(s_cst, 4)
            dve.wait_ge(s_kvs, 1)
            kvp = bank[2][0:DH, 0:4 * (DH + 1)].rearrange("p (g n) -> p g n", g=4)
            dve.tensor_tensor(kv[:, :, :], kvp[:, :, 0:DH], heads[:, :].unsqueeze(1).to_broadcast([DH, 4, DH]), ALU.mult).then_inc(s_kvc, 1)
            link(dve.tensor_copy(ksum[:, :], kvp[:, :, DH]))
            dve.tensor_tensor(ks[:, :, :], heads[:, :].unsqueeze(1).to_broadcast([DH, 4, DH]),
                              ksum[:, :].unsqueeze(2).to_broadcast([DH, 4, DH]), ALU.mult).then_inc(s_kvc, 1)
            for i in range(4):
                b, m = i // 2, i % 2
                dve.wait_ge(s_o, i + 1)
                link(dve.reciprocal(den[:, i % 2, :], bank[6 + i % 2][0:DH, 0:NTOK]))
                dve.tensor_tensor(oT[0:DH, m, b * NTOK:(b + 1) * NTOK], bank[4 + i % 2][0:DH, 0:NTOK], den[:, i % 2, :],
                                  ALU.mult).then_inc(s_oc, 1)
            for c in range(NC):
                dve.wait_ge(s_pr, c + 1)
                ins = dve.tensor_tensor(x2t[:, c, :], bank[c % 2][0:TC, 0:D], an[:, c, :], ALU.add)
                ins.then_inc(s_x2, 1)
                dve.wait_ge(s_x2, c + 1)
                link(dve.bn_stats(stats[:, c, :], x2t[:, c, :]))
                link(dve.bn_aggr(mv[:, c, :], stats[:, c, :]))
            dve.nop(nofuse=True).then_inc(s_st, 1)
            dve.wait_ge(s_r, 2)
            for c in range(NC):
                normalise(norm, x2t, r1, c).then_inc(s_n, 1)
            turned(4, 2)
            for c in range(NC):
                dve.wait_ge(s_base, c + 1)
                dve.wait_ge(s_f2, c + 1)
                ins = dve.tensor_tensor(h3[:, c, :], bank[c % 2][0:TC, 0:D], base[:, c, :], ALU.add)
                ins.then_inc(s_h3, 1)
                dve.wait_ge(s_h3, c + 1)
                link(dve.bn_stats(stats[:, c, :], h3[:, c, :]))
                link(dve.bn_aggr(mv[:, c, :], stats[:, c, :]))
            dve.nop(nofuse=True).then_inc(s_st, 1)
            dve.wait_ge(s_r, 3)
            for c in range(NC):
                normalise(norm, h3, r1, c).then_inc(s_n, 1)
            turned(8, None)

            dve.wait_ge(s_lg, 1)
            lg = bank[4][0:TC, 0:NC * E].rearrange("p (c e) -> p c e", c=NC)
            link(dve.tensor_reduce(sm[:, :], lg, AX_X, ALU.max))
            dve.tensor_tensor(sc[:, :, :], lg, sm[:, :].unsqueeze(2).to_broadcast([TC, NC, E]), ALU.subtract).then_inc(s_mx, 1)
            dve.wait_ge(s_ex, 1)
            link(dve.tensor_reduce(sm[:, :], sc[:, :, :], AX_X, ALU.add))
            link(dve.reciprocal(sm[:, :], sm[:, :]))
            link(dve.tensor_tensor(sc[:, :, :], sc[:, :, :], sm[:, :].unsqueeze(2).to_broadcast([TC, NC, E]), ALU.mult))
            for c in range(NC):
                last = dve.max(top[:, c, :], sc[:, c, :])
            link(last)
            for c in range(NC):
                last = dve.max_index(topi[:, c, :], top[:, c, :], sc[:, c, :])
            link(last)
            link(dve.tensor_copy(topf[:, :, :], topi[:, :, 0:2]))
            for k in range(2):
                last = dve.tensor_tensor(oneh[:, k, :, :], iota_slot[0:TC, 0:E].unsqueeze(1).to_broadcast([TC, NC, E]),
                                         topf[:, :, k:k + 1].to_broadcast([TC, NC, E]), ALU.is_equal)
            link(last)
            ins = dve.tensor_tensor(sel[:, :, :], oneh[:, 0, :, :], oneh[:, 1, :, :], ALU.add)
            ins.then_inc(s_sel, 1)
            link(dve.tensor_tensor(tws[:, :], top[:, :, 0], top[:, :, 1], ALU.add))
            link(dve.tensor_scalar(tws[:, :], tws[:, :], 1e-20, None, ALU.add))
            link(dve.reciprocal(tws[:, :], tws[:, :]))
            link(dve.tensor_tensor(tw[:, :, :], top[:, :, 0:2], tws[:, :].unsqueeze(2).to_broadcast([TC, NC, 2]), ALU.mult))
            dve.wait_ge(s_rk, 1)
            link(dve.tensor_copy(cnt[:, :, :], bank[5][0:TC, 0:NC * E].rearrange("p (c e) -> p c e", c=NC)))
            link(dve.memset(pre[:, 0, :], 0.0))
            for c in range(NC):
                link(dve.tensor_tensor(pre[:, c + 1, :], pre[:, c, :], cnt[:, c, :], ALU.add))
            link(dve.tensor_tensor(rank[:, :, :], bank[5][0:TC, NC * E:2 * NC * E].rearrange("p (c e) -> p c e", c=NC),
                                   pre[:, 0:NC, :], ALU.add))
            link(dve.tensor_scalar(due[:, :], pre[:, NC, :], float(SLOTS - 1), None, ALU.add))
            link(dve.tensor_copy(blk_i[:, :], due[:, :]))
            link(dve.tensor_scalar(blk_i[:, :], blk_i[:, :], SLOTS.bit_length() - 1, None, ALU.logical_shift_right))
            dve.tensor_scalar(blk[:, 1, :], pre[:, NC, :], 0.0, None, ALU.is_gt)
            link(dve.tensor_copy(blk[:, 0, :], blk_i[:, :]))
            link(dve.tensor_copy(cum[:, 0, :, :], blk[:, :, :]))
            at, step = 0, 1
            while step < E:
                dve.tensor_copy(cum[:, 1 - at, :, 0:step], cum[:, at, :, 0:step])
                link(dve.tensor_tensor(cum[:, 1 - at, :, step:E], cum[:, at, :, step:E], cum[:, at, :, 0:E - step], ALU.add))
                at, step = 1 - at, 2 * step
            upto = cum[:, at, :, :]
            link(dve.tensor_tensor(before[:, :, :], upto, blk[:, :, :], ALU.subtract))
            link(dve.tensor_scalar(due[:, :], before[:, 1, :], float(WBUF), None, ALU.add))
            for t, (limit, count) in enumerate(((before[:, 0, :], blk[:, 1, :]), (upto[:, 1, :], ones[0:TC, 0:E]),
                                                (due[:, :], blk[:, 0, :]), (before[:, 0, :], ones[0:TC, 0:E]))):
                last = dve.scalar_tensor_tensor(out=facts[:, t, :], in0=limit, scalar=part[0:TC, 0:1], in1=count,
                                                op0=ALU.is_le, op1=ALU.mult)
            link(last)
            link(dve.tensor_reduce(fact[:, :], facts[:, :, :], AX_X, ALU.add))
            dve.tensor_scalar(fact[:, ACTIVE:ACTIVE + 1], fact[:, ACTIVE:ACTIVE + 1], float(E - 1), None, ALU.min)
            link(dve.tensor_scalar(fact[:, SPENT:SPENT + 1], fact[:, SPENT:SPENT + 1], 1.0, None, ALU.add))
            dve.nop(nofuse=True).then_inc(s_fact, 1)
            link(dve.tensor_copy(total_f[0:1, :], upto[0:1, :, E - 1]))
            link(dve.tensor_copy(total[0:1, :], total_f[0:1, :]))
            link(dve.tensor_scalar(total_f[0:1, 1:2], total_f[0:1, 1:2], float(WBUF - 1), None, ALU.add))
            link(dve.tensor_copy(total[0:1, 1:2], total_f[0:1, 1:2]))
            link(dve.tensor_scalar(total[0:1, 1:2], total[0:1, 1:2], WBUF.bit_length() - 1, None, ALU.logical_shift_right))
            dve.wait_ge(s_tab, 1)
            link(dve.tensor_copy(table[0:1, 0:4, :], bank[6][0:1, 0:4 * TC].rearrange("p (t n) -> p t n", t=4)))
            link(dve.tensor_scalar(table[0:1, SLOT, :], table[0:1, NUMBER, :], WBUF - 1, None, ALU.bitwise_and))
            dve.nop(nofuse=True).then_inc(s_sched, 1)
            link(dve.tensor_scalar(before[:, 0, :], before[:, 0, :], 1.0, float(SLOTS), ALU.add, ALU.mult))
            link(dve.tensor_tensor(place[:, :, :], rank[:, :, :], before[:, 0, :].unsqueeze(1).to_broadcast([TC, NC, E]), ALU.add))
            for k in range(2):
                link(dve.tensor_tensor(placed[:, :, :], place[:, :, :], oneh[:, k, :, :], ALU.mult))
                link(dve.tensor_reduce(dest_f[:, :, k], placed[:, :, :], AX_X, ALU.add))
            link(dve.tensor_copy(dest[:, :, :], dest_f[:, :, :]))
            dve.nop(nofuse=True).then_inc(s_dest, 1)

            def copy_turned(dst, src, done):
                for g in range(2):
                    dve.tensor_copy(dst[:, 2 * g:2 * g + 2, :],
                                    src[:, g * 2 * SLOTS:(g + 1) * 2 * SLOTS].rearrange("p (k s) -> p k s", k=2)).then_inc(done[g], 1)

            def copy_h1(b1):
                dve.wait_ge(s_t1, b1)
                dve.nop(nofuse=True)
                copy_turned(bh1T, bank[2], s_h1T)

            def second_layers(b1, at):
                dve.wait_ge(s_w2, b1)
                slot = lookup(dve, SLOT, at, 0, WBUF - 1)
                dve.nop(nofuse=True)
                for g in range(2):
                    f = slice(g * EHID // 2, (g + 1) * EHID // 2)
                    dve.tensor_tensor(bpre[:, f], bank[1][:, f], eb2[:, bass.ds(slot, 1), f].rearrange("p o f -> p (o f)"),
                                      ALU.add).then_inc(s_pre[g], 1)
                dve.wait_ge(s_t2, b1)
                dve.nop(nofuse=True)
                copy_turned(bh2T, bank[3], s_h2T)
                e1 = lookup(dve, EXPERT, at, 1, E)
                dve.wait_ge(s_w3, b1)
                dve.nop(nofuse=True)
                dve.tensor_scalar(bzT[0:BOT, :], bank[5][0:BOT, 0:SLOTS], b3T[:, bass.ds(e1, 1)], None, ALU.add).then_inc(s_z, 1)

            nb = blocks(dve)
            copy_h1(1)
            with dve.Fori(0, nb - 1) as b:
                b1 = dve.snap(b + 1)
                second_layers(b1, b)
                copy_h1(b1 + 1)
            second_layers(nb, nb - 1)

            dve.wait_ge(s_pk, 16 * 2 * NC)
            for c in range(NC):
                link(dve.scalar_tensor_tensor(out=norm[:, c, :], in0=picked_y[:, c, 0, :], scalar=tw[:, c, 0:1],
                                              in1=h3[:, c, :], op0=ALU.mult, op1=ALU.add))
                dve.scalar_tensor_tensor(out=an[:, c, :], in0=picked_y[:, c, 1, :], scalar=tw[:, c, 1:2],
                                         in1=norm[:, c, :], op0=ALU.mult, op1=ALU.add).then_inc(s_fin, 1)

        @block.scalar
        def _(act):
            link = chained(act, s_ac)
            act.wait_ge(s_x12, 16 * 72)
            for b in range(NBATCH):
                for iy in range(2):
                    o = b * 12 + iy * 6
                    act.copy(x1r[:, o:o + 6, :].rearrange("p (x c) l -> p c x l", c=3),
                             x1[:, 3 * b:3 * b + 3, iy, :].rearrange("p c (l x) -> p c x l", x=2)).then_inc(s_xr, 1)
                for iy in range(4):
                    o = b * 48 + iy * 12
                    act.copy(x2r[:, o:o + 12, :].rearrange("p (x c) l -> p c x l", c=3),
                             x2[:, 3 * b:3 * b + 3, iy, :].rearrange("p c (l x) -> p c x l", x=4)).then_inc(s_xr, 1)
            act.wait_ge(s_id, 3)
            for g, (q, n) in enumerate(GROUPS):
                act.wait_ge(s_bc, g + 1)
                if g >= 2:
                    act.wait_ge(s_gat, 2 * (g - 1))
                link(act.activation(hot_t[:, g % 2, 0:n * 128], bank[4 + g % 2][:, 0:n * 128], ACT.Abs, bias=neg_part[:, 0:1]))
                act.activation(hot[:, g % 2, 0:n * 128], hot_t[:, g % 2, 0:n * 128], ACT.Relu, scale=-1.0, bias=1.0).then_inc(s_hot, 1)
            act.wait_ge(s_hatp, 2)
            for t, o in ((hat1, off1), (hat2, off2)):
                for b in range(NBATCH):
                    link(act.activation(t[:, b, :], t[:, b, :], ACT.Abs, bias=o[:, b:b + 1]))
            for t in (hat1, hat2):
                act.activation(t[:, :, :], t[:, :, :], ACT.Relu, scale=-1.0, bias=1.0).then_inc(s_hat, 1)
            act.wait_ge(s_wT, 1)
            act.copy(w2T[:, :, :], bank[0][0:96, :].rearrange("p (g e) -> p g e", g=8)).then_inc(s_wTc, 1)
            act.wait_ge(s_wT, 2)
            act.copy(w0T[:, :], bank[1][0:48, 0:64]).then_inc(s_wTc, 1)
            act.copy(w1T[:, :, :], bank[1][0:96, 64:192].rearrange("p (g e) -> p g e", g=2)).then_inc(s_wTc, 1)
            act.copy(wfT[:, 2, :], bank[1][0:EMB, 192:384]).then_inc(s_wTc, 1)
            act.wait_ge(s_wT, 3)
            act.copy(wfT[:, 0:2, :], bank[2][0:EMB, 0:384].rearrange("p (l d) -> p l d", l=2)).then_inc(s_wTc, 1)
            act.wait_ge(s_wT, 4)
            act.copy(gateT[:, :, :], bank[3][0:DH, 0:64].rearrange("p (k e) -> p k e", k=2)).then_inc(s_wTc, 1)
            act.copy(b3T[:, 1:E + 1], bank[3][0:BOT, 320:352]).then_inc(s_wTc, 1)
            act.wait_ge(s_fT, 1)
            act.copy(f0T[:, :], bank[0][0:48, :]).then_inc(s_fTc, 1)
            act.wait_ge(s_y, 1)
            act.wait_ge(s_tw, 16 * 10)
            act.activation(y0T[:, :], bank[2][0:EMB, :], ACT.Identity, bias=tb[:, 0:1]).then_inc(s_yc, 1)
            act.wait_ge(s_g, 1)
            act.copy(g1[:, :], bank[4][:, 0:D]).then_inc(s_gc, 1)
            act.wait_ge(s_g, 2)
            act.copy(g2[:, :], bank[5][0:32, 0:D]).then_inc(s_gc, 1)
            for i in range(4):
                act.wait_ge(s_q, i + 1)
                if i >= 2:
                    act.wait_ge(s_qc, i - 1)
                act.activation(qe[:, i % 2, :], bank[4 + i][0:DH, 0:NTOK], ACT.Exp).then_inc(s_qe, 1)
            for c in range(NC):
                act.wait_ge(s_kv, c + 1)
                if c >= 2:
                    act.wait_ge(s_kc, c - 1)
                act.activation(ke[:, c % 2, :], bank[c % 2][0:TC, 0:D], ACT.Exp).then_inc(s_vc, 1)
                act.copy(vt[:, c, :, 0:DH], bank[c % 2][0:TC, D:2 * D].rearrange("p (m e) -> p m e", m=2)).then_inc(s_ke, 1)
            for i in range(12):
                f, b = i // 2, i % 2
                act.wait_ge(s_f1, i + 1)
                act.activation(h1T[:, f, b * NTOK:(b + 1) * NTOK], bank[4 + i % 4][:, 0:NTOK], ACT.Gelu,
                               bias=fc1_b[:, f:f + 1]).then_inc(s_f1c, 1)
            act.wait_ge(s_mx, 1)
            act.activation(sc[:, :, :], sc[:, :, :], ACT.Exp).then_inc(s_ex, 1)

            act.wait_ge(s_sched, 1)

            def copy_x(b1):
                act.wait_ge(s_xt, b1)
                act.nop(nofuse=True)
                act.copy(bxT[0:DH, :, :], bank[4][0:DH, 0:2 * SLOTS].rearrange("p (k s) -> p k s", k=2)).then_inc(s_xc, 1)

            def gelu_1(b1):
                act.wait_ge(s_w1, b1)
                act.nop(nofuse=True)
                for g in range(2):
                    f = slice(g * EHID // 2, (g + 1) * EHID // 2)
                    act.activation(bh1[:, f], bank[0][:, f], ACT.Gelu).then_inc(s_h1[g], 1)

            def gelu_2(b1):
                for g in range(2):
                    f = slice(g * EHID // 2, (g + 1) * EHID // 2)
                    act.wait_ge(s_pre[g], b1)
                    act.nop(nofuse=True)
                    act.activation(bh2[:, f], bpre[:, f], ACT.Gelu).then_inc(s_h2[g], 1)

            def fetch_w3(at):
                slot = lookup(act, SLOT, at, 0, WBUF - 1)
                act.copy(bw3[:, :], ew3[:, bass.ds(slot, 1), :].rearrange("p o f -> p (o f)")).then_inc(s_w3c, 1)

            def copy_y(b1):
                act.wait_ge(s_wl, b1 + 1)
                act.nop(nofuse=True)
                act.wait_ge(s_yfree, b1)
                act.nop(nofuse=True)
                act.copy(by[:, :], bank[6][0:SLOTS, 0:D]).then_inc(s_by, 1)

            act.nop(nofuse=True).then_inc(s_by, 1)
            nb = blocks(act)
            copy_x(1)
            gelu_1(1)
            fetch_w3(0)
            copy_x(2)
            with act.Fori(1, nb) as b1:
                gelu_2(b1)
                gelu_1(b1 + 1)
                copy_x(b1 + 2)
                copy_y(b1)
                fetch_w3(b1)
            gelu_2(nb)
            copy_y(nb)

        @block.tensor
        def _(pe):
            pe.wait_ge(s_hi, 1)
            pe.wait_ge(s_id, 3)

            def spread(g):
                q, n = GROUPS[g]
                if g >= 2:
                    pe.wait_ge(s_hot, g - 1)
                for k in range(n):
                    ins = pe.matmul(bank[4 + g % 2][:, k * 128:(k + 1) * 128], hi_bf[:, q + k:q + k + 1].to_broadcast([128, 128]),
                                    ident_bf[:, :], start=True, stop=True)
                ins.then_inc(s_bc, 1)

            def gather(g):
                q, n = GROUPS[g]
                pe.wait_ge(s_hot, g + 1)
                if g == 0:
                    pe.wait_ge(s_x, 16)
                if g == 8:
                    pe.wait_ge(s_xr, 12)
                for k in range(0, n, 2):
                    i = (q + k) // 2
                    l = PAIRS[i][1]
                    rows = (x0, x1r, x2r)[l][:, :, :].rearrange("p f w -> p (f w)")
                    if i >= 2:
                        pe.wait_ge(s_pick, i - 1)
                    for kk in range(2):
                        ins = pe.matmul(bank[6 + i % 2][:, kk * D:(kk + 1) * D],
                                        hot[:, g % 2, (k + kk) * 128:(k + kk + 1) * 128], rows, start=True, stop=True)
                    ins.then_inc(s_gat, 1)

            def turn_weights():
                pe.wait_ge(s_tw, 16 * 10)
                for g in range(8):
                    ins = pe.transpose(bank[0][0:96, g * 64:(g + 1) * 64], w2[:, g * 96:(g + 1) * 96], ident[0:EMB, 0:EMB])
                ins.then_inc(s_wT, 1)
                pe.transpose(bank[1][0:48, 0:64], w0[:, :], ident[0:EMB, 0:EMB])
                for g in range(2):
                    pe.transpose(bank[1][0:96, 64 + g * 64:128 + g * 64], w1[:, g * 96:(g + 1) * 96], ident[0:EMB, 0:EMB])
                for k in range(2):
                    ins = pe.transpose(bank[1][0:EMB, 192 + k * 96:288 + k * 96], wf[:, k, 128:192], ident[0:DH, 0:DH])
                ins.then_inc(s_wT, 1)
                for l in range(2):
                    for k in range(2):
                        ins = pe.transpose(bank[2][0:EMB, l * D + k * 96:l * D + (k + 1) * 96], wf[:, k, l * 64:(l + 1) * 64],
                                           ident[0:DH, 0:DH])
                ins.then_inc(s_wT, 1)
                for k in range(2):
                    pe.transpose(bank[3][0:DH, k * 32:(k + 1) * 32], gate[:, k * DH:(k + 1) * DH], ident[0:E, 0:E])
                pe.transpose(bank[3][0:BOT, 320:352], eb3[:, :], ident[0:E, 0:E]).then_inc(s_wT, 1)

            spread(0)
            for g in range(len(GROUPS)):
                if g + 1 < len(GROUPS):
                    spread(g + 1)
                gather(g)
            turn_weights()
            pe.wait_ge(s_wTc, 7)
            pe.wait_ge(s_pick, 16)
            for b in range(NBATCH):
                for t in range(2):
                    ins = pe.transpose(bank[0][0:48, (b * 2 + t) * 128:(b * 2 + t + 1) * 128],
                                       feat[0][:, b, t * 48:(t + 1) * 48], ident[:, :])
            ins.then_inc(s_fT, 1)
            pe.wait_ge(s_pick, 21)
            for b in range(NBATCH):
                pe.transpose(bank[1][0:96, b * 128:(b + 1) * 128], feat[1][:, b, :], ident[:, :])
            for b in range(NBATCH):
                ins = pe.transpose(bank[1][0:96, 256 + b * 128:256 + (b + 1) * 128], feat[2][:, b, :], ident[:, :])
            ins.then_inc(s_fT, 1)
            pe.wait_ge(s_fTc, 2)
            pe.matmul(bank[2][0:EMB, :], w0T[:, :], f0T[:, :], start=True, stop=True).then_inc(s_y, 1)
            t1 = f12T[:, 0:2, :].rearrange("p b (t g) -> p b t g", g=2)
            t2 = f12T[:, 2:4, :].rearrange("p b (t g) -> p b t g", g=8)
            for g in range(2):
                pe.matmul(bank[3][0:EMB, 0:128], w1T[:, g, :], t1[:, :, :, g], start=(g == 0), stop=(g == 1))
            for g in range(8):
                ins = pe.matmul(bank[3][0:EMB, 128:160], w2T[:, g, :], t2[:, :, :, g], start=(g == 0), stop=(g == 7))
            ins.then_inc(s_y, 1)
            pe.wait_ge(s_yc, 3)
            pe.matmul(bank[4][:, 0:D], y1T[:, :], wfT[:, 1, :], start=True, stop=True).then_inc(s_g, 1)
            pe.matmul(bank[5][0:32, 0:D], y2T[:, :], wfT[:, 2, :], start=True, stop=True).then_inc(s_g, 1)
            pe.wait_ge(s_gc, 2)
            pe.wait_ge(s_hat, 2)
            for c in range(NC):
                b, t = c // CPB, c % CPB
                m = TC if t < CPB - 1 else TC - TXT
                if c >= 2:
                    pe.wait_ge(s_hc, c - 1)
                o = bank[6 + c % 2][0:m, 0:D]
                pe.matmul(o, y0T[:, b * NIMG + t * TC:b * NIMG + t * TC + m], wfT[:, 0, :], start=True, stop=False)
                pe.matmul(o, hat1[:, b, t * TC:t * TC + m], g1[:, :], start=False, stop=False)
                pe.matmul(o, hat2[:, b, t * TC:t * TC + m], g2[:, :], start=False, stop=True).then_inc(s_h, 1)

            def turn_normed(first):
                pe.wait_ge(s_n, first + NC)
                for k in range(2):
                    for b in range(NBATCH):
                        for t in range(CPB):
                            ins = pe.transpose(bank[2 * k + b][0:DH, t * TC:(t + 1) * TC],
                                               norm[:, b * CPB + t, k * DH:(k + 1) * DH], ident[0:TC, 0:TC])
                        ins.then_inc(s_nT, 1)

            turn_normed(0)
            pe.wait_ge(s_xT, 4)
            pe.wait_ge(s_aw, 16 * 21)
            pe.wait_ge(s_ones, 1)
            for i in range(4):
                m, b = i // 2, i % 2
                for k in range(2):
                    r = DH + k
                    ins = pe.matmul(bank[4 + i][0:DH, 0:NTOK], qkv_w[0:r, k, m * DH:(m + 1) * DH],
                                    xT[0:r, k, b * NTOK:(b + 1) * NTOK], start=(k == 0), stop=(k == 1))
                ins.then_inc(s_q, 1)
            for c in range(NC):
                if c >= 2:
                    pe.wait_ge(s_kc, c - 1)
                for k in range(2):
                    r = DH + k
                    ins = pe.matmul(bank[c % 2][0:TC, 0:2 * D], xT[0:r, k, c * TC:(c + 1) * TC], qkv_w[0:r, k, D:3 * D],
                                    start=(k == 0), stop=(k == 1))
                ins.then_inc(s_kv, 1)
            pe.wait_ge(s_cst, 4)
            pe.wait_ge(s_kc, NC)
            for b in range(NBATCH):
                for m in range(2):
                    for t in range(CPB):
                        c = b * CPB + t
                        ins = pe.matmul(bank[2][0:DH, (2 * b + m) * (DH + 1):(2 * b + m + 1) * (DH + 1)],
                                        kt[:, c, m * DH:(m + 1) * DH], vt[:, c, m, :], start=(t == 0), stop=(t == CPB - 1))
            ins.then_inc(s_kvs, 1)
            pe.wait_ge(s_kvc, 2)
            pe.wait_ge(s_qc, 4)
            for i in range(4):
                b, m = i // 2, i % 2
                if i >= 2:
                    pe.wait_ge(s_oc, i - 1)
                q = qT[:, m, b * NTOK:(b + 1) * NTOK]
                pe.matmul(bank[4 + i % 2][0:DH, 0:NTOK], kv[:, i, :], q, start=True, stop=True)
                pe.matmul(bank[6 + i % 2][0:DH, 0:NTOK], ks[:, i, :], q, start=True, stop=True).then_inc(s_o, 1)
            pe.wait_ge(s_oc, 4)
            for c in range(NC):
                if c >= 2:
                    pe.wait_ge(s_x2, c - 1)
                for m in range(2):
                    r = DH + m
                    ins = pe.matmul(bank[c % 2][0:TC, 0:D], oT[0:r, m, c * TC:(c + 1) * TC], proj_w[0:r, m, :],
                                    start=(m == 0), stop=(m == 1))
                ins.then_inc(s_pr, 1)
            turn_normed(NC)
            pe.wait_ge(s_xT, 8)
            for i in range(12):
                f, b = i // 2, i % 2
                if i >= 4:
                    pe.wait_ge(s_f1c, i - 3)
                for k in range(2):
                    ins = pe.matmul(bank[4 + i % 4][:, 0:NTOK], fc1_w[:, k, f * 128:(f + 1) * 128],
                                    xT[0:DH, k, b * NTOK:(b + 1) * NTOK], start=(k == 0), stop=(k == 1))
                ins.then_inc(s_f1, 1)
            pe.wait_ge(s_f1c, 12)
            for c in range(NC):
                if c >= 2:
                    pe.wait_ge(s_h3, c - 1)
                for f in range(6):
                    ins = pe.matmul(bank[c % 2][0:TC, 0:D], h1T[:, f, c * TC:(c + 1) * TC], fc2_w[:, f, :],
                                    start=(f == 0), stop=(f == 5))
                ins.then_inc(s_f2, 1)
            turn_normed(2 * NC)
            pe.wait_ge(s_xT, 12)
            for c in range(NC):
                for k in range(2):
                    ins = pe.matmul(bank[4][0:TC, c * E:(c + 1) * E], xT[0:DH, k, c * TC:(c + 1) * TC], gateT[:, k, :],
                                    start=(k == 0), stop=(k == 1))
            ins.then_inc(s_lg, 1)
            pe.wait_ge(s_sel, 1)
            flat = sel[:, :, :].rearrange("p c e -> p (c e)")
            pe.matmul(bank[5][0:TC, 0:NC * E], ones[0:TC, 0:TC], flat, start=True, stop=True)
            pe.matmul(bank[5][0:TC, NC * E:2 * NC * E], earlier[:, :], flat, start=True, stop=True).then_inc(s_rk, 1)

            pe.wait_ge(s_fact, 1)
            for t in range(4):
                ins = pe.matmul(bank[6][0:1, t * TC:(t + 1) * TC], fact[:, t:t + 1], ident[0:TC, 0:TC], start=True, stop=True)
            ins.then_inc(s_tab, 1)

            pe.wait_ge(s_sched, 1)

            def turn_block(b1):
                pe.wait_ge(s_xl, b1 * 16)
                pe.nop(nofuse=True)
                for k in range(2):
                    ins = pe.transpose(bank[4][0:DH, k * SLOTS:(k + 1) * SLOTS], bx[:, k * DH:(k + 1) * DH], ident[:, :])
                ins.then_inc(s_xt, 1)

            def w1_block(b1, at):
                pe.wait_ge(s_xc, b1)
                pe.nop(nofuse=True)
                slot = lookup(pe, SLOT, at, 0, WBUF - 1)
                pe.wait_ge(s_kl, lookup(pe, NUMBER, at, 1, E))
                pe.nop(nofuse=True)
                for k in range(2):
                    r = DH + k
                    ins = pe.matmul(bank[0][:, :], bxT[0:r, k, :], ew1[0:r, bass.ds(slot, 1), k, :].rearrange("p o f -> p (o f)"),
                                    start=(k == 0), stop=(k == 1))
                ins.then_inc(s_w1, 1)

            def turn_hidden(b1, hidden, ready, to, done):
                for k in range(4):
                    if k % 2 == 0:
                        pe.wait_ge(ready[k // 2], b1)
                        pe.nop(nofuse=True)
                    ins = pe.transpose(to[:, k * SLOTS:(k + 1) * SLOTS], hidden[:, k * 128:(k + 1) * 128], ident[:, :])
                ins.then_inc(done, 1)

            def w2_block(b1, at):
                slot = lookup(pe, SLOT, at, 0, WBUF - 1)
                for k in range(4):
                    if k % 2 == 0:
                        pe.wait_ge(s_h1T[k // 2], b1)
                        pe.nop(nofuse=True)
                    ins = pe.matmul(bank[1][:, :], bh1T[:, k, :], ew2[:, bass.ds(slot, 1), k, :].rearrange("p o f -> p (o f)"),
                                    start=(k == 0), stop=(k == 3))
                ins.then_inc(s_w2, 1)
                return slot

            def w3_block(b1):
                pe.wait_ge(s_w3c, b1)
                pe.nop(nofuse=True)
                for k in range(4):
                    if k % 2 == 0:
                        pe.wait_ge(s_h2T[k // 2], b1)
                        pe.nop(nofuse=True)
                    ins = pe.matmul(bank[5][0:BOT, 0:SLOTS], bw3[:, k * BOT:(k + 1) * BOT], bh2T[:, k, :], start=(k == 0), stop=(k == 3))
                ins.then_inc(s_w3, 1)

            def wl_block(b1, slot):
                pe.wait_ge(s_z, b1)
                pe.nop(nofuse=True)
                pe.wait_ge(s_by, b1)
                pe.nop(nofuse=True)
                pe.matmul(bank[6][:, 0:D], bzT[:, :], ewl[:, bass.ds(slot, 1), :].rearrange("p o f -> p (o f)"),
                          start=True, stop=True).then_inc(s_wl, 1)

            pe.nop(nofuse=True).then_inc(s_wl, 1)
            nb = blocks(pe)
            turn_block(1)
            w1_block(1, 0)
            turn_block(2)
            turn_hidden(1, bh1, s_h1, bank[2], s_t1)
            with pe.Fori(1, nb) as b1:
                slot = w2_block(b1, b1 - 1)
                w1_block(b1 + 1, b1)
                turn_hidden(b1, bh2, s_h2, bank[3], s_t2)
                turn_block(b1 + 2)
                w3_block(b1)
                turn_hidden(b1 + 1, bh1, s_h1, bank[2], s_t1)
                wl_block(b1, slot)
            slot = w2_block(nb, nb - 1)
            turn_hidden(nb, bh2, s_h2, bank[3], s_t2)
            w3_block(nb)
            wl_block(nb, slot)


_INS = (["x", "txt"] + [f"L0_tok_{n}" for n in ("W0", "b0", "W1", "b1", "W2", "b2", "Wf", "bf", "idx0", "idx1", "idx2")]
        + [f"L0_attn_{n}" for n in ("qkv_w", "qkv_b", "proj_w", "proj_b", "fc1_w", "fc1_b", "fc2_w", "fc2_b",
                                    "ln1_w", "ln1_b", "ln2_w", "ln2_b")]
        + [f"L0_ffn_{n}" for n in ("gate_w", "W1", "b1", "W2", "b2", "W3", "b3", "Wl", "bl")])


def kernel(**inputs):
    import numpy as _np
    import concourse.bacc as _bacc
    from concourse import mybir as _mybir
    from concourse.bass_utils import run_bass_kernel_spmd as _run

    nc = _bacc.Bacc("TRN2", target_bir_lowering=False, num_devices=1)
    arrays, args = {}, {}
    for name in _INS:
        a = _np.ascontiguousarray(inputs[name])
        arrays[f"in_{name}_dram"] = a
        args[name] = nc.dram_tensor(f"in_{name}_dram", a.shape, _mybir.dt.from_np(a.dtype), kind="ExternalInput").ap()
    out = nc.dram_tensor("out_0_dram", (NBATCH, NTOK, D), F32, kind="ExternalOutput").ap()
    fusion_kernel(nc, args, out)
    r = _run(nc, [arrays], core_ids=[0])
    return r.results[0]["out_0_dram"]
```

```python
from contextlib import ExitStack

import concourse.bass as bass
from concourse import mybir

ALU = mybir.AluOpType
ACT = mybir.ActivationFunctionType
AX_X = mybir.AxisListType.X
F32 = mybir.dt.float32
BF16 = mybir.dt.bfloat16
I32 = mybir.dt.int32
U32 = mybir.dt.uint32

NBATCH, CH, IMG = 2, 3, 64
TXT = 32
EMB = 64
D = 192
NIMG = IMG * IMG // 16
NTOK = NIMG + TXT
HEAD = 16
HID = 768
E = 32
EHID, BOT = 512, 64
LEVELS = ((1, 5, 6), (2, 3, 24), (4, 1, 96))

TC = 96
NC = NBATCH * NTOK // TC
CPB = NTOK // TC
NT = NBATCH * NTOK
DH = D // 2
HPH = D // 2 // 16
SLOTS = 128
MAXB = 2 * NT // SLOTS + E
SHARED = 11520
WBUF = 4
NUMBER, ACTIVE, SPENT, EXPERT, SLOT = range(5)
X2_SP = 4
NQ = 42
GROUPS = [(4 * g, min(4, NQ - 4 * g)) for g in range(11)]
PAIRS = [(2 * i, 0 if i < 16 else 1 if i < 20 else 2) for i in range(21)]


def dram_views(a):
    x = a["x"]
    v = {}
    v["x0"] = x.rearrange("b c y (h w) -> (y h) (b c) w", h=2)
    v["x1"] = x.rearrange("b c (p i) (h w) -> h p (b c) i w", i=2, h=4)
    v["x2"] = x.rearrange("b c (p i) (h w) -> h p (b c) i w", i=4, h=8)
    v["i0"] = a["L0_tok_idx0"].rearrange("(t p g) -> p t g", t=2, p=128)
    v["i1"] = a["L0_tok_idx1"].rearrange("(p k) -> p k", k=8)
    v["i2"] = a["L0_tok_idx2"].rearrange("(p k) -> p k", k=2)
    return v


def column(ap):
    return ap.rearrange("(n o) -> n o", o=1)


def row(ap):
    return ap.rearrange("(o n) -> o n", o=1)


def fusion_kernel(nc, a, out):
    rows = nc.dram_tensor("expert_rows", [(MAXB + 3) * SLOTS, D], F32, kind="Internal").ap()
    dv = dram_views(a)
    out_chunks = out.rearrange("b (c p) d -> (b c) p d", p=TC)

    with ExitStack() as ctx:
        def sb(name, shape, dt=F32):
            return ctx.enter_context(nc.sbuf_tensor(name, shape, dt))

        def sem(name):
            return ctx.enter_context(nc.semaphore(name))

        shared = sb("shared", [128, SHARED])

        def carver(start=0):
            at = [start]

            def carve(name, shape):
                n = 1
                for k in shape[1:]:
                    n *= k
                at[0] += n
                assert at[0] <= SHARED, name
                v = shared[0:shape[0], at[0] - n:at[0]]
                if len(shape) == 3:
                    return v.rearrange("p (a b) -> p a b", b=shape[2])
                return v.rearrange("p (a b c) -> p a b c", b=shape[2], c=shape[3]) if len(shape) == 4 else v
            return carve

        early, late, attn = carver(), carver(), carver(3 * NC * D)
        routing = carver(3 * NC * D + 6 * NT)

        bank = [ctx.enter_context(nc.psum_tensor(f"bank{i}", [128, 512], F32)) for i in range(8)]

        ident = sb("ident", [128, 128]); ident_bf = sb("ident_bf", [128, 128], BF16)
        iota_row = sb("iota_row", [128, E])
        neg_part = sb("neg_part", [128, 1])
        ones = sb("ones", [128, 128]); earlier = sb("earlier", [TC, TC]); heads = sb("heads", [DH, DH])
        minus_half = sb("minus_half", [128, NC])
        hat1 = early("hat1", [128, NBATCH, NIMG]); hat2 = sb("hat2", [32, NBATCH, NIMG])
        hat_t = early("hat_t", [128, NBATCH, NIMG])
        off1 = sb("off1", [128, NBATCH]); off2 = sb("off2", [32, NBATCH])
        x0 = early("x0", [128, 6, 32]); x1 = early("x1", [128, 6, 2, 16]); x2 = early("x2", [128, 6, 4, 8])
        x1r = early("x1r", [128, 24, 8]); x2r = early("x2r", [128, 96, 2])
        idx = sb("idx", [128, NQ], I32); hi_i = sb("hi_i", [128, NQ], I32); lo_i = sb("lo_i", [128, NQ], I32)
        hi_bf = sb("hi_bf", [128, NQ], BF16); lo_f = sb("lo_f", [128, NQ])
        lo_mask = [early("lo_mask0", [128, 32, 32]), early("lo_mask1", [128, 8, 8]), early("lo_mask2", [128, 2, 2])]
        hot_t = early("hot_t", [128, 2, 512]); hot = early("hot", [128, 2, 512])
        picked = early("picked", [128, 2, 384])
        feat = [early("feat0", [128, 2, 32 * 3]), early("feat1", [128, 2, 8 * 12]), early("feat2", [128, 2, 2 * 48])]
        w0 = early("w0", [EMB, 48]); w1 = early("w1", [EMB, 192]); w2 = early("w2", [EMB, 768])
        wf = early("wf", [DH, 2, D]); gate = early("gate", [E, D])
        eb3 = early("eb3", [E, BOT])
        w2T = early("w2T", [96, 8, EMB]); w0T = sb("w0T", [48, EMB]); w1T = sb("w1T", [96, 2, EMB])
        wfT = sb("wfT", [EMB, 3, D]); gateT = sb("gateT", [DH, 2, E])
        b3T = sb("b3T", [BOT, E + 2])
        tb = sb("tb", [EMB, 3]); bf_bc = sb("bf_bc", [TC, D])
        f0T = early("f0T", [48, 512]); f12T = early("f12T", [96, 4, 128])
        y0T = early("y0T", [EMB + 32, 512]); y1T = sb("y1T", [EMB, 128]); y2T = sb("y2T", [EMB, 32])
        g1 = sb("g1", [128, D]); w0g2 = sb("w0g2", [EMB + 32, D])
        h3 = late("h3", [TC, NC, D]); x2t = late("x2t", [TC, NC, D]); xT = late("xT", [DH + 1, 2, NT])
        h1T = late("h1T", [128, 6, NT])
        h = sb("h", [TC, NC, D]); an = sb("an", [TC, NC, D]); norm = sb("norm", [TC, NC, D])
        stats = sb("stats", [TC, NC, 6]); mv = sb("mv", [TC, NC, 2])
        var_e = sb("var_e", [TC, NC]); r1 = sb("r1", [TC, NC]); r2 = sb("r2", [TC, NC]); r12 = sb("r12", [TC, NC])
        rt = sb("rt", [TC, NC])
        qT = attn("qT", [DH, 2, NT]); oT = attn("oT", [DH + 1, 2, NT])
        qe = attn("qe", [DH, 2, NTOK]); ke = attn("ke", [TC, 2, D])
        kt = attn("kt", [TC, NC, D]); vt = attn("vt", [TC, NC, 2, DH + 1])
        kvx = attn("kvx", [DH, 4, DH + HPH]); ksum = sb("ksum", [DH, 4])
        ot = attn("ot", [TC, 2, D]); rz = sb("rz", [TC, NC, 2, HPH])
        qkv_w = sb("qkv_w", [DH + 1, 2, 3 * D]); proj_w = sb("proj_w", [DH + 1, 2, D])
        fc1_w = sb("fc1_w", [DH, 2, HID]); fc2_w = sb("fc2_w", [128, 6, D])
        fc1_b = sb("fc1_b", [128, 6]); fc2_bc = sb("fc2_bc", [TC, D])
        lnw = sb("lnw", [DH, 4, 2])
        sc = routing("sc", [TC, NC, E]); sm = sb("sm", [TC, NC]); top = sb("top", [TC, NC, 8])
        topi = sb("topi", [TC, NC, 8], U32); topf = sb("topf", [TC, NC, 2]); tw = sb("tw", [TC, NC, 2])
        tws = sb("tws", [TC, NC]); oneh = routing("oneh", [TC, 2, NC, E]); sel = routing("sel", [TC, NC, E])
        pre = routing("pre", [TC, NC, E]); rank = routing("rank", [TC, NC, E])
        place = routing("place", [TC, NC, E]); placed = routing("placed", [TC, 2, NC, E])
        dest_f = sb("dest_f", [TC, NC, 2]); dest = sb("dest", [TC, NC, 2], I32)
        blk_i = sb("blk_i", [TC, E], I32); blk = sb("blk", [TC, 2, E])
        cum = sb("cum", [TC, 2, 2, E]); before = sb("before", [TC, 2, E]); due = sb("due", [TC, E]); takes = sb("takes", [TC, E]); row_0 = sb("row_0", [TC, E])
        part = sb("part", [128, 1]); facts = sb("facts", [TC, 4, E]); fact = sb("fact", [TC, 4])
        table = sb("table", [1, 5, TC], I32); total = sb("total", [1, 3], I32); total_f = sb("total_f", [1, 2])
        ew1 = sb("ew1", [DH + 1, WBUF, 2, EHID]); ew2 = sb("ew2", [128, WBUF, 4, EHID]); ew3 = sb("ew3", [128, WBUF, 4 * BOT])
        ewl = sb("ewl", [BOT + 1, WBUF, D]); eb2 = sb("eb2", [128, WBUF, EHID])
        gelu_of_one = sb("gelu_of_one", [1, 1])
        zero = sb("zero", [SLOTS, D])
        bx = sb("bx", [SLOTS, D]); bxT = sb("bxT", [DH + 1, 2, SLOTS]); bh1 = sb("bh1", [SLOTS, EHID]); bh1T = sb("bh1T", [128, 4, SLOTS])
        bpre = sb("bpre", [SLOTS, EHID]); bh2 = sb("bh2", [SLOTS, EHID]); bh2T = sb("bh2T", [128, 4, SLOTS])
        bw3 = sb("bw3", [128, 4 * BOT]); bzT = sb("bzT", [BOT + 1, SLOTS]); by = sb("by", [SLOTS, D])
        base = an
        picked_y = h1T[0:TC, :, 0:2 * D].rearrange("p c (k d) -> p c k d", k=2)

        s_x = sem("x_loaded"); s_x1 = sem("x1_loaded"); s_x2 = [sem("x2_loaded_by_sync"), sem("x2_loaded_by_pool")]; s_idx = sem("idx_loaded")
        s_tw = sem("token_weights_loaded"); s_aw = sem("qkv_and_norm_weights_loaded"); s_mw = sem("proj_and_mlp_weights_loaded"); s_txt = sem("text_loaded")
        s_id = sem("identity_built"); s_cst = sem("constants_built"); s_off = sem("hat_offsets_built")
        s_wT = sem("weights_turned"); s_wTc = sem("turned_weights_copied")
        s_hi = sem("hi_ready"); s_bc = sem("hi_spread"); s_hot = sem("hi_onehot_ready"); s_gat = sem("pair_gathered")
        s_pick = sem("pair_picked"); s_xr = sem("x_reordered"); s_hatp = sem("hat_position"); s_hat = sem("hats_built")
        s_fT = sem("features_turned"); s_fTc = sem("features_copied"); s_y = sem("levels_done"); s_yc = sem("levels_copied")
        s_g = sem("level_fused"); s_gc = sem("level_fused_copied"); s_h = sem("h_summed"); s_hc = sem("h_ready")
        s_st = sem("stats_ready"); s_r = sem("rstd_ready"); s_n = sem("normed"); s_nT = sem("normed_turned")
        s_xT = sem("xT_ready"); s_q = sem("q_done"); s_qe = sem("q_exp"); s_qc = sem("q_ready")
        s_kv = sem("kv_done"); s_ke = sem("k_exp"); s_vc = sem("v_ready"); s_kc = sem("k_ready")
        s_kvs = sem("kv_summed"); s_kvc = sem("kv_ready"); s_o = sem("attn_out"); s_oc = sem("attn_out_divided")
        s_oT = sem("attn_out_turned"); s_oTc = sem("attn_out_ready")
        s_pr = sem("proj_done"); s_x2r = sem("x2_ready"); s_base = sem("base_ready")
        s_f1 = sem("fc1_done"); s_f1c = sem("fc1_ready"); s_f2 = sem("fc2_done"); s_h3 = sem("h3_ready")
        s_lg = sem("logits_done"); s_mx = sem("logits_shifted"); s_ex = sem("exp_done"); s_sel = sem("selected")
        s_rk = sem("ranks_done"); s_sched = sem("schedule_ready");
        s_dest = sem("row_numbers_ready"); s_fact = sem("facts_ready"); s_tab = sem("tables_spread")
        s_sc = sem("tokens_scattered"); s_xl = sem("block_loaded"); s_xt = sem("block_turned"); s_xc = sem("block_x_ready")
        s_kl = sem("expert_loaded"); s_w1 = sem("block_w1_done"); s_h1 = [sem(f"block_h1_half_{g}") for g in range(2)]
        s_t1 = sem("block_h1_turned"); s_h1T = [sem(f"block_h1T_half_{g}") for g in range(2)]
        s_w2 = sem("block_w2_done"); s_pre = [sem(f"block_w2_b2_half_{g}") for g in range(2)]
        s_h2 = [sem(f"block_h2_half_{g}") for g in range(2)]; s_t2 = sem("block_h2_turned")
        s_h2T = [sem(f"block_h2T_half_{g}") for g in range(2)]; s_w3c = sem("block_w3_weights_ready"); s_w3 = sem("block_w3_done")
        s_z = sem("block_z_ready"); s_wl = sem("block_wl_done"); s_by = sem("block_y_ready"); s_ys = sem("block_y_stored")
        s_zd = sem("zeros_stored"); s_yfree = sem("block_y_free")
        s_ew = [sem(f"expert_weights_{s}") for s in range(WBUF)]
        s_pk = [sem(f"rows_picked_{c}") for c in range(NC)]; s_fin = sem("out_ready"); s_zero = sem("zeros_ready"); s_out = sem("out_stored")
        s_dc = sem("vector_chain"); s_pc = sem("pool_chain"); s_ac = sem("scalar_chain"); s_ones = sem("ones_rows")

        block = ctx.enter_context(nc.Block())

        def lookup(eng, t, at, lo, hi):
            return eng.value_load(table[0:1, t, bass.ds(at, 1)], min_val=lo, max_val=hi)

        def blocks(eng):
            return eng.value_load(total[0:1, 0:1], min_val=2 * NT // SLOTS, max_val=MAXB)

        def blocks_but_one(eng):
            return eng.value_load(total[0:1, 2:3], min_val=2 * NT // SLOTS - 1, max_val=MAXB - 1)

        def chained(eng, s):
            count = [0]

            def link(ins):
                count[0] += 1
                ins.then_inc(s, 1)
                eng.wait_ge(s, count[0])

            def count_up(ins):
                count[0] += 1
                ins.then_inc(s, 1)
                return count[0]
            return link, count_up

        def load_expert(sp, k, s):
            e = lookup(sp, ACTIVE, k, 0, E - 1)

            def at(name):
                return a[name][bass.ds(e, 1)]
            sp.dma_start(ew1[0:DH, s, :, :], at("L0_ffn_W1").rearrange("o (k p) h -> p (o k) h", p=DH)).then_inc(s_ew[s], 16)
            sp.dma_start(ew1[DH:DH + 1, s, 1, :], at("L0_ffn_b1")).then_inc(s_ew[s], 16)
            sp.dma_start(ew2[:, s, :, :], at("L0_ffn_W2").rearrange("o (k p) h -> p (o k) h", p=128)).then_inc(s_ew[s], 16)
            sp.dma_start(eb2[:, s, :], at("L0_ffn_b2").to_broadcast([128, EHID])).then_inc(s_ew[s], 16)
            sp.dma_start(ew3[:, s, :].rearrange("p (k h) -> p k h", k=4),
                         at("L0_ffn_W3").rearrange("o (k p) h -> p (o k) h", p=128)).then_inc(s_ew[s], 16)
            sp.dma_start(ewl[0:BOT, s, :], at("L0_ffn_Wl").rearrange("o p h -> (o p) h")).then_inc(s_ew[s], 16)
            sp.dma_start(ewl[BOT:BOT + 1, s, :], at("L0_ffn_bl")).then_inc(s_ew[s], 16)

        @block.sync
        def _(sp):
            sp.dma_start(idx[:, 0:32].rearrange("p (t g) -> p t g", t=2), dv["i0"]).then_inc(s_idx, 16)
            sp.dma_start(idx[:, 32:40], dv["i1"]).then_inc(s_idx, 16)
            sp.dma_start(idx[:, 40:42], dv["i2"]).then_inc(s_idx, 16)
            sp.dma_start(x0[:, :, :], dv["x0"]).then_inc(s_x, 16)
            for i in range(4):
                for iy in range(2):
                    sp.dma_start(x1[i:128:4, :, iy, :], dv["x1"][i, :, :, iy]).then_inc(s_x1, 16)
            for i in range(X2_SP):
                for iy in range(4):
                    sp.dma_start(x2[i:128:8, :, iy, :], dv["x2"][i, :, :, iy]).then_inc(s_x2[0], 16)
            sp.wait_ge(s_zero, 1)
            sp.wait_ge(s_st, 1)
            sp.dma_start(rows.rearrange("(k p) d -> p k d", p=SLOTS),
                         zero[:, :].unsqueeze(1).to_broadcast([SLOTS, MAXB + 3, D])).then_inc(s_zd, 16)
            sp.wait_ge(s_sched, 1)
            rounds = sp.value_load(total[0:1, 1:2], min_val=1, max_val=E // WBUF)

            def tell_loaded(s, loads):
                sp.wait_ge(s_ew[s], loads)
                sp.nop(nofuse=True).then_inc(s_kl, 1)

            load_expert(sp, 0, 1)
            sp.wait_ge(s_xl, 16)
            tell_loaded(1, 112)
            for j in range(1, WBUF):
                load_expert(sp, j, (j + 1) % WBUF)
                if j > 1:
                    tell_loaded(j, 112)
            tell_loaded(0, 112)
            with sp.If(rounds > 1):
                with sp.Fori(1, rounds) as i:
                    for j in range(WBUF):
                        k = sp.snap(i * WBUF + j)
                        sp.wait_ge(s_wl, lookup(sp, SPENT, k, 1, MAXB + 1))
                        sp.nop(nofuse=True)
                        load_expert(sp, k, (j + 1) % WBUF)
                        if j:
                            tell_loaded(j, i * 112 + 112)
                    tell_loaded(0, i * 112 + 112)
            for c in range(NC):
                sp.wait_ge(s_fin, c + 1)
                sp.dma_start(out_chunks[c], an[:, c, :]).then_inc(s_out, 16)
            sp.wait_ge(s_out, 16 * NC)

        @block.gpsimd
        def _(pool):
            link, _ = chained(pool, s_pc)
            link(pool.memset(ident[:, :], 0.0))
            link(pool.affine_select(out=ident[:, :], in_=ident[:, :], compare_op=ALU.not_equal, fill=1.0, base=0,
                                    pattern=[[-1, 128]], channel_multiplier=1))
            pool.tensor_copy(ident_bf[:, :], ident[:, :]).then_inc(s_id, 1)
            pool.iota(neg_part[:, :], [[0, 1]], base=0, channel_multiplier=-1,
                      allow_small_or_imprecise_dtypes=True).then_inc(s_id, 1)
            pool.iota(iota_row[:, :], [[1, E]], base=0, channel_multiplier=0,
                      allow_small_or_imprecise_dtypes=True).then_inc(s_id, 1)
            pool.iota(hat_t[:, :, :], [[0, NBATCH], [1, NIMG]], base=0, channel_multiplier=0,
                      allow_small_or_imprecise_dtypes=True).then_inc(s_off, 1)
            pool.iota(off1[:, :], [[64, NBATCH]], base=0, channel_multiplier=-1,
                      allow_small_or_imprecise_dtypes=True).then_inc(s_off, 1)
            pool.iota(off2[:, :], [[16, NBATCH]], base=0, channel_multiplier=-1,
                      allow_small_or_imprecise_dtypes=True).then_inc(s_off, 1)
            pool.memset(ones[:, :], 1.0).then_inc(s_cst, 1)
            pool.memset(minus_half[:, :], -0.5).then_inc(s_cst, 1)
            link(pool.memset(earlier[:, :], 1.0))
            pool.affine_select(out=earlier[:, :], in_=earlier[:, :], compare_op=ALU.is_gt, fill=0.0, base=0,
                               pattern=[[1, TC]], channel_multiplier=-1).then_inc(s_cst, 1)
            link(pool.memset(heads[:, :], 1.0))
            hv = heads[:, :].rearrange("p (h d) -> p h d", d=HEAD)
            link(pool.affine_select(out=hv, in_=hv, compare_op=ALU.is_ge, fill=0.0, base=0,
                                    pattern=[[-HEAD, DH // HEAD], [0, HEAD]], channel_multiplier=1))
            pool.affine_select(out=hv, in_=hv, compare_op=ALU.is_ge, fill=0.0, base=HEAD - 1,
                               pattern=[[HEAD, DH // HEAD], [0, HEAD]], channel_multiplier=-1).then_inc(s_cst, 1)

            for i in range(X2_SP, 8):
                for iy in range(4):
                    pool.dma_start(x2[i:128:8, :, iy, :], dv["x2"][i, :, :, iy]).then_inc(s_x2[1], 16)
            for i, name in enumerate(("L0_tok_W0", "L0_tok_W1", "L0_tok_W2")):
                pool.dma_start((w0, w1, w2)[i][:, :], a[name]).then_inc(s_tw, 16)
            pool.dma_start(wf[:, :, :], a["L0_tok_Wf"].rearrange("(k p) d -> p k d", p=DH)).then_inc(s_tw, 16)
            pool.dma_start(gate[:, :], a["L0_ffn_gate_w"]).then_inc(s_tw, 16)
            pool.dma_start(eb3[:, :], a["L0_ffn_b3"]).then_inc(s_tw, 16)
            for i in range(3):
                pool.dma_start(tb[:, i:i + 1], column(a[f"L0_tok_b{i}"])).then_inc(s_tw, 16)
            pool.dma_start(bf_bc[:, :], row(a["L0_tok_bf"]).to_broadcast([TC, D])).then_inc(s_tw, 16)
            for b in range(NBATCH):
                pool.dma_start(h[TC - TXT:TC, CPB * b + CPB - 1, :], a["txt"][b]).then_inc(s_txt, 16)
            pool.dma_start(qkv_w[0:DH, :, :], a["L0_attn_qkv_w"].rearrange("(k p) n -> p k n", p=DH)).then_inc(s_aw, 16)
            pool.dma_start(qkv_w[DH:DH + 1, 1, :], row(a["L0_attn_qkv_b"])).then_inc(s_aw, 16)
            for i, name in enumerate(("ln1_w", "ln1_b", "ln2_w", "ln2_b")):
                pool.dma_start(lnw[:, i, :], a[f"L0_attn_{name}"].rearrange("(k p) -> p k", p=DH), allow_slow_non_contiguous=True).then_inc(s_aw, 16)
            pool.dma_start(proj_w[0:DH, :, :], a["L0_attn_proj_w"].rearrange("(k p) n -> p k n", p=DH)).then_inc(s_mw, 16)
            pool.dma_start(proj_w[DH:DH + 1, 1, :], row(a["L0_attn_proj_b"])).then_inc(s_mw, 16)
            pool.dma_start(fc1_w[:, :, :], a["L0_attn_fc1_w"].rearrange("(k p) n -> p k n", p=DH)).then_inc(s_mw, 16)
            pool.dma_start(fc2_w[:, :, :], a["L0_attn_fc2_w"].rearrange("(k p) n -> p k n", p=128)).then_inc(s_mw, 16)
            pool.dma_start(fc1_b[:, :], a["L0_attn_fc1_b"].rearrange("(k p) -> p k", p=128), allow_slow_non_contiguous=True).then_inc(s_mw, 16)
            pool.dma_start(fc2_bc[:, :], row(a["L0_attn_fc2_b"]).to_broadcast([TC, D])).then_inc(s_mw, 16)

            def rstd(to, variance, eps, b):
                c = slice(CPB * b, CPB * (b + 1))
                link(pool.tensor_scalar(var_e[:, c], variance[:, c], eps, None, ALU.add))
                return pool.tensor_tensor(to[:, c], var_e[:, c], minus_half[0:TC, c], ALU.pow)

            for b in range(NBATCH):
                c = slice(CPB * b, CPB * (b + 1))
                pool.wait_ge(s_st, b + 1)
                link(rstd(r1, mv[:, :, 1], 1e-5, b))
                link(pool.tensor_tensor(rt[:, c], r1[:, c], r1[:, c], ALU.mult))
                link(pool.tensor_tensor(rt[:, c], rt[:, c], mv[:, c, 1], ALU.mult))
                link(rstd(r2, rt, 1e-8, b))
                link(pool.tensor_tensor(r12[:, c], r1[:, c], r2[:, c], ALU.mult))
                pool.nop(nofuse=True).then_inc(s_r, 1)
            for t in (oT, xT):
                link(pool.memset(t[DH:DH + 1, 1, :], 1.0))
            link(pool.memset(bzT[BOT:BOT + 1, :], 1.0))
            link(pool.memset(bxT[DH:DH + 1, 1, :], 1.0))
            pool.memset(vt[:, :, :, DH:DH + 1], 1.0).then_inc(s_ones, 1)
            for b in range(NBATCH):
                pool.wait_ge(s_st, NBATCH + b + 1)
                rstd(r1, mv[:, :, 1], 1e-8, b).then_inc(s_r, 1)
            pool.wait_ge(s_mw, 16 * 6)
            for c in range(NC):
                link(pool.tensor_tensor(base[:, c, :], h[:, c, :], x2t[:, c, :], ALU.add))
                pool.tensor_tensor(base[:, c, :], base[:, c, :], fc2_bc[:, :], ALU.add).then_inc(s_base, 1)
            for b in range(NBATCH):
                pool.wait_ge(s_st, 2 * NBATCH + b + 1)
                rstd(r1, mv[:, :, 1], 1e-5, b).then_inc(s_r, 1)

            pool.wait_ge(s_dest, 1)
            pool.wait_ge(s_zd, 16)
            for c in range(NC):
                for k in range(2):
                    pool.indirect_dma_start(out=rows[:, :], out_offset=bass.IndirectOffsetOnAxis(ap=dest[:, c, k:k + 1], axis=0),
                                            in_=norm[:, c, :], in_offset=None).then_inc(s_sc, 16)
            def store_block(b1):
                pool.wait_ge(s_by, b1 + 1)
                pool.nop(nofuse=True)
                pool.dma_start(rows[bass.ds(b1 * SLOTS, SLOTS), :], by[:, :]).then_inc(s_ys, 16)
                pool.wait_ge(s_ys, b1 * 16)
                pool.nop(nofuse=True).then_inc(s_yfree, 1)

            pool.nop(nofuse=True).then_inc(s_yfree, 1)
            pool.wait_ge(s_sched, 1)
            nb = blocks(pool)
            with pool.Fori(1, nb) as b1:
                store_block(b1)
            store_block(nb)

            for c in range(NC):
                for k in range(2):
                    pool.indirect_dma_start(out=picked_y[:, c, k, :], out_offset=None, in_=rows[:, :],
                                            in_offset=bass.IndirectOffsetOnAxis(ap=dest[:, c, k:k + 1], axis=0)
                                            ).then_inc(s_pk[c], 16)

        @block.vector
        def _(dve):
            link, count_up = chained(dve, s_dc)
            dve.memset(zero[:, :], 0.0).then_inc(s_zero, 1)
            dve.wait_ge(s_idx, 48)
            for (at, n), bits in zip(((0, 32), (32, 8), (40, 2)), (5, 3, 1)):
                dve.tensor_scalar(hi_i[:, at:at + n], idx[:, at:at + n], bits, None, ALU.logical_shift_right)
                last = dve.tensor_scalar(lo_i[:, at:at + n], idx[:, at:at + n], (1 << bits) - 1, None, ALU.bitwise_and)
            link(last)
            dve.tensor_copy(hi_bf[:, :], hi_i[:, :]).then_inc(s_hi, 1)
            link(dve.tensor_copy(lo_f[:, :], lo_i[:, :]))
            dve.wait_ge(s_id, 3)
            for l, (at, n) in enumerate(((0, 32), (32, 8), (40, 2))):
                w = 1 << LEVELS[l][1]
                last = dve.tensor_tensor(lo_mask[l][:, :, :], iota_row[:, 0:w].unsqueeze(1).to_broadcast([128, n, w]),
                                         lo_f[:, at:at + n].unsqueeze(2).to_broadcast([128, n, w]), ALU.is_equal)
            link(last)
            dve.tensor_scalar(part[:, :], neg_part[:, :], -1.0, None, ALU.mult)
            dve.wait_ge(s_off, 3)
            for l, (t, n) in enumerate(((hat1, 64), (hat2, 16))):
                p = t.shape[0]
                link(dve.tensor_scalar(t[:, :, :], hat_t[0:p, :, :], n / NIMG, 0.5 * n / NIMG - 0.5, ALU.mult, ALU.add))
                dve.tensor_scalar(t[:, :, :], t[:, :, :], 0.0, float(n - 1), ALU.max, ALU.min).then_inc(s_hatp, 1)
            for i, (q, l) in enumerate(PAIRS):
                f, w = LEVELS[l][2], 1 << LEVELS[l][1]
                q0 = q - (0, 32, 40)[l]
                dve.wait_ge(s_gat, i + 1)
                tmp = picked[:, i % 2, :].rearrange("p (k f w) -> p k f w", k=2, w=w)
                link(dve.tensor_tensor(tmp, bank[6 + i % 2][:, 0:384].rearrange("p (k f w) -> p k f w", k=2, w=w),
                                       lo_mask[l][:, q0:q0 + 2, :].unsqueeze(2).to_broadcast([128, 2, f, w]), ALU.mult))
                dst = feat[l][:, :, :].rearrange("p b (k f) -> p k b f", f=f // 2)[:, q0:q0 + 2]
                src = picked[:, i % 2, :].rearrange("p (k b f w) -> p k b f w", k=2, b=2, w=w)
                dve.tensor_reduce(dst, src, AX_X, ALU.add).then_inc(s_pick, 1)
            dve.wait_ge(s_fT, 2)
            dve.tensor_copy(f12T[:, :, :], bank[1][0:96, :].rearrange("p (a q) -> p a q", a=4)).then_inc(s_fTc, 1)
            dve.wait_ge(s_y, 2)
            dve.wait_ge(s_tw, 16 * 10)
            dve.tensor_scalar(y1T[:, :], bank[3][0:EMB, 0:128], tb[:, 1:2], None, ALU.add).then_inc(s_yc, 1)
            dve.tensor_scalar(y2T[:, :], bank[3][0:EMB, 128:160], tb[:, 2:3], None, ALU.add).then_inc(s_yc, 1)
            dve.wait_ge(s_txt, 32)
            for c in range(NC + 1):
                if c < NC:
                    m = TC if c % CPB < CPB - 1 else TC - TXT
                    dve.wait_ge(s_h, c + 1)
                    dve.tensor_tensor(h[0:m, c, :], bank[6 + c % 2][0:m, 0:D], bf_bc[0:m, :], ALU.add).then_inc(s_hc, 1)
                if c >= 1:
                    dve.wait_ge(s_dc, done)
                    ins = dve.bn_aggr(mv[:, c - 1, :], stats[:, c - 1, :])
                    if c % CPB == 0:
                        ins.then_inc(s_st, 1)
                if c < NC:
                    dve.wait_ge(s_hc, c + 1)
                    done = count_up(dve.bn_stats(stats[:, c, :], h[:, c, :]))

            def normalise(dst, src, scale, c):
                return dve.tensor_scalar(dst[:, c, :], src[:, c, :], mv[:, c, 0:1], scale[:, c:c + 1],
                                         ALU.subtract, ALU.mult)

            def turned(first, k_lnw):
                for b in range(NBATCH):
                    for k in range(2):
                        i = 2 * k + b
                        dve.wait_ge(s_nT, first + 2 * b + k + 1)
                        dst = xT[0:DH, k, b * NTOK:(b + 1) * NTOK]
                        if k_lnw is None:
                            ins = dve.tensor_copy(dst, bank[i][0:DH, 0:NTOK])
                        else:
                            ins = dve.tensor_scalar(dst, bank[i][0:DH, 0:NTOK], lnw[:, k_lnw, k:k + 1],
                                                    lnw[:, k_lnw + 1, k:k + 1], ALU.mult, ALU.add)
                        ins.then_inc(s_xT, 1)

            for c in range(NC):
                dve.wait_ge(s_r, c // CPB + 1)
                normalise(norm, h, r12, c).then_inc(s_n, 1)
            dve.wait_ge(s_aw, 16 * 6)
            turned(0, 0)
            for c in range(NC):
                last = normalise(an, h, r1, c)
            link(last)
            for i in range(4):
                b, m = i // 2, i % 2
                dve.wait_ge(s_qe, i + 1)
                link(dve.tensor_scalar(qe[:, i % 2, :], qe[:, i % 2, :], 1.0, None, ALU.min))
                dve.scalar_tensor_tensor(out=qT[:, m, b * NTOK:(b + 1) * NTOK], in0=bank[4 + i][0:DH, 0:NTOK], scalar=0.0,
                                         in1=qe[:, i % 2, :], op0=ALU.max, op1=ALU.add).then_inc(s_qc, 1)
            for c in range(NC):
                dve.wait_ge(s_ke, c + 1)
                link(dve.tensor_scalar(ke[:, c % 2, :], ke[:, c % 2, :], 1.0, None, ALU.min))
                dve.scalar_tensor_tensor(out=kt[:, c, :], in0=bank[c % 4][0:TC, 0:D], scalar=0.0,
                                         in1=ke[:, c % 2, :], op0=ALU.max, op1=ALU.add).then_inc(s_kc, 1)
            dve.wait_ge(s_cst, 4)
            dve.wait_ge(s_kvs, 1)
            kvp = bank[2][0:DH, 0:4 * (DH + 1)].rearrange("p (g n) -> p g n", g=4)
            dve.tensor_tensor(kvx[:, :, 0:DH], kvp[:, :, 0:DH], heads[:, :].unsqueeze(1).to_broadcast([DH, 4, DH]), ALU.mult).then_inc(s_kvc, 1)
            link(dve.tensor_copy(ksum[:, :], kvp[:, :, DH]))
            one_column = heads[:, :].rearrange("p (h d) -> p h d", d=HEAD)[:, :, 0]
            dve.tensor_tensor(kvx[:, :, DH:DH + HPH], one_column.unsqueeze(1).to_broadcast([DH, 4, HPH]),
                              ksum[:, :].unsqueeze(2).to_broadcast([DH, 4, HPH]), ALU.mult).then_inc(s_kvc, 1)

            def attended(c):
                return bank[4 + c % 2][0:TC, 0:2 * (DH + HPH)].rearrange("p (m n) -> p m n", m=2)

            def invert(c):
                dve.wait_ge(s_o, c + 1)
                return count_up(dve.reciprocal(rz[:, c, :, :], attended(c)[:, :, DH:DH + HPH]))

            def divide(c, inverted):
                if c >= 2:
                    dve.wait_ge(s_oT, c - 1)
                dve.wait_ge(s_dc, inverted)
                for m in range(2):
                    ins = dve.tensor_tensor(ot[:, c % 2, m * DH:(m + 1) * DH].rearrange("p (h d) -> p h d", d=HEAD),
                                            attended(c)[:, m, 0:DH].rearrange("p (h d) -> p h d", d=HEAD),
                                            rz[:, c, m, :].unsqueeze(2).to_broadcast([TC, HPH, HEAD]), ALU.mult)
                ins.then_inc(s_oc, 1)

            for c in range(3):
                divide(c, invert(c))
            for c in range(NC):
                dve.wait_ge(s_pr, c + 1)
                ins = dve.tensor_tensor(x2t[:, c, :], bank[c % 2][0:TC, 0:D], an[:, c, :], ALU.add)
                ins.then_inc(s_x2r, 1)
                if c + 3 < NC:
                    inverted = invert(c + 3)
                dve.wait_ge(s_x2r, c + 1)
                done = count_up(dve.bn_stats(stats[:, c, :], x2t[:, c, :]))
                if c + 3 < NC:
                    divide(c + 3, inverted)
                dve.wait_ge(s_dc, done)
                ins = dve.bn_aggr(mv[:, c, :], stats[:, c, :])
                if c % CPB == CPB - 1:
                    ins.then_inc(s_st, 1)
            for c in range(NC):
                dve.wait_ge(s_r, NBATCH + c // CPB + 1)
                normalise(norm, x2t, r1, c).then_inc(s_n, 1)
            turned(4, 2)
            for c in range(NC):
                dve.wait_ge(s_base, c + 1)
                dve.wait_ge(s_f2, c + 1)
                ins = dve.tensor_tensor(h3[:, c, :], bank[c % 2][0:TC, 0:D], base[:, c, :], ALU.add)
                ins.then_inc(s_h3, 1)
                dve.wait_ge(s_h3, c + 1)
                link(dve.bn_stats(stats[:, c, :], h3[:, c, :]))
                link(dve.bn_aggr(mv[:, c, :], stats[:, c, :]))
                if c % CPB == CPB - 1:
                    dve.nop(nofuse=True).then_inc(s_st, 1)
            for c in range(NC):
                dve.wait_ge(s_r, 2 * NBATCH + c // CPB + 1)
                normalise(norm, h3, r1, c).then_inc(s_n, 1)
            turned(8, None)

            dve.wait_ge(s_lg, 1)
            lg = bank[4][0:TC, 0:NC * E].rearrange("p (c e) -> p c e", c=NC)
            link(dve.tensor_reduce(sm[:, :], lg, AX_X, ALU.max))
            dve.tensor_tensor(sc[:, :, :], lg, sm[:, :].unsqueeze(2).to_broadcast([TC, NC, E]), ALU.subtract).then_inc(s_mx, 1)
            dve.wait_ge(s_ex, 1)
            link(dve.tensor_reduce(sm[:, :], sc[:, :, :], AX_X, ALU.add))
            link(dve.reciprocal(sm[:, :], sm[:, :]))
            link(dve.tensor_tensor(sc[:, :, :], sc[:, :, :], sm[:, :].unsqueeze(2).to_broadcast([TC, NC, E]), ALU.mult))
            for c in range(NC):
                last = dve.max(top[:, c, :], sc[:, c, :])
            link(last)
            for c in range(NC):
                last = dve.max_index(topi[:, c, :], top[:, c, :], sc[:, c, :])
            link(last)
            link(dve.tensor_copy(topf[:, :, :], topi[:, :, 0:2]))
            for k in range(2):
                last = dve.tensor_tensor(oneh[:, k, :, :], iota_row[0:TC, 0:E].unsqueeze(1).to_broadcast([TC, NC, E]),
                                         topf[:, :, k:k + 1].to_broadcast([TC, NC, E]), ALU.is_equal)
            link(last)
            ins = dve.tensor_tensor(sel[:, :, :], oneh[:, 0, :, :], oneh[:, 1, :, :], ALU.add)
            ins.then_inc(s_sel, 1)
            link(dve.tensor_tensor(tws[:, :], top[:, :, 0], top[:, :, 1], ALU.add))
            link(dve.tensor_scalar(tws[:, :], tws[:, :], 1e-20, None, ALU.add))
            link(dve.reciprocal(tws[:, :], tws[:, :]))
            link(dve.tensor_tensor(tw[:, :, :], top[:, :, 0:2], tws[:, :].unsqueeze(2).to_broadcast([TC, NC, 2]), ALU.mult))
            link(dve.memset(pre[:, 0, :], 0.0))
            dve.wait_ge(s_rk, 1)
            counts = bank[5][0:TC, 0:NC * E].rearrange("p (c e) -> p c e", c=NC)

            def add_chunk(c):
                return dve.tensor_tensor(pre[:, c + 1, :], pre[:, c, :], counts[:, c, :], ALU.add)

            dve.tensor_reduce(takes[:, :], bank[5][0:TC, 0:NC * E].rearrange("p (c e) -> p e c", c=NC), AX_X, ALU.add)
            link(add_chunk(0))
            dve.tensor_scalar(due[:, :], takes[:, :], float(SLOTS - 1), None, ALU.add)
            link(add_chunk(1))
            dve.tensor_copy(blk_i[:, :], due[:, :])
            link(add_chunk(2))
            dve.tensor_scalar(blk_i[:, :], blk_i[:, :], SLOTS.bit_length() - 1, None, ALU.logical_shift_right)
            link(add_chunk(3))
            dve.tensor_scalar(blk[:, 1, :], takes[:, :], 0.0, None, ALU.is_gt)
            dve.tensor_copy(blk[:, 0, :], blk_i[:, :])
            link(add_chunk(4))
            dve.tensor_copy(cum[:, 0, :, :], blk[:, :, :])
            link(dve.tensor_tensor(rank[:, :, :], bank[5][0:TC, NC * E:2 * NC * E].rearrange("p (c e) -> p c e", c=NC),
                                   pre[:, :, :], ALU.add))
            at, step = 0, 1
            while step < E:
                dve.tensor_copy(cum[:, 1 - at, :, 0:step], cum[:, at, :, 0:step])
                link(dve.tensor_tensor(cum[:, 1 - at, :, step:E], cum[:, at, :, step:E], cum[:, at, :, 0:E - step], ALU.add))
                at, step = 1 - at, 2 * step
            upto = cum[:, at, :, :]
            link(dve.tensor_tensor(before[:, :, :], upto, blk[:, :, :], ALU.subtract))
            link(dve.tensor_scalar(row_0[:, :], before[:, 0, :], 1.0, float(SLOTS), ALU.add, ALU.mult))
            link(dve.tensor_tensor(place[:, :, :], rank[:, :, :], row_0[:, :].unsqueeze(1).to_broadcast([TC, NC, E]), ALU.add))
            link(dve.tensor_tensor(placed[:, :, :, :], place[:, :, :].unsqueeze(1).to_broadcast([TC, 2, NC, E]),
                                   oneh[:, :, :, :], ALU.mult))
            link(dve.tensor_reduce(dest_f[:, :, :].rearrange("p c k -> p k c"), placed[:, :, :, :], AX_X, ALU.add))
            link(dve.tensor_copy(dest[:, :, :], dest_f[:, :, :]))
            dve.nop(nofuse=True).then_inc(s_dest, 1)

            link(dve.tensor_scalar(due[:, :], before[:, 1, :], float(WBUF), None, ALU.add))
            for t, (limit, count) in enumerate(((before[:, 0, :], blk[:, 1, :]), (upto[:, 1, :], ones[0:TC, 0:E]),
                                                (due[:, :], blk[:, 0, :]), (before[:, 0, :], ones[0:TC, 0:E]))):
                last = dve.scalar_tensor_tensor(out=facts[:, t, :], in0=limit, scalar=part[0:TC, 0:1], in1=count,
                                                op0=ALU.is_le, op1=ALU.mult)
            link(last)
            link(dve.tensor_reduce(fact[:, :], facts[:, :, :], AX_X, ALU.add))
            dve.tensor_scalar(fact[:, ACTIVE:ACTIVE + 1], fact[:, ACTIVE:ACTIVE + 1], float(E - 1), None, ALU.min)
            link(dve.tensor_scalar(fact[:, SPENT:SPENT + 1], fact[:, SPENT:SPENT + 1], 1.0, None, ALU.add))
            dve.nop(nofuse=True).then_inc(s_fact, 1)
            link(dve.tensor_copy(total_f[0:1, :], upto[0:1, :, E - 1]))
            dve.tensor_copy(total[0:1, 0:1], total_f[0:1, 0:1])
            link(dve.tensor_scalar(total[0:1, 2:3], total_f[0:1, 0:1], -1.0, None, ALU.add))
            link(dve.tensor_scalar(total_f[0:1, 1:2], total_f[0:1, 1:2], float(WBUF - 1), None, ALU.add))
            link(dve.tensor_copy(total[0:1, 1:2], total_f[0:1, 1:2]))
            link(dve.tensor_scalar(total[0:1, 1:2], total[0:1, 1:2], WBUF.bit_length() - 1, None, ALU.logical_shift_right))
            dve.wait_ge(s_tab, 1)
            link(dve.tensor_copy(table[0:1, 0:4, :], bank[6][0:1, 0:4 * TC].rearrange("p (t n) -> p t n", t=4)))
            link(dve.tensor_scalar(table[0:1, SLOT, :], table[0:1, NUMBER, :], WBUF - 1, None, ALU.bitwise_and))
            dve.nop(nofuse=True).then_inc(s_sched, 1)
            def copy_turned(dst, src, done):
                for g in range(2):
                    dve.tensor_copy(dst[:, 2 * g:2 * g + 2, :],
                                    src[:, g * 2 * SLOTS:(g + 1) * 2 * SLOTS].rearrange("p (k s) -> p k s", k=2)).then_inc(done[g], 1)

            def copy_h1(b1):
                dve.wait_ge(s_t1, b1)
                dve.nop(nofuse=True)
                copy_turned(bh1T, bank[2], s_h1T)

            def add_b2(b1, at):
                slot = lookup(dve, SLOT, at, 0, WBUF - 1)
                dve.wait_ge(s_w2, b1)
                dve.nop(nofuse=True)
                for g in range(2):
                    f = slice(g * EHID // 2, (g + 1) * EHID // 2)
                    dve.tensor_tensor(bpre[:, f], bank[1][:, f], eb2[:, bass.ds(slot, 1), f].rearrange("p o f -> p (o f)"),
                                      ALU.add).then_inc(s_pre[g], 1)

            def copy_h2(b1):
                dve.wait_ge(s_t2, b1)
                dve.nop(nofuse=True)
                copy_turned(bh2T, bank[3], s_h2T)

            def add_b3(b1, at):
                e1 = lookup(dve, EXPERT, at, 1, E)
                dve.wait_ge(s_w3, b1)
                dve.nop(nofuse=True)
                dve.tensor_scalar(bzT[0:BOT, :], bank[5][0:BOT, 0:SLOTS], b3T[:, bass.ds(e1, 1)], None, ALU.add).then_inc(s_z, 1)

            nb = blocks(dve)
            copy_h1(1)
            with dve.Fori(0, nb - 1) as b:
                b1 = dve.snap(b + 1)
                add_b2(b1, b)
                copy_h2(b1)
                copy_h1(b1 + 1)
                add_b3(b1, b)
            add_b2(nb, nb - 1)
            copy_h2(nb)
            add_b3(nb, nb - 1)

            for c in range(NC):
                dve.wait_ge(s_pk[c], 32)
                link(dve.scalar_tensor_tensor(out=norm[:, c, :], in0=picked_y[:, c, 0, :], scalar=tw[:, c, 0:1],
                                              in1=h3[:, c, :], op0=ALU.mult, op1=ALU.add))
                dve.scalar_tensor_tensor(out=an[:, c, :], in0=picked_y[:, c, 1, :], scalar=tw[:, c, 1:2],
                                         in1=norm[:, c, :], op0=ALU.mult, op1=ALU.add).then_inc(s_fin, 1)

        @block.scalar
        def _(act):
            link, _ = chained(act, s_ac)
            def reorder_x():
                act.wait_ge(s_x1, 16 * 8)
                for b in range(NBATCH):
                    for iy in range(2):
                        o = b * 12 + iy * 6
                        act.copy(x1r[:, o:o + 6, :].rearrange("p (x c) l -> p c x l", c=3),
                                 x1[:, 3 * b:3 * b + 3, iy, :].rearrange("p c (l x) -> p c x l", x=2)).then_inc(s_xr, 1)
                act.wait_ge(s_x2[0], 16 * 4 * X2_SP)
                act.wait_ge(s_x2[1], 16 * 4 * (8 - X2_SP))
                for b in range(NBATCH):
                    for iy in range(4):
                        o = b * 48 + iy * 12
                        act.copy(x2r[:, o:o + 12, :].rearrange("p (x c) l -> p c x l", c=3),
                                 x2[:, 3 * b:3 * b + 3, iy, :].rearrange("p c (l x) -> p c x l", x=4)).then_inc(s_xr, 1)

            act.wait_ge(s_id, 3)
            for g, (q, n) in enumerate(GROUPS):
                if g == 9:
                    reorder_x()
                act.wait_ge(s_bc, g + 1)
                if g >= 2:
                    act.wait_ge(s_gat, 2 * (g - 1))
                link(act.activation(hot_t[:, g % 2, 0:n * 128], bank[4 + g % 2][:, 0:n * 128], ACT.Abs, bias=neg_part[:, 0:1]))
                act.activation(hot[:, g % 2, 0:n * 128], hot_t[:, g % 2, 0:n * 128], ACT.Relu, scale=-1.0, bias=1.0).then_inc(s_hot, 1)
            act.wait_ge(s_hatp, 2)
            for t, o in ((hat1, off1), (hat2, off2)):
                for b in range(NBATCH):
                    link(act.activation(t[:, b, :], t[:, b, :], ACT.Abs, bias=o[:, b:b + 1]))
            act.activation(hat1[:, :, :], hat1[:, :, :], ACT.Relu, scale=-1.0, bias=1.0).then_inc(s_hat, 1)
            act.activation(y0T[EMB:EMB + 32, :], hat2[:, :, :].rearrange("p b t -> p (b t)"), ACT.Relu, scale=-1.0,
                           bias=1.0).then_inc(s_hat, 1)
            act.wait_ge(s_wT, 1)
            act.copy(w2T[:, :, :], bank[0][0:96, :].rearrange("p (g e) -> p g e", g=8)).then_inc(s_wTc, 1)
            act.wait_ge(s_wT, 2)
            act.copy(w0T[:, :], bank[1][0:48, 0:64]).then_inc(s_wTc, 1)
            act.copy(w1T[:, :, :], bank[1][0:96, 64:192].rearrange("p (g e) -> p g e", g=2)).then_inc(s_wTc, 1)
            act.copy(wfT[:, 2, :], bank[1][0:EMB, 192:384]).then_inc(s_wTc, 1)
            act.wait_ge(s_wT, 3)
            act.copy(w0g2[0:EMB, :], bank[2][0:EMB, 0:D]).then_inc(s_wTc, 1)
            act.copy(wfT[:, 1, :], bank[2][0:EMB, D:2 * D]).then_inc(s_wTc, 1)
            act.wait_ge(s_wT, 4)
            act.copy(gateT[:, :, :], bank[3][0:DH, 0:64].rearrange("p (k e) -> p k e", k=2)).then_inc(s_wTc, 1)
            act.copy(b3T[:, 1:E + 1], bank[3][0:BOT, 320:352]).then_inc(s_wTc, 1)
            act.wait_ge(s_fT, 1)
            act.copy(f0T[:, :], bank[0][0:48, :]).then_inc(s_fTc, 1)
            act.wait_ge(s_y, 1)
            act.wait_ge(s_tw, 16 * 10)
            act.activation(y0T[0:EMB, :], bank[2][0:EMB, :], ACT.Identity, bias=tb[:, 0:1]).then_inc(s_yc, 1)
            act.wait_ge(s_g, 1)
            act.copy(g1[:, :], bank[4][:, 0:D]).then_inc(s_gc, 1)
            act.wait_ge(s_g, 2)
            act.copy(w0g2[EMB:EMB + 32, :], bank[5][0:32, 0:D]).then_inc(s_gc, 1)
            for i in range(4):
                act.wait_ge(s_q, i + 1)
                if i >= 2:
                    act.wait_ge(s_qc, i - 1)
                act.activation(qe[:, i % 2, :], bank[4 + i][0:DH, 0:NTOK], ACT.Exp).then_inc(s_qe, 1)
            for c in range(NC):
                act.wait_ge(s_kv, c + 1)
                if c >= 2:
                    act.wait_ge(s_kc, c - 1)
                act.activation(ke[:, c % 2, :], bank[c % 4][0:TC, 0:D], ACT.Exp).then_inc(s_vc, 1)
                act.copy(vt[:, c, :, 0:DH], bank[c % 4][0:TC, D:2 * D].rearrange("p (m e) -> p m e", m=2)).then_inc(s_ke, 1)
            for c in range(NC):
                act.wait_ge(s_oT, c + 1)
                act.copy(oT[0:DH, :, c * TC:(c + 1) * TC],
                         bank[6 + c % 2][0:DH, 0:2 * TC].rearrange("p (m t) -> p m t", m=2)).then_inc(s_oTc, 1)
            act.wait_ge(s_mw, 16 * 6)
            for i in range(12):
                b, f = i // 6, i % 6
                act.wait_ge(s_f1, i + 1)
                act.activation(h1T[:, f, b * NTOK:(b + 1) * NTOK], bank[4 + i % 4][:, 0:NTOK], ACT.Gelu,
                               bias=fc1_b[:, f:f + 1]).then_inc(s_f1c, 1)
            act.wait_ge(s_mx, 1)
            act.activation(sc[:, :, :], sc[:, :, :], ACT.Exp).then_inc(s_ex, 1)

            act.wait_ge(s_sched, 1)

            def load_block(b1):
                act.dma_start(bx[:, :], rows[bass.ds(b1 * SLOTS, SLOTS), :]).then_inc(s_xl, 16)

            def copy_x(b1):
                act.wait_ge(s_xt, b1)
                act.nop(nofuse=True)
                act.copy(bxT[0:DH, :, :], bank[4][0:DH, 0:2 * SLOTS].rearrange("p (k s) -> p k s", k=2)).then_inc(s_xc, 1)
                load_block(b1 + 1)

            def gelu_1(b1):
                act.wait_ge(s_w1, b1)
                act.nop(nofuse=True)
                for g in range(2):
                    f = slice(g * EHID // 2, (g + 1) * EHID // 2)
                    act.activation(bh1[:, f], bank[0][:, f], ACT.Gelu).then_inc(s_h1[g], 1)

            def gelu_2(b1):
                for g in range(2):
                    f = slice(g * EHID // 2, (g + 1) * EHID // 2)
                    act.wait_ge(s_pre[g], b1)
                    act.nop(nofuse=True)
                    act.activation(bh2[:, f], bpre[:, f], ACT.Gelu).then_inc(s_h2[g], 1)

            def fetch_w3(at, fetched=True):
                slot = lookup(act, SLOT, at, 0, WBUF - 1)
                if fetched:
                    act.wait_ge(s_w3, at)
                    act.nop(nofuse=True)
                act.copy(bw3[:, :], ew3[:, bass.ds(slot, 1), :].rearrange("p o f -> p (o f)")).then_inc(s_w3c, 1)

            def copy_y(b1):
                act.wait_ge(s_wl, b1 + 1)
                act.nop(nofuse=True)
                act.wait_ge(s_yfree, b1)
                act.nop(nofuse=True)
                act.copy(by[:, :], bank[6][0:SLOTS, 0:D]).then_inc(s_by, 1)

            act.nop(nofuse=True).then_inc(s_by, 1)
            nb = blocks(act)
            link(act.activation(gelu_of_one[:, :], ones[0:1, 0:1], ACT.Gelu))
            act.wait_ge(s_sc, 16 * 2 * NC)
            load_block(1)
            copy_x(1)
            gelu_1(1)
            fetch_w3(0, fetched=False)
            copy_x(2)
            gelu_2(1)
            gelu_1(2)
            copy_x(3)
            fetch_w3(1)
            most = blocks_but_one(act)
            with act.Fori(1, most) as last:
                b1 = act.snap(last + 1)
                gelu_2(b1)
                gelu_1(b1 + 1)
                copy_y(last)
                copy_x(b1 + 2)
                fetch_w3(b1)
            gelu_2(nb)
            copy_y(most)
            copy_y(nb)
            act.wait_ge(s_xl, nb * 16 + 32)
            act.nop(nofuse=True)

        @block.tensor
        def _(pe):
            pe.wait_ge(s_hi, 1)
            pe.wait_ge(s_id, 3)

            def keep_warm(n, free):
                for _ in range(n):
                    pe.matmul(bank[free][:, 0:128], ident[:, :], ident[:, :], start=True, stop=True)

            def spread(g):
                q, n = GROUPS[g]
                if g >= 2:
                    pe.wait_ge(s_hot, g - 1)
                for k in range(n):
                    ins = pe.matmul(bank[4 + g % 2][:, k * 128:(k + 1) * 128], hi_bf[:, q + k:q + k + 1].to_broadcast([128, 128]),
                                    ident_bf[:, :], start=True, stop=True)
                ins.then_inc(s_bc, 1)

            def gather(g):
                q, n = GROUPS[g]
                pe.wait_ge(s_hot, g + 1)
                if g == 0:
                    pe.wait_ge(s_x, 16)
                if g == 8:
                    pe.wait_ge(s_xr, 4)
                if g == 10:
                    pe.wait_ge(s_xr, 12)
                for k in range(0, n, 2):
                    i = (q + k) // 2
                    l = PAIRS[i][1]
                    rows = (x0, x1r, x2r)[l][:, :, :].rearrange("p f w -> p (f w)")
                    if i >= 2:
                        pe.wait_ge(s_pick, i - 1)
                    for kk in range(2):
                        ins = pe.matmul(bank[6 + i % 2][:, kk * D:(kk + 1) * D],
                                        hot[:, g % 2, (k + kk) * 128:(k + kk + 1) * 128], rows, start=True, stop=True)
                    ins.then_inc(s_gat, 1)

            def turn_weights():
                pe.wait_ge(s_tw, 16 * 10)
                for g in range(8):
                    ins = pe.transpose(bank[0][0:96, g * 64:(g + 1) * 64], w2[:, g * 96:(g + 1) * 96], ident[0:EMB, 0:EMB])
                ins.then_inc(s_wT, 1)
                pe.transpose(bank[1][0:48, 0:64], w0[:, :], ident[0:EMB, 0:EMB])
                for g in range(2):
                    pe.transpose(bank[1][0:96, 64 + g * 64:128 + g * 64], w1[:, g * 96:(g + 1) * 96], ident[0:EMB, 0:EMB])
                for k in range(2):
                    ins = pe.transpose(bank[1][0:EMB, 192 + k * 96:288 + k * 96], wf[:, k, 128:192], ident[0:DH, 0:DH])
                ins.then_inc(s_wT, 1)
                for l in range(2):
                    for k in range(2):
                        ins = pe.transpose(bank[2][0:EMB, l * D + k * 96:l * D + (k + 1) * 96], wf[:, k, l * 64:(l + 1) * 64],
                                           ident[0:DH, 0:DH])
                ins.then_inc(s_wT, 1)
                for k in range(2):
                    pe.transpose(bank[3][0:DH, k * 32:(k + 1) * 32], gate[:, k * DH:(k + 1) * DH], ident[0:E, 0:E])
                pe.transpose(bank[3][0:BOT, 320:352], eb3[:, :], ident[0:E, 0:E]).then_inc(s_wT, 1)

            spread(0)
            for g in range(len(GROUPS)):
                if g + 1 < len(GROUPS):
                    spread(g + 1)
                gather(g)
            turn_weights()
            keep_warm(4, 4)
            pe.wait_ge(s_wTc, 8)
            pe.wait_ge(s_pick, 16)
            for b in range(NBATCH):
                for t in range(2):
                    ins = pe.transpose(bank[0][0:48, (b * 2 + t) * 128:(b * 2 + t + 1) * 128],
                                       feat[0][:, b, t * 48:(t + 1) * 48], ident[:, :])
            ins.then_inc(s_fT, 1)
            pe.wait_ge(s_pick, 21)
            for b in range(NBATCH):
                pe.transpose(bank[1][0:96, b * 128:(b + 1) * 128], feat[1][:, b, :], ident[:, :])
            for b in range(NBATCH):
                ins = pe.transpose(bank[1][0:96, 256 + b * 128:256 + (b + 1) * 128], feat[2][:, b, :], ident[:, :])
            ins.then_inc(s_fT, 1)
            keep_warm(5, 4)
            pe.wait_ge(s_fTc, 2)
            pe.matmul(bank[2][0:EMB, :], w0T[:, :], f0T[:, :], start=True, stop=True).then_inc(s_y, 1)
            t1 = f12T[:, 0:2, :].rearrange("p b (t g) -> p b t g", g=2)
            t2 = f12T[:, 2:4, :].rearrange("p b (t g) -> p b t g", g=8)
            for g in range(2):
                pe.matmul(bank[3][0:EMB, 0:128], w1T[:, g, :], t1[:, :, :, g], start=(g == 0), stop=(g == 1))
            for g in range(8):
                ins = pe.matmul(bank[3][0:EMB, 128:160], w2T[:, g, :], t2[:, :, :, g], start=(g == 0), stop=(g == 7))
            ins.then_inc(s_y, 1)
            keep_warm(4, 5)
            pe.wait_ge(s_yc, 3)
            pe.matmul(bank[4][:, 0:D], y1T[:, :], wfT[:, 1, :], start=True, stop=True).then_inc(s_g, 1)
            pe.matmul(bank[5][0:32, 0:D], y2T[:, :], wfT[:, 2, :], start=True, stop=True).then_inc(s_g, 1)
            keep_warm(3, 6)
            pe.wait_ge(s_gc, 2)
            pe.wait_ge(s_hat, 2)
            for c in range(NC):
                b, t = c // CPB, c % CPB
                m = TC if t < CPB - 1 else TC - TXT
                if c >= 2:
                    pe.wait_ge(s_hc, c - 1)
                o = bank[6 + c % 2][0:m, 0:D]
                pe.matmul(o, y0T[:, b * NIMG + t * TC:b * NIMG + t * TC + m], w0g2[:, :], start=True, stop=False)
                pe.matmul(o, hat1[:, b, t * TC:t * TC + m], g1[:, :], start=False, stop=True).then_inc(s_h, 1)

            def turn_normed(first):
                for b in range(NBATCH):
                    keep_warm(8, 4)
                    pe.wait_ge(s_n, first + CPB * (b + 1))
                    for k in range(2):
                        for t in range(CPB):
                            ins = pe.transpose(bank[2 * k + b][0:DH, t * TC:(t + 1) * TC],
                                               norm[:, b * CPB + t, k * DH:(k + 1) * DH], ident[0:TC, 0:TC])
                        ins.then_inc(s_nT, 1)

            turn_normed(0)
            pe.wait_ge(s_aw, 16 * 6)
            pe.wait_ge(s_ones, 1)
            for i in range(4):
                b, m = i // 2, i % 2
                pe.wait_ge(s_xT, 2 * b + 2)
                for k in range(2):
                    r = DH + k
                    ins = pe.matmul(bank[4 + i][0:DH, 0:NTOK], qkv_w[0:r, k, m * DH:(m + 1) * DH],
                                    xT[0:r, k, b * NTOK:(b + 1) * NTOK], start=(k == 0), stop=(k == 1))
                ins.then_inc(s_q, 1)
            for c in range(NC):
                if c >= 4:
                    pe.wait_ge(s_kc, c - 3)
                for k in range(2):
                    r = DH + k
                    ins = pe.matmul(bank[c % 4][0:TC, 0:2 * D], xT[0:r, k, c * TC:(c + 1) * TC], qkv_w[0:r, k, D:3 * D],
                                    start=(k == 0), stop=(k == 1))
                ins.then_inc(s_kv, 1)
            pe.wait_ge(s_cst, 4)
            keep_warm(6, 4)
            pe.wait_ge(s_kc, NC)
            for b in range(NBATCH):
                for m in range(2):
                    for t in range(CPB):
                        c = b * CPB + t
                        ins = pe.matmul(bank[2][0:DH, (2 * b + m) * (DH + 1):(2 * b + m + 1) * (DH + 1)],
                                        kt[:, c, m * DH:(m + 1) * DH], vt[:, c, m, :], start=(t == 0), stop=(t == CPB - 1))
            ins.then_inc(s_kvs, 1)
            pe.wait_ge(s_kvc, 2)
            pe.wait_ge(s_qc, 4)

            def attend(c):
                if c >= 2:
                    pe.wait_ge(s_oc, c - 1)
                for m in range(2):
                    ins = pe.matmul(bank[4 + c % 2][0:TC, m * (DH + HPH):(m + 1) * (DH + HPH)],
                                    qT[:, m, c * TC:(c + 1) * TC], kvx[:, c // CPB * 2 + m, :], start=True, stop=True)
                ins.then_inc(s_o, 1)

            def turn_out(c):
                pe.wait_ge(s_oc, c + 1)
                if c >= 2:
                    pe.wait_ge(s_oTc, c - 1)
                for m in range(2):
                    ins = pe.transpose(bank[6 + c % 2][0:DH, m * TC:(m + 1) * TC], ot[:, c % 2, m * DH:(m + 1) * DH],
                                       ident[0:TC, 0:TC])
                ins.then_inc(s_oT, 1)

            def project(c):
                pe.wait_ge(s_oTc, c + 1)
                if c >= 2:
                    pe.wait_ge(s_x2r, c - 1)
                for m in range(2):
                    r = DH + m
                    ins = pe.matmul(bank[c % 2][0:TC, 0:D], oT[0:r, m, c * TC:(c + 1) * TC], proj_w[0:r, m, :],
                                    start=(m == 0), stop=(m == 1))
                ins.then_inc(s_pr, 1)

            pe.wait_ge(s_mw, 16 * 6)
            attend(0)
            attend(1)
            for c in range(NC):
                turn_out(c)
                if c + 2 < NC:
                    attend(c + 2)
                if c >= 1:
                    project(c - 1)
            project(NC - 1)
            turn_normed(NC)
            for i in range(12):
                b, f = i // 6, i % 6
                pe.wait_ge(s_xT, 2 * b + 6)
                if i >= 4:
                    pe.wait_ge(s_f1c, i - 3)
                for k in range(2):
                    ins = pe.matmul(bank[4 + i % 4][:, 0:NTOK], fc1_w[:, k, f * 128:(f + 1) * 128],
                                    xT[0:DH, k, b * NTOK:(b + 1) * NTOK], start=(k == 0), stop=(k == 1))
                ins.then_inc(s_f1, 1)
            for c in range(NC):
                pe.wait_ge(s_f1c, 6 * (c // CPB + 1))
                if c >= 2:
                    pe.wait_ge(s_h3, c - 1)
                for f in range(6):
                    ins = pe.matmul(bank[c % 2][0:TC, 0:D], h1T[:, f, c * TC:(c + 1) * TC], fc2_w[:, f, :],
                                    start=(f == 0), stop=(f == 5))
                ins.then_inc(s_f2, 1)
            turn_normed(2 * NC)
            for c in range(NC):
                pe.wait_ge(s_xT, 8 + 2 * (c // CPB + 1))
                for k in range(2):
                    ins = pe.matmul(bank[4][0:TC, c * E:(c + 1) * E], xT[0:DH, k, c * TC:(c + 1) * TC], gateT[:, k, :],
                                    start=(k == 0), stop=(k == 1))
            ins.then_inc(s_lg, 1)
            pe.wait_ge(s_sel, 1)
            flat = sel[:, :, :].rearrange("p c e -> p (c e)")
            pe.matmul(bank[5][0:TC, 0:NC * E], ones[0:TC, 0:TC], flat, start=True, stop=True)
            pe.matmul(bank[5][0:TC, NC * E:2 * NC * E], earlier[:, :], flat, start=True, stop=True).then_inc(s_rk, 1)

            pe.wait_ge(s_fact, 1)
            for t in range(4):
                ins = pe.matmul(bank[6][0:1, t * TC:(t + 1) * TC], fact[:, t:t + 1], ident[0:TC, 0:TC], start=True, stop=True)
            ins.then_inc(s_tab, 1)

            pe.wait_ge(s_sched, 1)

            def turn_block(b1):
                pe.wait_ge(s_xl, b1 * 16)
                pe.nop(nofuse=True)
                for k in range(2):
                    ins = pe.transpose(bank[4][0:DH, k * SLOTS:(k + 1) * SLOTS], bx[:, k * DH:(k + 1) * DH], ident[:, :])
                ins.then_inc(s_xt, 1)

            def w1_block(b1, at):
                slot = lookup(pe, SLOT, at, 0, WBUF - 1)
                number = lookup(pe, NUMBER, at, 1, E)
                pe.wait_ge(s_xc, b1)
                pe.nop(nofuse=True)
                pe.wait_ge(s_kl, number)
                pe.nop(nofuse=True)
                for k in range(2):
                    r = DH + k
                    ins = pe.matmul(bank[0][:, :], bxT[0:r, k, :], ew1[0:r, bass.ds(slot, 1), k, :].rearrange("p o f -> p (o f)"),
                                    start=(k == 0), stop=(k == 1))
                ins.then_inc(s_w1, 1)
                return slot

            def turn_hidden(b1, hidden, ready, to, done):
                for k in range(4):
                    if k % 2 == 0:
                        pe.wait_ge(ready[k // 2], b1)
                        pe.nop(nofuse=True)
                    ins = pe.transpose(to[:, k * SLOTS:(k + 1) * SLOTS], hidden[:, k * 128:(k + 1) * 128], ident[:, :])
                ins.then_inc(done, 1)

            def w2_block(b1, slot):
                for k in range(4):
                    if k % 2 == 0:
                        pe.wait_ge(s_h1T[k // 2], b1)
                        pe.nop(nofuse=True)
                    ins = pe.matmul(bank[1][:, :], bh1T[:, k, :], ew2[:, bass.ds(slot, 1), k, :].rearrange("p o f -> p (o f)"),
                                    start=(k == 0), stop=(k == 3))
                ins.then_inc(s_w2, 1)

            def w3_block(b1):
                pe.wait_ge(s_w3c, b1)
                pe.nop(nofuse=True)
                for k in range(4):
                    if k % 2 == 0:
                        pe.wait_ge(s_h2T[k // 2], b1)
                        pe.nop(nofuse=True)
                    ins = pe.matmul(bank[5][0:BOT, 0:SLOTS], bw3[:, k * BOT:(k + 1) * BOT], bh2T[:, k, :], start=(k == 0), stop=(k == 3))
                ins.then_inc(s_w3, 1)

            def wl_block(b1, at):
                slot = lookup(pe, SLOT, at, 0, WBUF - 1)
                pe.wait_ge(s_z, b1)
                pe.nop(nofuse=True)
                pe.wait_ge(s_by, b1)
                pe.nop(nofuse=True)
                pe.matmul(bank[6][:, 0:D], bzT[:, :], ewl[:, bass.ds(slot, 1), :].rearrange("p o f -> p (o f)"),
                          start=True, stop=True).then_inc(s_wl, 1)

            pe.nop(nofuse=True).then_inc(s_wl, 1)
            nb = blocks(pe)
            keep_warm(32, 7)
            turn_block(1)
            keep_warm(3, 7)
            slot = w1_block(1, 0)
            turn_block(2)
            turn_hidden(1, bh1, s_h1, bank[2], s_t1)
            w2_block(1, slot)

            def to_next_block(b1, last):
                slot = w1_block(b1 + 1, b1)
                if last is not None:
                    wl_block(last, last - 1)
                turn_hidden(b1, bh2, s_h2, bank[3], s_t2)
                turn_block(b1 + 2)
                turn_hidden(b1 + 1, bh1, s_h1, bank[2], s_t1)
                w3_block(b1)
                w2_block(b1 + 1, slot)

            to_next_block(1, None)
            most = blocks_but_one(pe)
            with pe.Fori(1, most) as last:
                to_next_block(pe.snap(last + 1), last)
            wl_block(most, most - 1)
            turn_hidden(nb, bh2, s_h2, bank[3], s_t2)
            w3_block(nb)
            wl_block(nb, nb - 1)


_INS = (["x", "txt"] + [f"L0_tok_{n}" for n in ("W0", "b0", "W1", "b1", "W2", "b2", "Wf", "bf", "idx0", "idx1", "idx2")]
        + [f"L0_attn_{n}" for n in ("qkv_w", "qkv_b", "proj_w", "proj_b", "fc1_w", "fc1_b", "fc2_w", "fc2_b",
                                    "ln1_w", "ln1_b", "ln2_w", "ln2_b")]
        + [f"L0_ffn_{n}" for n in ("gate_w", "W1", "b1", "W2", "b2", "W3", "b3", "Wl", "bl")])


def kernel(**inputs):
    import numpy as _np
    import concourse.bacc as _bacc
    from concourse import mybir as _mybir
    from concourse.bass_utils import run_bass_kernel_spmd as _run

    nc = _bacc.Bacc("TRN2", target_bir_lowering=False, num_devices=1)
    arrays, args = {}, {}
    for name in _INS:
        a = _np.ascontiguousarray(inputs[name])
        arrays[f"in_{name}_dram"] = a
        args[name] = nc.dram_tensor(f"in_{name}_dram", a.shape, _mybir.dt.from_np(a.dtype), kind="ExternalInput").ap()
    out = nc.dram_tensor("out_0_dram", (NBATCH, NTOK, D), F32, kind="ExternalOutput").ap()
    fusion_kernel(nc, args, out)
    r = _run(nc, [arrays], core_ids=[0])
    return r.results[0]["out_0_dram"]
```
